# Optimizing a Trainium2 kernel written in Bass

```python
import numpy as np
import jax
import jax.numpy as jnp

def _softmax(x, axis=-1):
    return jax.nn.softmax(x, axis=axis)

def _gelu(x):
    return jax.nn.gelu(x, approximate=True)

def _silu(x):
    return jax.nn.silu(x)

def _sigmoid(x):
    return jax.nn.sigmoid(x)

def _layernorm(x, axis=-1, eps=1e-05):
    m = jnp.mean(x, axis=axis, keepdims=True)
    v = jnp.var(x, axis=axis, keepdims=True)
    return (x - m) / jnp.sqrt(v + eps)

def _scatter_add(tgt, idx, src, axis=0):
    return tgt.at[idx].add(src)

def _segment_sum(src, seg, n):
    return jax.ops.segment_sum(src, seg, n)
kernel_name = 'mk_lm_tower_d1_tok_ids768_r4_acb811'

def setup_inputs(seed: int=0):
    np.random.seed(seed)
    _w = jnp.asarray

    def _rec_inputs():
        import jax
        import jax.numpy as jnp
        _rk = jax.random.key(seed)
        x = jax.random.randint(jax.random.fold_in(_rk, 1), (64, 128), 0, 50003, jnp.int32)
        itok_BS_0_1003 = jax.random.randint(jax.random.fold_in(_rk, 21), (64, 128), 0, 251, jnp.int32)
        itok_BS_0_5 = jax.random.randint(jax.random.fold_in(_rk, 22), (64, 128), 0, 6, jnp.int32)
        mask_BS_i1_0 = jnp.where(jnp.ones((64, 128), dtype=bool), 1, 0).astype(jnp.int32)
        return (x, itok_BS_0_1003, itok_BS_0_5, mask_BS_i1_0)
    x, itok_BS_0_1003, itok_BS_0_5, mask_BS_i1_0 = _rec_inputs()

    def _L0_tok_setup():
        import math
        import jax, jax.numpy as jnp
        import numpy as np
        B, S, D = (64, 128, 192)
        MAX_LEN = 128
        V_PROBLEM, V_SKILL, V_CORRECT, V_SEG = (12500 + 4, 250 + 4, 2 + 4, 2 + 1)
        NUM_STREAMS = 3 + 2

        def _make_pe():
            pos = np.arange(MAX_LEN, dtype=np.float32)[:, None]
            div = np.exp(np.arange(0, D, 2, dtype=np.float32) * -(math.log(10000.0) / D))
            pe = np.zeros((MAX_LEN, D), dtype=np.float32)
            pe[:, 0::2] = np.sin(pos * div)
            pe[:, 1::2] = np.cos(pos * div)
            return jnp.asarray(pe)
        key = jax.random.key(seed)
        ks = jax.random.split(key, 10)
        return {'problem_ids': jax.random.randint(ks[0], (B, S), 0, V_PROBLEM), 'skill_ids': jax.random.randint(ks[1], (B, S), 0, V_SKILL), 'correct_ids': jax.random.randint(ks[2], (B, S), 0, V_CORRECT), 'segment_info': jax.random.randint(ks[3], (B, S), 0, V_SEG), 'problem_table': jax.random.normal(ks[4], (V_PROBLEM, D), jnp.float32) * 0.02, 'skill_table': jax.random.normal(ks[5], (V_SKILL, D), jnp.float32) * 0.02, 'correct_table': jax.random.normal(ks[6], (V_CORRECT, D), jnp.float32) * 0.02, 'segment_table': jax.random.normal(ks[7], (V_SEG, D), jnp.float32) * 0.02, 'pe': _make_pe(), 'combine_w': jax.random.normal(ks[8], (1, NUM_STREAMS), jnp.float32) * 0.3, 'combine_b': jax.random.normal(ks[9], (1,), jnp.float32) * 0.01}
    _L0_tok_all = _L0_tok_setup()
    _L0_tok_in = {k: v for k, v in _L0_tok_all.items() if k in ('problem_table', 'skill_table', 'correct_table', 'segment_table', 'pe', 'combine_w', 'combine_b')}
    del _L0_tok_all

    def _L0_attn_setup():
        import jax, jax.numpy as jnp
        import numpy as np
        HIDDEN = 192
        NUM_HEADS = 12
        HEAD_DIM = 64

        def _xavier(key, shape):
            fan_in, fan_out = (shape[1], shape[0])
            limit = float(np.sqrt(6.0 / (fan_in + fan_out)))
            return jax.random.uniform(key, shape, jnp.float32, -limit, limit)
        key = jax.random.key(seed)
        k1, k2, k3 = jax.random.split(key, 3)
        B, N = (4, 512)
        x = jax.random.normal(k1, (B, N, HIDDEN), dtype=jnp.float32)
        qkv_w = _xavier(k2, (3 * NUM_HEADS * HEAD_DIM, HIDDEN))
        qkv_b = jnp.zeros((3 * NUM_HEADS * HEAD_DIM,), jnp.float32)
        proj_w = _xavier(k3, (HIDDEN, NUM_HEADS * HEAD_DIM))
        proj_b = jnp.zeros((HIDDEN,), jnp.float32)
        return {'x': x, 'qkv_w': qkv_w, 'qkv_b': qkv_b, 'proj_w': proj_w, 'proj_b': proj_b}
    _L0_attn_all = _L0_attn_setup()
    _L0_attn_in = {k: v for k, v in _L0_attn_all.items() if k in ('qkv_w', 'qkv_b', 'proj_w', 'proj_b')}
    del _L0_attn_all

    def _L0_ffn_setup():
        import jax, jax.numpy as jnp
        import numpy as np
        DIM = 192
        HEADS = 12
        EXPERTS = 8
        HID = 768
        TOP_K = 2
        LN_EPS = 1e-05

        def _layer_norm(x, g, b):
            mu = x.mean(-1, keepdims=True)
            var = ((x - mu) ** 2).mean(-1, keepdims=True)
            return (x - mu) * jax.lax.rsqrt(var + LN_EPS) * g + b

        def _attention(x, qkv_w, qkv_b, proj_w, proj_b):
            B, N, C = x.shape
            hd = C // HEADS
            qkv = (x @ qkv_w + qkv_b).reshape(B, N, 3, HEADS, hd).transpose(2, 0, 3, 1, 4)
            q, k, v = (qkv[0], qkv[1], qkv[2])
            attn = jax.nn.softmax(jnp.einsum('bhnd,bhmd->bhnm', q, k) * hd ** (-0.5), axis=-1)
            o = jnp.einsum('bhnm,bhmd->bhnd', attn, v).transpose(0, 2, 1, 3).reshape(B, N, C)
            return o @ proj_w + proj_b

        def _moe_mlp(xn, gate_w, w1, b1, w2, b2):
            T = xn.shape[0]
            logits = xn @ gate_w
            top_logits, top_idx = jax.lax.top_k(logits, TOP_K)
            top_gates = jax.nn.softmax(top_logits, axis=-1)
            gates = jnp.zeros((T, EXPERTS), xn.dtype).at[jnp.arange(T)[:, None], top_idx].set(top_gates)
            h = jax.nn.gelu(jnp.einsum('td,edh->teh', xn, w1) + b1, approximate=False)
            y = jnp.einsum('teh,ehd->ted', h, w2) + b2
            return jnp.einsum('ted,te->td', y, gates)
        key = jax.random.key(seed)
        ks = jax.random.split(key, 16)
        s = 0.02
        return {'x': jax.random.normal(ks[0], (8, 196, DIM), jnp.float32), 'ln1_g': jnp.ones((DIM,), jnp.float32), 'ln1_b': jnp.zeros((DIM,), jnp.float32), 'qkv_w': jax.random.normal(ks[1], (DIM, 3 * DIM), jnp.float32) * s, 'qkv_b': jnp.zeros((3 * DIM,), jnp.float32), 'proj_w': jax.random.normal(ks[2], (DIM, DIM), jnp.float32) * s, 'proj_b': jnp.zeros((DIM,), jnp.float32), 'ln2_g': jnp.ones((DIM,), jnp.float32), 'ln2_b': jnp.zeros((DIM,), jnp.float32), 'gate_w': jax.random.normal(ks[3], (DIM, EXPERTS), jnp.float32) * s, 'w1': jax.random.normal(ks[4], (EXPERTS, DIM, HID), jnp.float32) * s, 'b1': jnp.zeros((EXPERTS, HID), jnp.float32), 'w2': jax.random.normal(ks[5], (EXPERTS, HID, DIM), jnp.float32) * s, 'b2': jnp.zeros((EXPERTS, DIM), jnp.float32)}
    _L0_ffn_all = _L0_ffn_setup()
    _L0_ffn_in = {k: v for k, v in _L0_ffn_all.items() if k in ('ln1_g', 'ln1_b', 'qkv_w', 'qkv_b', 'proj_w', 'proj_b', 'ln2_g', 'ln2_b', 'gate_w', 'w1', 'b1', 'w2', 'b2')}
    del _L0_ffn_all
    return {'x': x, 'itok_BS_0_1003': itok_BS_0_1003, 'itok_BS_0_5': itok_BS_0_5, 'mask_BS_i1_0': mask_BS_i1_0, 'L0_tok_problem_table': _L0_tok_in['problem_table'], 'L0_tok_skill_table': _L0_tok_in['skill_table'], 'L0_tok_correct_table': _L0_tok_in['correct_table'], 'L0_tok_segment_table': _L0_tok_in['segment_table'], 'L0_tok_pe': _L0_tok_in['pe'], 'L0_tok_combine_w': _L0_tok_in['combine_w'], 'L0_tok_combine_b': _L0_tok_in['combine_b'], 'L0_attn_qkv_w': _L0_attn_in['qkv_w'], 'L0_attn_qkv_b': _L0_attn_in['qkv_b'], 'L0_attn_proj_w': _L0_attn_in['proj_w'], 'L0_attn_proj_b': _L0_attn_in['proj_b'], 'L0_ffn_ln1_g': _L0_ffn_in['ln1_g'], 'L0_ffn_ln1_b': _L0_ffn_in['ln1_b'], 'L0_ffn_qkv_w': _L0_ffn_in['qkv_w'], 'L0_ffn_qkv_b': _L0_ffn_in['qkv_b'], 'L0_ffn_proj_w': _L0_ffn_in['proj_w'], 'L0_ffn_proj_b': _L0_ffn_in['proj_b'], 'L0_ffn_ln2_g': _L0_ffn_in['ln2_g'], 'L0_ffn_ln2_b': _L0_ffn_in['ln2_b'], 'L0_ffn_gate_w': _L0_ffn_in['gate_w'], 'L0_ffn_w1': _L0_ffn_in['w1'], 'L0_ffn_b1': _L0_ffn_in['b1'], 'L0_ffn_w2': _L0_ffn_in['w2'], 'L0_ffn_b2': _L0_ffn_in['b2']}

def reference(x, itok_BS_0_1003, itok_BS_0_5, mask_BS_i1_0, L0_tok_problem_table, L0_tok_skill_table, L0_tok_correct_table, L0_tok_segment_table, L0_tok_pe, L0_tok_combine_w, L0_tok_combine_b, L0_attn_qkv_w, L0_attn_qkv_b, L0_attn_proj_w, L0_attn_proj_b, L0_ffn_ln1_g, L0_ffn_ln1_b, L0_ffn_qkv_w, L0_ffn_qkv_b, L0_ffn_proj_w, L0_ffn_proj_b, L0_ffn_ln2_g, L0_ffn_ln2_b, L0_ffn_gate_w, L0_ffn_w1, L0_ffn_b1, L0_ffn_w2, L0_ffn_b2):
    import jax
    import jax.numpy as jnp

    def _L0_tok_ref(problem_ids, skill_ids, correct_ids, segment_info, problem_table, skill_table, correct_table, segment_table, pe, combine_w, combine_b):
        import math
        import jax, jax.numpy as jnp
        import numpy as np
        B, S, D = (64, 128, 192)
        MAX_LEN = 128
        V_PROBLEM, V_SKILL, V_CORRECT, V_SEG = (12500 + 4, 250 + 4, 2 + 4, 2 + 1)
        NUM_STREAMS = 3 + 2

        def _make_pe():
            pos = np.arange(MAX_LEN, dtype=np.float32)[:, None]
            div = np.exp(np.arange(0, D, 2, dtype=np.float32) * -(math.log(10000.0) / D))
            pe = np.zeros((MAX_LEN, D), dtype=np.float32)
            pe[:, 0::2] = np.sin(pos * div)
            pe[:, 1::2] = np.cos(pos * div)
            return jnp.asarray(pe)
        seg_t = segment_table.at[0].set(0.0)
        prob_t = problem_table.at[0].set(0.0)
        skill_t = skill_table.at[0].set(0.0)
        corr_t = correct_table.at[0].set(0.0)
        w = combine_w[0]
        out = w[0] * pe[None, :S, :] + w[1] * seg_t[segment_info] + w[2] * prob_t[problem_ids] + w[3] * skill_t[skill_ids] + w[4] * corr_t[correct_ids] + combine_b[0]
        return out

    def _L0_attn_ref(x, qkv_w, qkv_b, proj_w, proj_b):
        import jax, jax.numpy as jnp
        import numpy as np
        HIDDEN = 192
        NUM_HEADS = 12
        HEAD_DIM = 64

        def _xavier(key, shape):
            fan_in, fan_out = (shape[1], shape[0])
            limit = float(np.sqrt(6.0 / (fan_in + fan_out)))
            return jax.random.uniform(key, shape, jnp.float32, -limit, limit)
        B, N, _ = x.shape
        nh, H = (NUM_HEADS, HEAD_DIM)
        qkv = jnp.einsum('bnd,od->bno', x, qkv_w) + qkv_b
        q, k, v = jnp.split(qkv, 3, axis=-1)

        def heads(t):
            return t.reshape(B, N, nh, H).transpose(0, 2, 1, 3)
        q, k, v = (heads(q), heads(k), heads(v))
        scores = jnp.einsum('bhnd,bhmd->bhnm', q, k) / jnp.sqrt(jnp.float32(H))
        attn = jax.nn.softmax(scores, axis=-1)
        out = jnp.einsum('bhnm,bhmd->bhnd', attn, v)
        out = out.transpose(0, 2, 1, 3).reshape(B, N, nh * H)
        out = jnp.einsum('bnk,ok->bno', out, proj_w) + proj_b
        return out

    def _L0_ffn_ref(x, ln1_g, ln1_b, qkv_w, qkv_b, proj_w, proj_b, ln2_g, ln2_b, gate_w, w1, b1, w2, b2):
        import jax, jax.numpy as jnp
        import numpy as np
        DIM = 192
        HEADS = 12
        EXPERTS = 8
        HID = 768
        TOP_K = 2
        LN_EPS = 1e-05

        def _layer_norm(x, g, b):
            mu = x.mean(-1, keepdims=True)
            var = ((x - mu) ** 2).mean(-1, keepdims=True)
            return (x - mu) * jax.lax.rsqrt(var + LN_EPS) * g + b

        def _attention(x, qkv_w, qkv_b, proj_w, proj_b):
            B, N, C = x.shape
            hd = C // HEADS
            qkv = (x @ qkv_w + qkv_b).reshape(B, N, 3, HEADS, hd).transpose(2, 0, 3, 1, 4)
            q, k, v = (qkv[0], qkv[1], qkv[2])
            attn = jax.nn.softmax(jnp.einsum('bhnd,bhmd->bhnm', q, k) * hd ** (-0.5), axis=-1)
            o = jnp.einsum('bhnm,bhmd->bhnd', attn, v).transpose(0, 2, 1, 3).reshape(B, N, C)
            return o @ proj_w + proj_b

        def _moe_mlp(xn, gate_w, w1, b1, w2, b2):
            T = xn.shape[0]
            logits = xn @ gate_w
            top_logits, top_idx = jax.lax.top_k(logits, TOP_K)
            top_gates = jax.nn.softmax(top_logits, axis=-1)
            gates = jnp.zeros((T, EXPERTS), xn.dtype).at[jnp.arange(T)[:, None], top_idx].set(top_gates)
            h = jax.nn.gelu(jnp.einsum('td,edh->teh', xn, w1) + b1, approximate=False)
            y = jnp.einsum('teh,ehd->ted', h, w2) + b2
            return jnp.einsum('ted,te->td', y, gates)
        B, N, C = x.shape
        x = x + _attention(_layer_norm(x, ln1_g, ln1_b), qkv_w, qkv_b, proj_w, proj_b)
        xn = _layer_norm(x, ln2_g, ln2_b).reshape(B * N, C)
        moe_out = _moe_mlp(xn, gate_w, w1, b1, w2, b2).reshape(B, N, C)
        return x + moe_out
    h = _L0_tok_ref(x, itok_BS_0_1003, itok_BS_0_5, mask_BS_i1_0, L0_tok_problem_table, L0_tok_skill_table, L0_tok_correct_table, L0_tok_segment_table, L0_tok_pe, L0_tok_combine_w, L0_tok_combine_b)
    h = h + _L0_attn_ref(_layernorm(h, axis=-1), L0_attn_qkv_w, L0_attn_qkv_b, L0_attn_proj_w, L0_attn_proj_b)
    h = h + _L0_ffn_ref(_layernorm(h, axis=-1), L0_ffn_ln1_g, L0_ffn_ln1_b, L0_ffn_qkv_w, L0_ffn_qkv_b, L0_ffn_proj_w, L0_ffn_proj_b, L0_ffn_ln2_g, L0_ffn_ln2_b, L0_ffn_gate_w, L0_ffn_w1, L0_ffn_b1, L0_ffn_w2, L0_ffn_b2)
    return h

_drawn_inputs = setup_inputs


def setup_inputs(seed=0):
    import zlib

    import numpy as np

    out = dict(_drawn_inputs(seed))
    spreads = {'L0_attn_qkv_b': (0.0, 0.1),
     'L0_attn_proj_b': (0.0, 0.1),
     'L0_ffn_ln1_g': (1.0, 0.6),
     'L0_ffn_ln1_b': (0.0, 0.8),
     'L0_ffn_qkv_b': (0.0, 0.317),
     'L0_ffn_proj_b': (0.0, 0.1),
     'L0_ffn_ln2_g': (1.0, 0.573),
     'L0_ffn_ln2_b': (0.0, 0.593),
     'L0_ffn_b1': (0.0, 0.531),
     'L0_ffn_b2': (0.0, 0.1)}
    factors = {}
    for name, (base, spread) in spreads.items():
        noise = np.random.default_rng([zlib.crc32(name.encode()), seed]).standard_normal(out[name].shape)
        drawn = base * np.exp(spread * noise) if base else spread * noise
        out[name] = jnp.asarray(drawn.astype(out[name].dtype))
    for name, factor in factors.items():
        out[name] = (out[name] * factor).astype(out[name].dtype)
    return out
```

```python
from contextlib import ExitStack

import numpy as np

import concourse.bass as bass
from concourse import mybir

F32 = mybir.dt.float32
F16 = mybir.dt.float16
I32 = mybir.dt.int32
U32 = mybir.dt.uint32
ALU = mybir.AluOpType
ACT = mybir.ActivationFunctionType
AX = mybir.AxisListType.X

P = 128
D = 192
DB = D - P
HEADS = 12
HALF = 384
W_SCALE = 64.0
LN_EPS = 1e-5
N_EXP = 8
HID = 768
HC = HID // P
TILE = 256
GROUP = 4
N_GROUPS = HEADS // GROUP


def wait(eng, sem, value):
    if not (isinstance(value, int) and value <= 0):
        eng.wait_ge(sem, value)


def waits_apart(eng, over, *waits):
    waits = [(sem, value if isinstance(value, int) else eng.to_reg(value)) for sem, value in waits]
    eng.wait_ge(*over)
    for sem, value in waits:
        wait(eng, sem, value)


class Split:

    def __init__(self, sb, name, cols):
        self.cols = cols
        self.a_hi, self.a_lo, self.b_hi, self.b_lo = (
            sb(f"{name}_{part}", [P, cols], F16) for part in ("a_hi", "a_lo", "b_hi", "b_lo"))

    def passes(self, act_a_hi, act_a_lo, act_b, cols):
        return [(act_a_hi, self.a_hi[:, cols]), (act_a_lo, self.a_hi[:, cols]),
                (act_a_hi, self.a_lo[:, cols]), (act_b, self.b_hi[:, cols]), (act_b, self.b_lo[:, cols])]


def build(nc, A, out):
    n_seq = A["x"].shape[1]
    S_ALL = n_seq * D
    with ExitStack() as whole:
        def sb(name, shape, dt, ctx=whole):
            return ctx.enter_context(nc.sbuf_tensor(name, shape, dt))

        def sem(name):
            return whole.enter_context(nc.semaphore(name))

        h_all = sb("h_all", [P, S_ALL], F32)
        ident = sb("ident", [P, P], F32)
        ones_rows = sb("ones_rows", [P, P], F16)
        neg_low = sb("neg_low", [P, 1], F32)
        half_pow = sb("half_pow", [P, 1], F32)
        psum = [whole.enter_context(nc.psum_tensor(f"bank{i}", [P, 512], F32)) for i in range(8)]

        phases(nc, A, out, h_all, ident, ones_rows, neg_low, half_pow, psum, sb, sem, n_seq)


def load_split(eng, sems, stage, src, cols):
    eng.dma_start(stage[:, 0, 0:cols], src[0:P, :]).then_inc(sems, 16)
    eng.dma_start(stage[0:DB, 1, 0:cols], src[P:D, :]).then_inc(sems, 16)
    eng.dma_start(stage[DB:P, 1, 0:cols], src[P:D, :]).then_inc(sems, 16)


def phases(nc, A, out, h_all, ident, ones_rows, neg_low, half_pow, psum, sb, sem, n_seq):
    with ExitStack() as ctx:
        first_attention(nc, A, h_all, ident, ones_rows, neg_low, half_pow, psum,
                        lambda n, s, d: sb(n, s, d, ctx), sem, n_seq)
    with ExitStack() as routed:
        route = Route(nc, lambda n, s, d: sb(n, s, d, routed), n_seq)
        with ExitStack() as ctx:
            second_attention(nc, A, h_all, ident, ones_rows, half_pow, psum, route,
                             lambda n, s, d: sb(n, s, d, ctx), sem, n_seq)
        with ExitStack() as ctx:
            experts(nc, A, h_all, ident, ones_rows, psum, route, lambda n, s, d: sb(n, s, d, ctx), sem, n_seq)
        with ExitStack() as ctx:
            combine(nc, A, h_all, route, out, lambda n, s, d: sb(n, s, d, ctx), sem, n_seq)


def first_attention(nc, A, h_all, ident, ones_rows, neg_low, half_pow, psum, sb, sem, n_seq):
    HD = 64
    CH = 6
    QK = 2 * CH * P
    SCALE = float(HD) ** -0.5 / (W_SCALE * W_SCALE)
    VW = HD + 1

    w_qk = Split(sb, "w_qk", QK)
    w_v = Split(sb, "w_v", CH * P)
    wp_hi = sb("wp_hi", [P, CH, D], F16)
    wp_lo = sb("wp_lo", [P, CH, D], F16)
    bias_qk = sb("bias_qk", [P, QK], F16)
    bias_out = sb("bias_out", [P, D], F16)
    pe_base = sb("pe_base", [P, D], F32)
    names = ("problem", "skill", "correct", "segment")
    tables = [A[f"L0_tok_{n}_table"] for n in names]
    sizes = [t.shape[0] for t in tables]
    ids_all = sb("ids_all", [P, 4, n_seq], I32)
    ids_i = [ids_all[:, n, :] for n in range(4)]
    ids_now = [sb(f"ids_now{u}", [P, 4], I32) for u in range(2)]
    coef = [sb(f"{n}_coef", [P, n_seq], F32) for n in names]
    rows = [[sb(f"{n}_rows{u}", [P, D], F32) for u in range(2)] for n in names]

    stats = [sb(f"stats{u}", [P, 6], F32) for u in range(2)]
    moments = [sb(f"moments{u}", [P, 2], F32) for u in range(2)]
    var_eps = [sb(f"var_eps{u}", [P, 1], F32) for u in range(2)]
    rstd = [sb(f"rstd{u}", [P, 1], F32) for u in range(2)]
    y = [sb(f"y{u}", [P, 2 * P], F32) for u in range(2)]
    xt_hi = [sb(f"xt_hi{u}", [P, 2 * P], F16) for u in range(2)]
    xt_alo = [sb(f"xt_alo{u}", [P, P], F16) for u in range(2)]
    xt_b = [sb(f"xt_b{u}", [P, P], F16) for u in range(2)]
    q_hi = [sb(f"q_hi{u}", [P, CH * P], F16) for u in range(2)]
    q_lo = [sb(f"q_lo{u}", [P, CH * P], F16) for u in range(2)]
    kp_hi = [sb(f"kp_hi{u}", [P, CH, 2, P], F16) for u in range(2)]
    kp_lo = [sb(f"kp_lo{u}", [P, CH, 2, P], F16) for u in range(2)]
    v_hi = [sb(f"v_hi{u}", [P, HEADS, VW], F16) for u in range(2)]
    v_lo = [sb(f"v_lo{u}", [P, HEADS, HD], F16) for u in range(2)]
    row_max = [sb(f"row_max{u}", [P, GROUP], F32) for u in range(2)]
    neg_max = [sb(f"neg_max{u}", [P, GROUP], F32) for u in range(2)]
    prob = [sb(f"prob{u}", [P, GROUP, P], F32) for u in range(2)]
    pt_hi = [sb(f"pt_hi{u}", [P, GROUP, P], F16) for u in range(2)]
    pt_lo = [sb(f"pt_lo{u}", [P, GROUP, P], F16) for u in range(2)]
    recip = sb("recip", [P, HEADS], F32)
    o_norm = sb("o_norm", [P, HEADS, HD], F32)
    ot_hi = sb("ot_hi", [P, CH, P], F16)
    ot_lo = sb("ot_lo", [P, CH, P], F16)
    stage = sb("stage", [P, 2, QK], F32)
    stage_p = sb("stage_p", [P, CH, D], F32)
    stage_bias = sb("stage_bias", [33, QK], F32)
    stage_bout = sb("stage_bout", [33, D], F32)
    bout_hi = sb("bout_hi", [33, D], F16)
    bqk_hi = sb("bqk_hi", [33, QK], F16)
    bv_col = sb("bv_col", [P, CH], F32)
    wvec = sb("wvec", [P, 6], F32)
    idf = sb("idf", [P, n_seq], F32)
    idn = sb("idn", [P, n_seq], F32)

    bank_s, bank_t, bank_o, bank_w = psum[0:2], psum[2:4], psum[4:6], psum[6:8]

    loaded = sem("a_loaded")
    const_done = sem("a_const_done")
    wide_loaded = sem("a_wide_loaded")
    v_loaded = sem("a_v_loaded")
    split_step = sem("a_split_step")
    bias_sum = sem("a_bias_sum")
    masks_ready = sem("a_masks_ready")
    ids_ready = sem("a_ids_ready")
    ids_at_hand = sem("a_ids_at_hand")
    id_step = sem("a_id_step")
    weights_ready = sem("a_weights_ready")
    rows_loaded = [sem(f"a_rows_loaded{u}") for u in range(2)]
    embedded = sem("a_embedded")
    ln_step = sem("a_ln_step")
    rstd_ready = sem("a_rstd_ready")
    y_ready = sem("a_y_ready")
    xt_filled = sem("a_xt_filled")
    xt_hi_ready = sem("a_xt_hi_ready")
    xt_ready = sem("a_xt_ready")
    qkv_filled = sem("a_qkv_filled")
    qkv_hi = sem("a_qkv_hi")
    qkv_lo = sem("a_qkv_lo")
    scores_filled = sem("a_scores_filled")
    max_ready = sem("a_max_ready")
    neg_ready = sem("a_neg_ready")
    prob_ready = sem("a_prob_ready")
    pt_filled = sem("a_pt_filled")
    pt_hi_ready = sem("a_pt_hi_ready")
    pt_lo_ready = sem("a_pt_lo_ready")
    heads_done = sem("a_heads_done")
    recip_ready = sem("a_recip_ready")
    o_ready = sem("a_o_ready")
    ot_filled = sem("a_ot_filled")
    ot_hi_ready = sem("a_ot_hi_ready")
    ot_lo_ready = sem("a_ot_lo_ready")
    out_filled = sem("a_out_filled")
    h_ready = sem("a_h_ready")
    HI_AT = [1, 2, 4, 6, 7, 8]

    def seq(s):
        return bass.ts(s, D)

    wq_src, wv_src = A["L0_attn_qkv_wT"][:, 0:QK], A["L0_attn_qkv_wT"][:, QK:QK + CH * P]
    block = nc.Block()
    with block:
        @block.sync
        def _(sp):
            for n, ids in zip(("x", "itok_BS_0_1003", "itok_BS_0_5", "mask_BS_i1_0"), ids_i):
                sp.dma_start(ids, A[n]).then_inc(loaded, 16)
            sp.dma_start(wvec[:, 0:5], A["L0_tok_combine_w"].partition_broadcast(P)).then_inc(loaded, 16)
            sp.dma_start(wvec[:, 5:6], A["L0_tok_combine_b"].partition_broadcast(P)).then_inc(loaded, 16)
            sp.dma_start(pe_base[:], A["L0_tok_pe"]).then_inc(loaded, 16)
            load_split(sp, wide_loaded, stage, wq_src, QK)
            for r in (0, 32):
                sp.dma_start(stage_bias[r:r + 1, :], A["L0_attn_qkv_b"][:, 0:QK]).then_inc(wide_loaded, 16)
                sp.dma_start(stage_bout[r:r + 1, :], A["L0_attn_proj_b"]).then_inc(wide_loaded, 16)
            sp.dma_start(bv_col[:], A["L0_attn_qkv_b"][0, QK:QK + CH * P].rearrange("(c p) -> p c", p=P),
                         allow_slow_non_contiguous=True).then_inc(wide_loaded, 16)
            sp.dma_start(stage_p[:], A["L0_attn_proj_wT"].rearrange("(c p) d -> p c d", p=P)).then_inc(wide_loaded, 16)
            sp.wait_ge(split_step, 4)
            load_split(sp, v_loaded, stage, wv_src, CH * P)

        @block.gpsimd
        def _(pool):
            nc.gpsimd.memset(ident[:], 1.0).then_inc(masks_ready, 1)
            nc.gpsimd.memset(half_pow[:], -0.5).then_inc(masks_ready, 1)
            pool.wait_ge(masks_ready, 1)
            nc.gpsimd.affine_select(out=ident[:], in_=ident[:], compare_op=ALU.is_equal, fill=0.0, base=0,
                                    pattern=[[-1, P]], channel_multiplier=1).then_inc(masks_ready, 1)
            pool.wait_ge(masks_ready, 3)
            pool.wait_ge(ids_ready, 4)

            def gather(s, u):
                waits_apart(pool, (masks_ready, 3), (embedded, 4 * (s - 1) if isinstance(s, int) else 4 * s - 4))
                nc.gpsimd.tensor_copy(ids_now[u][:], ids_all[:, :, bass.ds(s, 1)].rearrange("p n o -> p (n o)")).then_inc(ids_at_hand, 1)
                waits_apart(pool, (masks_ready, 3), (ids_at_hand, s + 1))
                for n in range(4):
                    nc.gpsimd.indirect_dma_start(
                        out=rows[n][u][:, :], out_offset=None, in_=tables[n],
                        in_offset=bass.IndirectOffsetOnAxis(ap=ids_now[u][:, n:n + 1].bitcast(U32), axis=0),
                    ).then_inc(rows_loaded[u], 16)

            def rsqrt(s, u):
                pool.wait_ge(ln_step, 3 * s + 3)
                nc.gpsimd.tensor_tensor(rstd[u][:], var_eps[u][:], half_pow[:], ALU.pow).then_inc(rstd_ready, 1)

            gather(0, 0)
            gather(1, 1)
            rsqrt(0, 0)
            rsqrt(1, 1)

            def iteration(t, u):
                gather(t + 2, u)
                rsqrt(t + 2, u)

            iteration(0, 0)
            with pool.Fori(0, (n_seq - 4) // 2) as i:
                for v in range(2):
                    iteration(2 * i + 1 + v, 1 - v)
            iteration(n_seq - 3, 1)

        @block.scalar
        def _(act):
            def to_hi(dst, src):
                return nc.scalar.activation(dst, src, ACT.Copy, scale=W_SCALE)

            act.wait_ge(wide_loaded, 16 * 9)
            to_hi(w_qk.a_hi[:], stage[:, 0, :]).then_inc(weights_ready, 1)
            to_hi(w_qk.b_hi[:], stage[:, 1, :]).then_inc(weights_ready, 1)
            to_hi(wp_hi[:], stage_p[:]).then_inc(weights_ready, 1)
            to_hi(bqk_hi[0:1, :], stage_bias[0:1, :]).then_inc(weights_ready, 1)
            to_hi(bqk_hi[32:33, :], stage_bias[32:33, :]).then_inc(weights_ready, 1)
            act.wait_ge(v_loaded, 48)
            to_hi(w_v.a_hi[:], stage[:, 0, 0:CH * P]).then_inc(weights_ready, 1)
            to_hi(w_v.b_hi[:], stage[:, 1, 0:CH * P]).then_inc(weights_ready, 1)

            def xt_high(s, u):
                act.wait_ge(xt_filled, s + 1)
                wait(act, qkv_filled, 6 * (s - 1) if isinstance(s, int) else 6 * s - 6)
                nc.scalar.copy(xt_hi[u][:], bank_w[0][:, 0:2 * P]).then_inc(xt_hi_ready, 1)

            def qkv_high(s, u, j):
                w = bank_w[j % 2]
                act.wait_ge(qkv_filled, 6 * s + j + 1)
                if j < 2:
                    wait(act, scores_filled, 3 * (s - 1) if isinstance(s, int) else 3 * s - 3)
                    nc.scalar.copy(q_hi[u][:, j * HALF:(j + 1) * HALF], w[:, 0:HALF]).then_inc(qkv_hi, 1)
                elif j < 4:
                    for g in range(2):
                        r = slice(64 * g, 64 * g + 64)
                        nc.scalar.copy(kp_hi[u][r, 3 * (j - 2):3 * (j - 1), g, :],
                                       w[r, 0:HALF].rearrange("p (c k) -> p c k", k=P)).then_inc(qkv_hi, 1)
                else:
                    wait(act, heads_done, 3 * (s - 1) if isinstance(s, int) else 3 * s - 3)
                    nc.scalar.copy(v_hi[u][:, 6 * (j - 4):6 * (j - 3), 0:HD],
                                   w[:, 0:HALF].rearrange("p (h d) -> p h d", d=HD)).then_inc(qkv_hi, 1)

            def exps(t, g, b):
                act.wait_ge(neg_ready, 3 * t + g + 1)
                wait(act, pt_filled, 3 * t + g - 1)
                for e in range(GROUP):
                    nc.scalar.activation(prob[b][:, e, :], bank_s[b][:, e * P:(e + 1) * P], ACT.Exp,
                                         bias=neg_max[b][:, e:e + 1], scale=SCALE).then_inc(prob_ready, 1)

            def pt_high(t, g, b):
                act.wait_ge(pt_filled, 3 * t + g + 1)
                wait(act, heads_done, 3 * t + g - 1)
                nc.scalar.copy(pt_hi[b][:].rearrange("p e k -> p (e k)"), bank_t[b][:]).then_inc(pt_hi_ready, 1)

            def ot_high(t, half):
                act.wait_ge(ot_filled, 2 * t + half + 1)
                wait(act, out_filled, t)
                nc.scalar.copy(ot_hi[:, 3 * half:3 * half + 3, :].rearrange("p c k -> p (c k)"),
                               bank_o[half][:, 0:HALF]).then_inc(ot_hi_ready, 1)

            def project_all(s, u):
                for j in range(6):
                    qkv_high(s, u, j)

            act.wait_ge(const_done, 1)
            xt_high(0, 0)
            project_all(0, 0)
            xt_high(1, 1)

            def iteration(t, u, output=True, project=True, embed=True):
                b = u
                n = 1 - u
                exps(t, 0, b)
                if project:
                    qkv_high(t + 1, n, 0)
                if output:
                    ot_high(t - 1, 0)
                    ot_high(t - 1, 1)
                exps(t, 1, 1 - b)
                if project:
                    qkv_high(t + 1, n, 1)
                pt_high(t, 0, b)
                exps(t, 2, b)
                if project:
                    qkv_high(t + 1, n, 2)
                pt_high(t, 1, 1 - b)
                if project:
                    qkv_high(t + 1, n, 3)
                    qkv_high(t + 1, n, 4)
                pt_high(t, 2, b)
                if project:
                    qkv_high(t + 1, n, 5)
                if embed:
                    xt_high(t + 2, u)

            iteration(0, 0, output=False)
            with act.Fori(0, (n_seq - 4) // 2) as i:
                for v in range(2):
                    iteration(2 * i + 1 + v, 1 - v)
            iteration(n_seq - 3, 1)
            iteration(n_seq - 2, 0, embed=False)
            iteration(n_seq - 1, 1, embed=False, project=False)
            ot_high(n_seq - 1, 0)
            ot_high(n_seq - 1, 1)

        @block.vector
        def _(dve):
            nc.vector.memset(ones_rows[:], 0.0).then_inc(id_step, 1)
            nc.vector.memset(bias_qk[:], 0.0).then_inc(id_step, 1)
            nc.vector.memset(bias_out[:], 0.0).then_inc(id_step, 1)
            nc.vector.memset(neg_low[0:64, :], 0.0).then_inc(id_step, 1)
            nc.vector.memset(neg_low[64:P, :], -1.0).then_inc(id_step, 1)
            for u in range(2):
                for kp in (kp_hi[u], kp_lo[u]):
                    nc.vector.memset(kp[:], 0.0).then_inc(id_step, 1)
                nc.vector.memset(v_hi[u][:, :, HD:VW], 1.0).then_inc(id_step, 1)
            dve.wait_ge(id_step, 11)
            nc.vector.memset(ones_rows[0:1, :], 1.0).then_inc(id_step, 1)
            nc.vector.memset(ones_rows[32:33, :], 1.0).then_inc(id_step, 1)
            dve.wait_ge(loaded, 16 * 7)
            nc.vector.tensor_scalar(pe_base[:], pe_base[:], wvec[:, 0:1], wvec[:, 5:6], ALU.mult, ALU.add).then_inc(id_step, 1)
            done = 14
            for n, w_at in zip(range(4), (2, 3, 4, 1)):
                v_n = float(sizes[n])
                steps = [
                    lambda: nc.vector.tensor_copy(idf[:], ids_i[n]),
                    lambda: nc.vector.tensor_scalar(idn[:], idf[:], 0.0, v_n, ALU.is_lt, ALU.mult),
                    lambda: nc.vector.tensor_tensor(idf[:], idf[:], idn[:], ALU.add),
                    lambda: nc.vector.tensor_scalar(idf[:], idf[:], 0.0, v_n - 1.0, ALU.max, ALU.min),
                    lambda: nc.vector.tensor_scalar(coef[n][:], idf[:], 0.0, wvec[:, w_at:w_at + 1], ALU.not_equal, ALU.mult),
                ]
                for step in steps:
                    dve.wait_ge(id_step, done)
                    step().then_inc(id_step, 1)
                    done += 1
                nc.vector.tensor_copy(ids_i[n], idf[:]).then_inc(ids_ready, 1)
                dve.wait_ge(ids_ready, n + 1)
                dve.wait_ge(id_step, done)

            def embed(s, u, n):
                dve.wait_ge(rows_loaded[u], 32 * (s - u) + 64)
                wait(dve, embedded, 4 * s + n)
                base = pe_base[:] if n == 0 else h_all[:, seq(s)]
                nc.vector.scalar_tensor_tensor(h_all[:, seq(s)], rows[n][u][:], coef[n][:, bass.ds(s, 1)], base,
                                               ALU.mult, ALU.add).then_inc(embedded, 1)

            def ln_stats(s, u):
                waits_apart(dve, (const_done, 1), (embedded, 4 * s + 4))
                nc.vector.bn_stats(stats[u][:], h_all[:, seq(s)]).then_inc(ln_step, 1)

            def ln_aggr(s, u):
                waits_apart(dve, (const_done, 1), (ln_step, 3 * s + 1), (y_ready, 2 * s - 2))
                nc.vector.bn_aggr(moments[u][:], stats[u][:]).then_inc(ln_step, 1)

            def ln_eps(s, u):
                dve.wait_ge(ln_step, 3 * s + 2)
                nc.vector.tensor_scalar(var_eps[u][:], moments[u][:, 1:2], LN_EPS, None, ALU.add).then_inc(ln_step, 1)

            def ln_apply(s, u):
                dve.wait_ge(rstd_ready, s + 1)
                wait(dve, xt_filled, s - 1)
                for dst, src in ((y[u][:, 0:D], h_all[:, seq(s)]), (y[u][:, D:2 * P], h_all[:, bass.ds(s * D + P, DB)])):
                    nc.vector.tensor_scalar(dst, src, moments[u][:, 0:1], rstd[u][:, 0:1],
                                            ALU.subtract, ALU.mult).then_inc(y_ready, 1)

            def xt_low(s, u):
                dve.wait_ge(xt_hi_ready, s + 1)
                nc.vector.tensor_tensor(xt_alo[u][:], bank_w[0][:, 0:P], xt_hi[u][:, 0:P], ALU.subtract).then_inc(xt_ready, 1)
                nc.vector.scalar_tensor_tensor(xt_b[u][:], xt_hi[u][:, P:2 * P], neg_low[:, 0:1], bank_w[0][:, P:2 * P],
                                               ALU.mult, ALU.add).then_inc(xt_ready, 1)

            def qkv_low(s, u, j):
                w = bank_w[j % 2]
                dve.wait_ge(qkv_hi, 8 * s + HI_AT[j])
                if j < 2:
                    c = slice(j * HALF, (j + 1) * HALF)
                    nc.vector.tensor_tensor(q_lo[u][:, c], w[:, 0:HALF], q_hi[u][:, c], ALU.subtract).then_inc(qkv_lo, 1)
                elif j < 4:
                    for g in range(2):
                        r = slice(64 * g, 64 * g + 64)
                        c = slice(3 * (j - 2), 3 * (j - 1))
                        nc.vector.tensor_tensor(kp_lo[u][r, c, g, :], w[r, 0:HALF].rearrange("p (c k) -> p c k", k=P),
                                                kp_hi[u][r, c, g, :], ALU.subtract).then_inc(qkv_lo, 1)
                else:
                    c = slice(6 * (j - 4), 6 * (j - 3))
                    nc.vector.tensor_tensor(v_lo[u][:, c, :], w[:, 0:HALF].rearrange("p (h d) -> p h d", d=HD),
                                            v_hi[u][:, c, 0:HD], ALU.subtract).then_inc(qkv_lo, 1)

            def maxima(t, g, b):
                dve.wait_ge(scores_filled, 3 * t + g + 1)
                wait(dve, neg_ready, 3 * t + g - 1)
                nc.vector.tensor_reduce(row_max[b][:], bank_s[b][:].rearrange("p (e k) -> p e k", k=P), AX, ALU.max
                                        ).then_inc(max_ready, 1)

            def neg_maxima(t, g, b):
                dve.wait_ge(max_ready, 3 * t + g + 1)
                wait(dve, prob_ready, 4 * (3 * t + g - 1))
                nc.vector.tensor_scalar(neg_max[b][:], row_max[b][:], -SCALE, None, ALU.mult).then_inc(neg_ready, 1)

            def pt_low(t, g, b):
                dve.wait_ge(pt_hi_ready, 3 * t + g + 1)
                nc.vector.tensor_tensor(pt_lo[b][:].rearrange("p e k -> p (e k)"), bank_t[b][:],
                                        pt_hi[b][:].rearrange("p e k -> p (e k)"), ALU.subtract).then_inc(pt_lo_ready, 1)

            def o_view(half):
                return bank_o[half][:, 0:6 * VW].rearrange("p (h d) -> p h d", d=VW)

            def row_sums(t):
                for half in range(2):
                    dve.wait_ge(heads_done, 3 * t + 2 + half)
                    wait(dve, o_ready, 2 * t)
                    nc.vector.reciprocal(recip[:, 6 * half:6 * half + 6], o_view(half)[:, :, HD]).then_inc(recip_ready, 1)

            def normalise(t):
                for half in range(2):
                    dve.wait_ge(recip_ready, 2 * t + half + 1)
                    wait(dve, ot_filled, 2 * t)
                    nc.vector.tensor_tensor(o_norm[:, 6 * half:6 * half + 6, :], o_view(half)[:, :, 0:HD],
                                            recip[:, 6 * half:6 * half + 6].unsqueeze(2).to_broadcast([P, 6, HD]),
                                            ALU.mult).then_inc(o_ready, 1)

            def ot_low(t, half):
                dve.wait_ge(ot_hi_ready, 2 * t + half + 1)
                nc.vector.tensor_tensor(ot_lo[:, 3 * half:3 * half + 3, :].rearrange("p c k -> p (c k)"), bank_o[half][:, 0:HALF],
                                        ot_hi[:, 3 * half:3 * half + 3, :].rearrange("p c k -> p (c k)"),
                                        ALU.subtract).then_inc(ot_lo_ready, 1)

            def add_output(t):
                dve.wait_ge(out_filled, t + 1)
                nc.vector.scalar_tensor_tensor(h_all[:, seq(t)], bank_o[0][:, 0:D], 1.0 / (W_SCALE * W_SCALE), h_all[:, seq(t)],
                                               ALU.mult, ALU.add).then_inc(h_ready, 1)

            def embed_all(s, u):
                for n in range(4):
                    embed(s, u, n)
                ln_stats(s, u)
                ln_aggr(s, u)
                ln_eps(s, u)
                ln_apply(s, u)

            def to_lo(dst, src, hi):
                return nc.vector.scalar_tensor_tensor(dst, src, W_SCALE, hi, ALU.mult, ALU.subtract)

            dve.wait_ge(weights_ready, 1)
            to_lo(w_qk.a_lo[:], stage[:, 0, :], w_qk.a_hi[:]).then_inc(split_step, 1)
            dve.wait_ge(weights_ready, 2)
            to_lo(w_qk.b_lo[:], stage[:, 1, :], w_qk.b_hi[:]).then_inc(split_step, 1)
            dve.wait_ge(weights_ready, 5)
            to_lo(wp_lo[:], stage_p[:], wp_hi[:]).then_inc(split_step, 1)
            nc.vector.tensor_copy(bias_qk[0:1, :], bqk_hi[0:1, :]).then_inc(split_step, 1)
            to_lo(bias_qk[32:33, :], stage_bias[32:33, :], bqk_hi[32:33, :]).then_inc(split_step, 1)
            dve.wait_ge(bias_sum, 1)
            for r in (0, 32):
                nc.vector.tensor_tensor(stage_bout[r:r + 1, :], bank_t[0][r:r + 1, 0:D], stage_bout[r:r + 1, :], ALU.add
                                        ).then_inc(split_step, 1)
            dve.wait_ge(split_step, 7)
            for r in (0, 32):
                nc.vector.tensor_scalar(bout_hi[r:r + 1, :], stage_bout[r:r + 1, :], W_SCALE * W_SCALE, None, ALU.mult
                                        ).then_inc(split_step, 1)
            dve.wait_ge(split_step, 9)
            nc.vector.tensor_copy(bias_out[0:1, :], bout_hi[0:1, :]).then_inc(split_step, 1)
            nc.vector.scalar_tensor_tensor(bias_out[32:33, :], stage_bout[32:33, :], W_SCALE * W_SCALE, bout_hi[32:33, :],
                                           ALU.mult, ALU.subtract).then_inc(split_step, 1)
            dve.wait_ge(weights_ready, 7)
            to_lo(w_v.a_lo[:], stage[:, 0, 0:CH * P], w_v.a_hi[:]).then_inc(split_step, 1)
            to_lo(w_v.b_lo[:], stage[:, 1, 0:CH * P], w_v.b_hi[:]).then_inc(split_step, 1)
            dve.wait_ge(split_step, 13)
            nc.vector.memset(stats[0][:], 0.0).then_inc(const_done, 1)
            dve.wait_ge(const_done, 1)

            embed_all(0, 0)
            xt_low(0, 0)
            for j in range(6):
                qkv_low(0, 0, j)
            embed_all(1, 1)
            xt_low(1, 1)

            def iteration(t, u, output=True, project=True, embedding=True):
                b, n, s = u, 1 - u, t + 2
                maxima(t, 0, b)
                neg_maxima(t, 0, b)
                if project:
                    qkv_low(t + 1, n, 0)
                if output:
                    ot_low(t - 1, 0)
                    ot_low(t - 1, 1)
                maxima(t, 1, 1 - b)
                neg_maxima(t, 1, 1 - b)
                if embedding:
                    embed(s, u, 0)
                if project:
                    qkv_low(t + 1, n, 1)
                if output:
                    add_output(t - 1)
                if embedding:
                    embed(s, u, 1)
                pt_low(t, 0, b)
                if embedding:
                    embed(s, u, 2)
                maxima(t, 2, b)
                neg_maxima(t, 2, b)
                if embedding:
                    embed(s, u, 3)
                if project:
                    qkv_low(t + 1, n, 2)
                if embedding:
                    ln_stats(s, u)
                pt_low(t, 1, 1 - b)
                if embedding:
                    ln_aggr(s, u)
                if project:
                    qkv_low(t + 1, n, 3)
                if embedding:
                    ln_eps(s, u)
                if project:
                    qkv_low(t + 1, n, 4)
                pt_low(t, 2, b)
                if embedding:
                    ln_apply(s, u)
                if project:
                    qkv_low(t + 1, n, 5)
                row_sums(t)
                if embedding:
                    xt_low(s, u)
                normalise(t)

            iteration(0, 0, output=False)
            with dve.Fori(0, (n_seq - 4) // 2) as i:
                for v in range(2):
                    iteration(2 * i + 1 + v, 1 - v)
            iteration(n_seq - 3, 1)
            iteration(n_seq - 2, 0, embedding=False)
            iteration(n_seq - 1, 1, embedding=False, project=False)
            ot_low(n_seq - 1, 0)
            ot_low(n_seq - 1, 1)
            add_output(n_seq - 1)

        @block.tensor
        def _(pe):
            def mm(dst, lhsT, rhs, start, stop):
                return nc.tensor.matmul(dst, lhsT, rhs, start=start, stop=stop)

            pe.wait_ge(wide_loaded, 16 * 9)
            for r in (0, 32):
                for c in range(CH):
                    last = mm(bank_t[0][r:r + 1, 0:D], bv_col[:, c:c + 1], stage_p[:, c, :], c == 0, c == CH - 1)
            last.then_inc(bias_sum, 1)
            pe.wait_ge(masks_ready, 3)
            pe.wait_ge(const_done, 1)

            def transpose_y(s, u):
                pe.wait_ge(y_ready, 2 * s + 2)
                wait(pe, qkv_lo, 8 * (s - 1) + HI_AT[4] if isinstance(s, int) else 8 * s + (HI_AT[4] - 8))
                nc.tensor.transpose(bank_w[0][:, 0:P], y[u][:, 0:P], ident[:])
                nc.tensor.transpose(bank_w[0][:, P:2 * P], y[u][:, P:2 * P], ident[:]).then_inc(xt_filled, 1)

            def project(s, u, j):
                w = bank_w[j % 2]
                if j == 0:
                    pe.wait_ge(xt_ready, 2 * s + 2)
                elif j == 1:
                    wait(pe, qkv_lo, 8 * s)
                else:
                    pe.wait_ge(qkv_lo, 8 * s + HI_AT[j - 2])
                parts = (xt_hi[u][:, 0:P], xt_alo[u][:], xt_b[u][:])
                if j < 4:
                    for c in range(3):
                        col = slice((3 * j + c) * P, (3 * j + c + 1) * P)
                        dst = w[:, c * P:(c + 1) * P]
                        for k, (x_part, w_part) in enumerate(w_qk.passes(*parts, col)):
                            mm(dst, w_part, x_part, k == 0, False)
                        last = mm(dst, bias_qk[:, col], ones_rows[:], False, True)
                else:
                    col = slice((j - 4) * HALF, (j - 3) * HALF)
                    for k, (x_part, w_part) in enumerate(w_v.passes(*parts, col)):
                        last = mm(w[:, 0:HALF], x_part, w_part, k == 0, k == 4)
                last.then_inc(qkv_filled, 1)

            def scores(t, u, g, b):
                if g == 0:
                    pe.wait_ge(qkv_lo, 8 * t + HI_AT[3])
                wait(pe, prob_ready, 4 * (3 * t + g - 1))
                for c in range(2 * g, 2 * g + 2):
                    dst = bank_s[b][:, (c - 2 * g) * 256:(c - 2 * g + 1) * 256]
                    col = slice(c * P, (c + 1) * P)
                    kh, kl = (kp[u][:, c, :, :].rearrange("p g k -> p (g k)") for kp in (kp_hi, kp_lo))
                    mm(dst, q_hi[u][:, col], kh, True, False)
                    mm(dst, q_hi[u][:, col], kl, False, False)
                    last = mm(dst, q_lo[u][:, col], kh, False, True)
                last.then_inc(scores_filled, 1)

            def transpose_prob(t, g, b):
                pe.wait_ge(prob_ready, 4 * (3 * t + g) + 4)
                wait(pe, pt_lo_ready, 3 * t + g - 1)
                for e in range(GROUP):
                    last = nc.tensor.transpose(bank_t[b][:, e * P:(e + 1) * P], prob[b][:, e, :], ident[:])
                last.then_inc(pt_filled, 1)

            def weigh_values(t, u, g, b):
                pe.wait_ge(pt_lo_ready, 3 * t + g + 1)
                if g == 0:
                    pe.wait_ge(qkv_lo, 8 * t + 8)
                    wait(pe, h_ready, t)
                for e in range(GROUP):
                    h = GROUP * g + e
                    o = bank_o[h // 6][:, (h % 6) * VW:(h % 6 + 1) * VW]
                    mm(o, pt_hi[b][:, e, :], v_hi[u][:, h, :], True, False)
                    mm(o, pt_lo[b][:, e, :], v_hi[u][:, h, :], False, False)
                    last = mm(o[:, 0:HD], pt_hi[b][:, e, :], v_lo[u][:, h, :], False, True)
                last.then_inc(heads_done, 1)

            def transpose_o(t, half):
                pe.wait_ge(o_ready, 2 * t + half + 1)
                for c in range(3):
                    last = nc.tensor.transpose(bank_o[half][:, c * P:(c + 1) * P],
                                               o_norm[:, 6 * half + 2 * c:6 * half + 2 * c + 2, :].rearrange("p h d -> p (h d)"),
                                               ident[:])
                last.then_inc(ot_filled, 1)

            def project_out(t):
                pe.wait_ge(ot_lo_ready, 2 * t + 2)
                dst = bank_o[0][:, 0:D]
                for c in range(CH):
                    mm(dst, ot_hi[:, c, :], wp_hi[:, c, :], c == 0, False)
                    mm(dst, ot_hi[:, c, :], wp_lo[:, c, :], False, False)
                    mm(dst, ot_lo[:, c, :], wp_hi[:, c, :], False, False)
                mm(dst, ones_rows[:], bias_out[:], False, True).then_inc(out_filled, 1)

            transpose_y(0, 0)
            for j in range(6):
                project(0, 0, j)
            transpose_y(1, 1)

            def iteration(t, u, output=True, proj=True, embed=True):
                b, n = u, 1 - u
                scores(t, u, 0, b)
                if proj:
                    project(t + 1, n, 0)
                if output:
                    transpose_o(t - 1, 0)
                    transpose_o(t - 1, 1)
                scores(t, u, 1, 1 - b)
                transpose_prob(t, 0, b)
                if proj:
                    project(t + 1, n, 1)
                if output:
                    project_out(t - 1)
                scores(t, u, 2, b)
                if proj:
                    project(t + 1, n, 2)
                transpose_prob(t, 1, 1 - b)
                weigh_values(t, u, 0, b)
                if proj:
                    project(t + 1, n, 3)
                weigh_values(t, u, 1, 1 - b)
                transpose_prob(t, 2, b)
                if proj:
                    project(t + 1, n, 4)
                    project(t + 1, n, 5)
                weigh_values(t, u, 2, b)
                if embed:
                    transpose_y(t + 2, u)

            iteration(0, 0, output=False)
            with pe.Fori(0, (n_seq - 4) // 2) as i:
                for v in range(2):
                    iteration(2 * i + 1 + v, 1 - v)
            iteration(n_seq - 3, 1)
            iteration(n_seq - 2, 0, embed=False)
            iteration(n_seq - 1, 1, embed=False, proj=False)
            transpose_o(n_seq - 1, 0)
            transpose_o(n_seq - 1, 1)
            project_out(n_seq - 1)


def second_attention(nc, A, h_all, ident, ones_rows, half_pow, psum, route, sb, sem, n_seq):
    HD = 16
    CH = 3
    QK = 2 * CH * P
    NG, GH = 4, 3
    VW = HD + 1
    SCALE = float(HD) ** -0.5 / (W_SCALE * W_SCALE)

    w_qk = Split(sb, "u_qk", QK)
    w_v = Split(sb, "u_v", D)
    w_p = Split(sb, "u_p", D)
    w_g = Split(sb, "u_g", N_EXP)
    bias_qk = sb("u_bias_qk", [P, QK], F16)
    bias_out = sb("u_bias_out", [P, D], F16)
    sel = sb("u_sel", [P, 2], F32)
    norm1 = sb("u_norm1", [P, 4], F32)
    norm2 = sb("u_norm2", [P, 4], F32)
    y_all = sb("u_y_all", [P, n_seq * D], F32)

    def pair(name, shape, dt):
        return [sb(f"{name}{u}", shape, dt) for u in range(2)]

    stats = [pair(f"u_stats_{k}", [P, 6], F32) for k in range(3)]
    moments = [pair(f"u_moments_{k}", [P, 2], F32) for k in range(3)]
    var_eps = [pair(f"u_var_eps_{k}", [P, 1], F32) for k in range(3)]
    rstd = [pair(f"u_rstd_{k}", [P, 1], F32) for k in range(3)]
    z = pair("u_z", [P, 2 * P], F32)
    xf = pair("u_xf", [P, 2 * P], F32)
    xt_hi = pair("u_xt_hi", [P, 2 * P], F16)
    xt_alo = pair("u_xt_alo", [P, P], F16)
    xt_b = pair("u_xt_b", [P, P], F16)
    q_hi = sb("u_q_hi", [P, CH * P], F16)
    q_st = pair("u_q_st", [P, CH * P], F16)
    k_hi = pair("u_k_hi", [P, CH * P], F16)
    k_lo = pair("u_k_lo", [P, CH * P], F16)
    v_hi = pair("u_v_hi", [P, HEADS, VW], F16)
    v_lo = pair("u_v_lo", [P, HEADS, HD], F16)
    row_max = pair("u_row_max", [P, GH], F32)
    neg_max = pair("u_neg_max", [P, GH], F32)
    prob = pair("u_prob", [P, GH, P], F32)
    pt_hi = pair("u_pt_hi", [P, GH * P], F16)
    pt_lo = pair("u_pt_lo", [P, GH * P], F16)
    recip = sb("u_recip", [P, HEADS], F32)
    o_norm = sb("u_o_norm", [P, HEADS + 4, HD], F32)
    ot_hi = sb("u_ot_hi", [P, 2 * P], F16)
    ot_alo = sb("u_ot_alo", [P, P], F16)
    ot_b = sb("u_ot_b", [P, P], F16)
    z2 = pair("u_z2", [P, 2 * P], F32)
    xf2 = sb("u_xf2", [P, 2 * P], F32)
    xm_hi = sb("u_xm_hi", [P, 2 * P], F16)
    xm_alo = sb("u_xm_alo", [P, P], F16)
    xm_b = sb("u_xm_b", [P, P], F16)
    logits = sb("u_logits", [P, N_EXP], F32)
    top = sb("u_top", [P, 8], F32)
    at = sb("u_at", [P, 8], U32)
    atf = sb("u_atf", [P, 2], F32)
    gap = sb("u_gap", [P, 1], F32)
    e2 = sb("u_e2", [P, 1], F32)
    den = sb("u_den", [P, 1], F32)
    minus_one = sb("u_minus_one", [P, 1], F32)
    picked = pair("u_picked", [P, 2, N_EXP], F32)
    picked_any = pair("u_picked_any", [P, N_EXP], F16)
    before = sb("u_before", [P, P], F16)
    all_ones = sb("u_all_ones", [P, P], F16)
    counted = pair("u_counted", [P, 2, N_EXP], F32)
    place = pair("u_place", [P, N_EXP], F32)
    picked_place = sb("u_picked_place", [P, N_EXP], F32)
    slot_f = pair("u_slot_f", [P, 2], F32)
    slot_now = pair("u_slot_now", [P, 2], I32)
    expert_no = sb("u_expert_no", [P, N_EXP], F32)
    stage = sb("u_stage", [P, 2, QK], F32)
    stage_v = sb("u_stage_v", [P, 2, D], F32)
    stage_p = sb("u_stage_p", [P, 2, D], F32)
    stage_g = sb("u_stage_g", [P, 2, N_EXP], F32)
    stage_bias = sb("u_stage_bias", [33, QK], F32)
    bqk_hi = sb("u_bqk_hi", [33, QK], F16)
    stage_bout = sb("u_stage_bout", [33, D], F32)
    bout_hi = sb("u_bout_hi", [33, D], F16)
    bv_col = sb("u_bv_col", [P, 2], F32)

    bank_st, bank_o, bank_w, bank_e = psum[0:4], psum[4], psum[5:7], psum[7]

    loaded = sem("b_loaded")
    weights_ready = sem("b_weights_ready")
    split_step = sem("b_split_step")
    bias_sum = sem("b_bias_sum")
    ln_step = [sem(f"b_ln{k}_step") for k in range(3)]
    rstd_ready = [sem(f"b_rstd{k}_ready") for k in range(3)]
    y_ready = sem("b_y_ready")
    z_ready = sem("b_z_ready")
    xt_filled = sem("b_xt_filled")
    xf_ready = sem("b_xf_ready")
    xt_hi_ready = sem("b_xt_hi_ready")
    xt_ready = sem("b_xt_ready")
    qkv_filled = sem("b_qkv_filled")
    qkv_hi = sem("b_qkv_hi")
    qkv_lo = sem("b_qkv_lo")
    scores_filled = sem("b_scores_filled")
    max_ready = sem("b_max_ready")
    neg_ready = sem("b_neg_ready")
    prob_ready = sem("b_prob_ready")
    pt_filled = sem("b_pt_filled")
    pt_hi_ready = sem("b_pt_hi_ready")
    pt_lo_ready = sem("b_pt_lo_ready")
    heads_done = sem("b_heads_done")
    recip_ready = sem("b_recip_ready")
    o_ready = sem("b_o_ready")
    ot_filled = sem("b_ot_filled")
    ot_hi_ready = sem("b_ot_hi_ready")
    ot_lo_ready = sem("b_ot_lo_ready")
    out_filled = sem("b_out_filled")
    x1_ready = sem("b_x1_ready")
    h_ready = sem("b_h_ready")
    z2_ready = sem("b_z2_ready")
    xm_filled = sem("b_xm_filled")
    xf2_ready = sem("b_xf2_ready")
    xm_hi_ready = sem("b_xm_hi_ready")
    xm_ready = sem("b_xm_ready")
    logits_filled = sem("b_logits_filled")
    logits_out = sem("b_logits_out")
    top_ready = sem("b_top_ready")
    at_ready = sem("b_at_ready")
    gap_ready = sem("b_gap_ready")
    e2_ready = sem("b_e2_ready")
    den_ready = sem("b_den_ready")
    gate_ready = sem("b_gate_ready")
    experts_kept = sem("b_experts_kept")
    atf_ready = sem("b_atf_ready")
    picked_ready = sem("b_picked_ready")
    any_ready = sem("b_any_ready")
    count_filled = sem("b_count_filled")
    count_out = sem("b_count_out")
    place_ready = sem("b_place_ready")
    running_ready = sem("b_running_ready")
    slot_ready = sem("b_slot_ready")
    slot_now_ready = sem("b_slot_now_ready")
    slot_kept = sem("b_slot_kept")
    queued = [sem(f"b_queued{u}") for u in range(2)]
    consts_ready = sem("b_consts_ready")

    def seq(s):
        return bass.ts(s, D)

    COUNTS = slice(2 * P + 2 * N_EXP, 2 * P + 4 * N_EXP)
    block = nc.Block()
    with block:
        @block.sync
        def _(sp):
            load_split(sp, loaded, stage, A["qk_dup_wT"], QK)
            load_split(sp, loaded, stage_v, A["L0_ffn_qkv_w"][:, 2 * D:3 * D], D)
            load_split(sp, loaded, stage_p, A["L0_ffn_proj_w"], D)
            load_split(sp, loaded, stage_g, A["L0_ffn_gate_w"], N_EXP)
            for r in (0, 32):
                sp.dma_start(stage_bias[r:r + 1, :], A["qk_dup_b"]).then_inc(loaded, 16)
                sp.dma_start(stage_bout[r:r + 1, :], A["L0_ffn_proj_b"]).then_inc(loaded, 16)
            with nc.allow_non_contiguous_dma(reason="columns of 192 numbers, once"):
                v_b = A["L0_ffn_qkv_b"][0, 2 * D:3 * D]
                sp.dma_start(bv_col[:, 0:1], v_b[0:P].unsqueeze(1)).then_inc(loaded, 16)
                sp.dma_start(bv_col[0:DB, 1:2], v_b[P:D].unsqueeze(1)).then_inc(loaded, 16)
                for tile, names in ((norm1, ("L0_ffn_ln1_g", "L0_ffn_ln1_b")), (norm2, ("L0_ffn_ln2_g", "L0_ffn_ln2_b"))):
                    for k, n in enumerate(names):
                        sp.dma_start(tile[:, k:k + 1], A[n][0, 0:P].unsqueeze(1)).then_inc(loaded, 16)
                        for r in (0, DB):
                            sp.dma_start(tile[r:r + DB, 2 + k:3 + k], A[n][0, P:D].unsqueeze(1)).then_inc(loaded, 16)
            sp.dma_start(sel[:], A["sel"]).then_inc(loaded, 16)
            sp.dma_start(expert_no[:], A["expert_no"].partition_broadcast(P)).then_inc(loaded, 16)
            sp.dma_start(route.running[:], A["queue_start"].partition_broadcast(P)).then_inc(loaded, 16)
        LOADS = 16 * (12 + 4 + 2 + 12 + 3)

        @block.gpsimd
        def _(pool):
            def rsqrt(k, s, u):
                pool.wait_ge(ln_step[k], 3 * s + 3)
                nc.gpsimd.tensor_tensor(rstd[k][u][:], var_eps[k][u][:], half_pow[:], ALU.pow).then_inc(rstd_ready[k], 1)

            def gate(s, u):
                at2 = bass.ds(2 * s, 1), bass.ds(2 * s + 1, 1)
                pool.wait_ge(top_ready, s + 1)
                wait(pool, e2_ready, s)
                nc.gpsimd.tensor_tensor(gap[:], top[:, 1:2], top[:, 0:1], ALU.subtract).then_inc(gap_ready, 1)
                waits_apart(pool, (loaded, LOADS), (at_ready, s + 1))
                nc.gpsimd.tensor_copy(atf[:], at[:, 0:2]).then_inc(atf_ready, 1)
                waits_apart(pool, (loaded, LOADS), (atf_ready, s + 1), (slot_ready, 2 * s - 2))
                nc.gpsimd.tensor_copy(route.experts[:, bass.ds(2 * s, 2)], atf[:]).then_inc(experts_kept, 1)
                for k in range(2):
                    nc.gpsimd.tensor_scalar(picked[u][:, k, :], expert_no[:], atf[:, k:k + 1], None, ALU.is_equal
                                            ).then_inc(picked_ready, 1)
                pool.wait_ge(picked_ready, 2 * s + 2)
                wait(pool, count_filled, s - 1)
                nc.gpsimd.tensor_tensor(picked_any[u][:], picked[u][:, 0, :], picked[u][:, 1, :], ALU.add).then_inc(any_ready, 1)
                waits_apart(pool, (loaded, LOADS), (e2_ready, s + 1))
                nc.gpsimd.tensor_scalar(den[:], e2[:], 1.0, None, ALU.add).then_inc(den_ready, 1)
                pool.wait_ge(den_ready, s + 1)
                nc.gpsimd.tensor_tensor(route.gates[:, at2[0]], den[:], minus_one[:], ALU.pow).then_inc(gate_ready, 1)
                pool.wait_ge(gate_ready, 2 * s + 1)
                nc.gpsimd.tensor_tensor(route.gates[:, at2[1]], route.gates[:, at2[0]], e2[:], ALU.mult).then_inc(gate_ready, 1)

            def places(s, u):
                pool.wait_ge(count_out, s + 1)
                wait(pool, running_ready, s)
                wait(pool, slot_ready, 2 * s)
                nc.gpsimd.tensor_tensor(place[u][:], counted[u][:, 0, :], route.running[:], ALU.add).then_inc(place_ready, 1)
                pool.wait_ge(place_ready, s + 1)
                nc.gpsimd.tensor_tensor(route.running[:], route.running[:], counted[u][:, 1, :], ALU.add).then_inc(running_ready, 1)

            def enqueue(s, u):
                waits_apart(pool, (loaded, LOADS), (slot_ready, 2 * s + 2), (queued[u], 16 * (s - u)))
                nc.gpsimd.tensor_copy(slot_now[u][:], slot_f[u][:]).then_inc(slot_now_ready, 1)
                waits_apart(pool, (loaded, LOADS), (slot_now_ready, s + 1))
                nc.gpsimd.tensor_copy(route.slots[:, bass.ds(2 * s, 2)], slot_now[u][:]).then_inc(slot_kept, 1)
                for k in range(2):
                    nc.gpsimd.indirect_dma_start(
                        out=route.x_queue, out_offset=bass.IndirectOffsetOnAxis(ap=slot_now[u][:, k:k + 1].bitcast(U32), axis=0),
                        in_=z2[u][:, :], in_offset=None).then_inc(queued[u], 16)

            nc.gpsimd.memset(minus_one[:], -1.0).then_inc(consts_ready, 1)
            nc.gpsimd.memset(all_ones[:], 1.0).then_inc(consts_ready, 1)
            pool.wait_ge(consts_ready, 2)
            nc.gpsimd.affine_select(out=before[:], in_=all_ones[:], compare_op=ALU.is_gt, fill=0.0, base=0,
                                    pattern=[[1, P]], channel_multiplier=-1).then_inc(consts_ready, 1)
            pool.wait_ge(loaded, LOADS)
            for s in range(2):
                rsqrt(0, s, s)
                rsqrt(1, s, s)

            def iteration(t, u, output=True, embed=True, queue=True):
                if queue:
                    places(t - 2, u)
                if embed:
                    rsqrt(0, t + 2, u)
                if output:
                    rsqrt(2, t - 1, 1 - u)
                if embed:
                    rsqrt(1, t + 2, u)
                if queue:
                    enqueue(t - 2, u)
                if output:
                    gate(t - 1, 1 - u)

            iteration(0, 0, output=False, queue=False)
            iteration(1, 1, queue=False)
            with pool.Fori(0, (n_seq - 4) // 2) as i:
                for v in range(2):
                    iteration(2 * i + 2 + v, v)
            iteration(n_seq - 2, 0, embed=False)
            iteration(n_seq - 1, 1, embed=False)
            places(n_seq - 2, 0)
            rsqrt(2, n_seq - 1, 1)
            enqueue(n_seq - 2, 0)
            gate(n_seq - 1, 1)
            places(n_seq - 1, 1)
            enqueue(n_seq - 1, 1)
            for u in range(2):
                pool.wait_ge(queued[u], 16 * n_seq)

        @block.scalar
        def _(act):
            def to_hi(dst, src):
                return nc.scalar.activation(dst, src, ACT.Copy, scale=W_SCALE)

            act.wait_ge(loaded, LOADS)
            for w, st in ((w_qk, stage), (w_v, stage_v), (w_p, stage_p), (w_g, stage_g)):
                to_hi(w.a_hi[:], st[:, 0, :]).then_inc(weights_ready, 1)
                to_hi(w.b_hi[:], st[:, 1, :]).then_inc(weights_ready, 1)
            to_hi(bqk_hi[0:1, :], stage_bias[0:1, :]).then_inc(weights_ready, 1)
            to_hi(bqk_hi[32:33, :], stage_bias[32:33, :]).then_inc(weights_ready, 1)

            def affine(dst, bank, norm, sems, first_wait):
                first_wait()
                for k in range(2):
                    nc.scalar.activation(dst[:, k * P:(k + 1) * P], bank[:, k * P:(k + 1) * P], ACT.Identity,
                                         bias=norm[:, 2 * k + 1:2 * k + 2], scale=norm[:, 2 * k:2 * k + 1]).then_inc(sems, 1)

            def xt_affine(s, u):
                act.wait_ge(xt_filled, s + 1)
                affine(xf[u], bank_w[0], norm1, xf_ready, lambda: wait(act, xt_ready, 2 * s - 2))

            def xt_high(s, u):
                act.wait_ge(xf_ready, 2 * s + 2)
                wait(act, qkv_filled, 3 * s - 3)
                nc.scalar.copy(xt_hi[u][:], xf[u][:]).then_inc(xt_hi_ready, 1)

            def qkv_high(s, u, j):
                act.wait_ge(qkv_filled, 3 * s + j + 1)
                w = bank_w[j % 2]
                if j == 0:
                    wait(act, qkv_lo, 3 * s - 2)
                    nc.scalar.copy(q_hi[:], w[:, 0:HALF]).then_inc(qkv_hi, 1)
                elif j == 1:
                    wait(act, scores_filled, 4 * s - 4)
                    nc.scalar.copy(k_hi[u][:], w[:, 0:HALF]).then_inc(qkv_hi, 1)
                else:
                    wait(act, heads_done, 4 * s - 4)
                    nc.scalar.copy(v_hi[u][:, :, 0:HD], w[:, 0:D].rearrange("p (h d) -> p h d", d=HD)).then_inc(qkv_hi, 1)

            def exps(t, g):
                act.wait_ge(neg_ready, 4 * t + g + 1)
                wait(act, pt_filled, 4 * t + g - 1)
                for e in range(GH):
                    nc.scalar.activation(prob[g % 2][:, e, :], bank_st[g][:, e * P:(e + 1) * P], ACT.Exp,
                                         bias=neg_max[g % 2][:, e:e + 1], scale=SCALE).then_inc(prob_ready, 1)

            def pt_high(t, g):
                act.wait_ge(pt_filled, 4 * t + g + 1)
                wait(act, heads_done, 4 * t + g - 1)
                nc.scalar.copy(pt_hi[g % 2][:], bank_st[g][:, 0:HALF]).then_inc(pt_hi_ready, 1)

            def ot_high(t):
                act.wait_ge(ot_filled, t + 1)
                wait(act, out_filled, t)
                nc.scalar.copy(ot_hi[:], bank_e[:, 0:2 * P]).then_inc(ot_hi_ready, 1)

            def xm_affine(t):
                act.wait_ge(xm_filled, t + 1)
                affine(xf2, bank_e, norm2, xf2_ready, lambda: wait(act, xm_ready, 2 * t))

            def xm_high(t):
                act.wait_ge(xf2_ready, 2 * t + 2)
                wait(act, logits_filled, t)
                nc.scalar.copy(xm_hi[:], xf2[:]).then_inc(xm_hi_ready, 1)

            def second_exp(t):
                act.wait_ge(gap_ready, t + 1)
                wait(act, gate_ready, 2 * t)
                nc.scalar.activation(e2[:], gap[:], ACT.Exp).then_inc(e2_ready, 1)

            xt_affine(0, 0)
            xt_high(0, 0)
            for j in range(3):
                qkv_high(0, 0, j)
            xt_affine(1, 1)
            xt_high(1, 1)

            def iteration(t, u, output=True, project=True, embed=True):
                n = 1 - u
                exps(t, 0)
                if output:
                    ot_high(t - 1)
                exps(t, 1)
                if project:
                    qkv_high(t + 1, n, 0)
                pt_high(t, 0)
                exps(t, 2)
                if project:
                    qkv_high(t + 1, n, 1)
                pt_high(t, 1)
                exps(t, 3)
                if output:
                    xm_affine(t - 1)
                pt_high(t, 2)
                if output:
                    xm_high(t - 1)
                if project:
                    qkv_high(t + 1, n, 2)
                pt_high(t, 3)
                if embed:
                    xt_affine(t + 2, u)
                if output:
                    second_exp(t - 1)
                if embed:
                    xt_high(t + 2, u)

            iteration(0, 0, output=False)
            iteration(1, 1)
            with act.Fori(0, (n_seq - 4) // 2) as i:
                for v in range(2):
                    iteration(2 * i + 2 + v, v)
            iteration(n_seq - 2, 0, embed=False)
            iteration(n_seq - 1, 1, embed=False, project=False)
            ot_high(n_seq - 1)
            xm_affine(n_seq - 1)
            xm_high(n_seq - 1)
            second_exp(n_seq - 1)

        @block.vector
        def _(dve):
            def to_lo(dst, src, hi):
                return nc.vector.scalar_tensor_tensor(dst, src, W_SCALE, hi, ALU.mult, ALU.subtract)

            nc.vector.memset(bias_qk[:], 0.0).then_inc(split_step, 1)
            nc.vector.memset(bias_out[:], 0.0).then_inc(split_step, 1)
            for u in range(2):
                nc.vector.memset(v_hi[u][:, :, HD:VW], 1.0).then_inc(split_step, 1)
            dve.wait_ge(weights_ready, 10)
            for w, st in ((w_qk, stage), (w_v, stage_v), (w_p, stage_p), (w_g, stage_g)):
                to_lo(w.a_lo[:], st[:, 0, :], w.a_hi[:]).then_inc(split_step, 1)
                to_lo(w.b_lo[:], st[:, 1, :], w.b_hi[:]).then_inc(split_step, 1)
            dve.wait_ge(split_step, 2)
            nc.vector.tensor_copy(bias_qk[0:1, :], bqk_hi[0:1, :]).then_inc(split_step, 1)
            to_lo(bias_qk[32:33, :], stage_bias[32:33, :], bqk_hi[32:33, :]).then_inc(split_step, 1)
            dve.wait_ge(bias_sum, 1)
            for r in (0, 32):
                nc.vector.tensor_tensor(stage_bout[r:r + 1, :], bank_e[r:r + 1, 0:D], stage_bout[r:r + 1, :], ALU.add
                                        ).then_inc(split_step, 1)
            dve.wait_ge(split_step, 16)
            for r in (0, 32):
                nc.vector.tensor_scalar(bout_hi[r:r + 1, :], stage_bout[r:r + 1, :], W_SCALE * W_SCALE, None, ALU.mult
                                        ).then_inc(split_step, 1)
            dve.wait_ge(split_step, 18)
            nc.vector.tensor_copy(bias_out[0:1, :], bout_hi[0:1, :]).then_inc(split_step, 1)
            nc.vector.scalar_tensor_tensor(bias_out[32:33, :], stage_bout[32:33, :], W_SCALE * W_SCALE, bout_hi[32:33, :],
                                           ALU.mult, ALU.subtract).then_inc(split_step, 1)
            dve.wait_ge(split_step, 20)

            def ln(k, s, u, src, *waits):
                waits_apart(dve, (loaded, LOADS), *waits)
                nc.vector.bn_stats(stats[k][u][:], src).then_inc(ln_step[k], 1)
                waits_apart(dve, (loaded, LOADS), (ln_step[k], 3 * s + 1))
                nc.vector.bn_aggr(moments[k][u][:], stats[k][u][:]).then_inc(ln_step[k], 1)
                dve.wait_ge(ln_step[k], 3 * s + 2)
                nc.vector.tensor_scalar(var_eps[k][u][:], moments[k][u][:, 1:2], LN_EPS, None, ALU.add).then_inc(ln_step[k], 1)

            def ln_h(s, u):
                ln(0, s, u, h_all[:, seq(s)], (y_ready, s - 1))

            def make_y(s, u):
                dve.wait_ge(rstd_ready[0], s + 1)
                nc.vector.tensor_scalar(y_all[:, seq(s)], h_all[:, seq(s)], moments[0][u][:, 0:1], rstd[0][u][:, 0:1],
                                        ALU.subtract, ALU.mult).then_inc(y_ready, 1)

            def ln_y(s, u):
                ln(1, s, u, y_all[:, seq(s)], (y_ready, s + 1), (z_ready, 2 * s - 2))

            def make_z(s, u):
                dve.wait_ge(rstd_ready[1], s + 1)
                wait(dve, xt_filled, s - 1)
                for dst, src in ((z[u][:, 0:D], y_all[:, seq(s)]), (z[u][:, D:2 * P], y_all[:, bass.ds(s * D + P, DB)])):
                    nc.vector.tensor_scalar(dst, src, moments[1][u][:, 0:1], rstd[1][u][:, 0:1],
                                            ALU.subtract, ALU.mult).then_inc(z_ready, 1)

            def low_parts(alo, b, hi, full, sems):
                nc.vector.tensor_tensor(alo, full[:, 0:P], hi[:, 0:P], ALU.subtract).then_inc(sems, 1)
                nc.vector.scalar_tensor_tensor(b, hi[:, P:2 * P], sel[:, 0:1], full[:, P:2 * P], ALU.mult, ALU.add
                                               ).then_inc(sems, 1)

            def xt_low(s, u):
                dve.wait_ge(xt_hi_ready, s + 1)
                low_parts(xt_alo[u][:], xt_b[u][:], xt_hi[u], xf[u], xt_ready)

            def qkv_low(s, u, j):
                dve.wait_ge(qkv_hi, 3 * s + j + 1)
                w = bank_w[j % 2]
                if j == 0:
                    wait(dve, scores_filled, 4 * s - 4)
                    nc.vector.scalar_tensor_tensor(q_st[u][:], q_hi[:], sel[:, 1:2], w[:, 0:HALF], ALU.mult, ALU.add
                                                   ).then_inc(qkv_lo, 1)
                elif j == 1:
                    nc.vector.tensor_tensor(k_lo[u][:], w[:, 0:HALF], k_hi[u][:], ALU.subtract).then_inc(qkv_lo, 1)
                else:
                    nc.vector.tensor_tensor(v_lo[u][:], w[:, 0:D].rearrange("p (h d) -> p h d", d=HD), v_hi[u][:, :, 0:HD],
                                            ALU.subtract).then_inc(qkv_lo, 1)

            def maxima(t, g):
                dve.wait_ge(scores_filled, 4 * t + g + 1)
                wait(dve, neg_ready, 4 * t + g - 1)
                nc.vector.tensor_reduce(row_max[g % 2][:], bank_st[g][:, 0:HALF].rearrange("p (e k) -> p e k", k=P), AX, ALU.max
                                        ).then_inc(max_ready, 1)
                dve.wait_ge(max_ready, 4 * t + g + 1)
                wait(dve, prob_ready, 3 * (4 * t + g - 1))
                nc.vector.tensor_scalar(neg_max[g % 2][:], row_max[g % 2][:], -SCALE, None, ALU.mult).then_inc(neg_ready, 1)

            def pt_low(t, g):
                dve.wait_ge(pt_hi_ready, 4 * t + g + 1)
                nc.vector.tensor_tensor(pt_lo[g % 2][:], bank_st[g][:, 0:HALF], pt_hi[g % 2][:], ALU.subtract).then_inc(pt_lo_ready, 1)

            def normalise(t):
                o_view = bank_o[:, 0:HEADS * VW].rearrange("p (h d) -> p h d", d=VW)
                dve.wait_ge(heads_done, 4 * t + 4)
                wait(dve, o_ready, 2 * t)
                nc.vector.reciprocal(recip[:], o_view[:, :, HD]).then_inc(recip_ready, 1)
                dve.wait_ge(recip_ready, t + 1)
                wait(dve, ot_filled, t)
                for dst, src in ((slice(0, HEADS), slice(0, HEADS)), (slice(HEADS, HEADS + 4), slice(8, HEADS))):
                    n_heads = src.stop - src.start
                    nc.vector.tensor_tensor(o_norm[:, dst, :], o_view[:, src, 0:HD],
                                            recip[:, src].unsqueeze(2).to_broadcast([P, n_heads, HD]), ALU.mult).then_inc(o_ready, 1)

            def ot_low(t):
                dve.wait_ge(ot_hi_ready, t + 1)
                low_parts(ot_alo[:], ot_b[:], ot_hi, bank_e, ot_lo_ready)

            def make_x1(t):
                dve.wait_ge(out_filled, t + 1)
                nc.vector.scalar_tensor_tensor(y_all[:, seq(t)], bank_e[:, 0:D], 1.0 / (W_SCALE * W_SCALE), y_all[:, seq(t)],
                                               ALU.mult, ALU.add).then_inc(x1_ready, 1)

            def ln_x1(t, u):
                ln(2, t, u, y_all[:, seq(t)], (x1_ready, t + 1), (z2_ready, 2 * t))

            def make_z2(t, u):
                dve.wait_ge(rstd_ready[2], t + 1)
                wait(dve, queued[u], 16 * (t - u))
                for dst, src in ((z2[u][:, 0:D], y_all[:, seq(t)]), (z2[u][:, D:2 * P], y_all[:, bass.ds(t * D + P, DB)])):
                    nc.vector.tensor_scalar(dst, src, moments[2][u][:, 0:1], rstd[2][u][:, 0:1],
                                            ALU.subtract, ALU.mult).then_inc(z2_ready, 1)

            def add_x1(t):
                dve.wait_ge(x1_ready, t + 1)
                nc.vector.tensor_tensor(h_all[:, seq(t)], h_all[:, seq(t)], y_all[:, seq(t)], ALU.add).then_inc(h_ready, 1)

            def xm_low(t):
                dve.wait_ge(xm_hi_ready, t + 1)
                wait(dve, logits_filled, t)
                low_parts(xm_alo[:], xm_b[:], xm_hi, xf2, xm_ready)

            def gate(t):
                dve.wait_ge(logits_filled, t + 1)
                nc.vector.tensor_scalar(logits[:], bank_e[:, 2 * P:2 * P + N_EXP], 1.0 / W_SCALE, None, ALU.mult).then_inc(logits_out, 1)
                waits_apart(dve, (loaded, LOADS), (logits_out, t + 1), (gap_ready, t))
                nc.vector.max(top[:], logits[:]).then_inc(top_ready, 1)
                waits_apart(dve, (loaded, LOADS), (top_ready, t + 1), (atf_ready, t))
                nc.vector.max_index(at[:], top[:], logits[:]).then_inc(at_ready, 1)

            def counts(t, u):
                dve.wait_ge(count_filled, t + 1)
                wait(dve, running_ready, t)
                nc.vector.tensor_copy(counted[u][:].rearrange("p a e -> p (a e)"), bank_e[:, COUNTS]).then_inc(count_out, 1)

            def slots(t, u):
                dve.wait_ge(place_ready, t + 1)
                wait(dve, slot_now_ready, t)
                for k in range(2):
                    wait(dve, slot_ready, 2 * t + k)
                    nc.vector.tensor_tensor_reduce(picked_place[:], picked[u][:, k, :], place[u][:], 1.0, 0.0, ALU.mult, ALU.add,
                                                   slot_f[u][:, k:k + 1]).then_inc(slot_ready, 1)

            def norms(s, u):
                ln_h(s, u)
                make_y(s, u)
                ln_y(s, u)
                make_z(s, u)

            norms(0, 0)
            xt_low(0, 0)
            for j in range(3):
                qkv_low(0, 0, j)
            norms(1, 1)
            xt_low(1, 1)

            def iteration(t, u, output=True, project=True, embed=True, queue=True):
                n, s = 1 - u, t + 2
                maxima(t, 0)
                if queue:
                    counts(t - 2, u)
                if output:
                    normalise(t - 1)
                maxima(t, 1)
                if output:
                    ot_low(t - 1)
                if project:
                    qkv_low(t + 1, n, 0)
                if queue:
                    slots(t - 2, u)
                if embed:
                    ln_h(s, u)
                pt_low(t, 0)
                if output:
                    make_x1(t - 1)
                    ln_x1(t - 1, n)
                maxima(t, 2)
                if embed:
                    make_y(s, u)
                if project:
                    qkv_low(t + 1, n, 1)
                if output:
                    make_z2(t - 1, n)
                pt_low(t, 1)
                if embed:
                    ln_y(s, u)
                maxima(t, 3)
                if output:
                    add_x1(t - 1)
                if embed:
                    make_z(s, u)
                pt_low(t, 2)
                if output:
                    xm_low(t - 1)
                if project:
                    qkv_low(t + 1, n, 2)
                pt_low(t, 3)
                if output:
                    gate(t - 1)
                if embed:
                    xt_low(s, u)

            iteration(0, 0, output=False, queue=False)
            iteration(1, 1, queue=False)
            with dve.Fori(0, (n_seq - 4) // 2) as i:
                for v in range(2):
                    iteration(2 * i + 2 + v, v)
            iteration(n_seq - 2, 0, embed=False)
            iteration(n_seq - 1, 1, embed=False, project=False)
            t = n_seq - 1
            counts(t - 1, 0)
            slots(t - 1, 0)
            normalise(t)
            ot_low(t)
            make_x1(t)
            ln_x1(t, 1)
            make_z2(t, 1)
            add_x1(t)
            xm_low(t)
            gate(t)
            counts(t, 1)
            slots(t, 1)

        @block.tensor
        def _(pe):
            def mm(dst, lhsT, rhs, start, stop):
                return nc.tensor.matmul(dst, lhsT, rhs, start=start, stop=stop)

            pe.wait_ge(loaded, LOADS)
            for r in (0, 32):
                mm(bank_e[r:r + 1, 0:D], bv_col[:, 0:1], stage_p[:, 0, :], True, False)
                last = mm(bank_e[r:r + 1, 0:D], bv_col[0:DB, 1:2], stage_p[0:DB, 1, :], False, True)
            last.then_inc(bias_sum, 1)
            pe.wait_ge(split_step, 20)

            def transpose_x(bank, src):
                nc.tensor.transpose(bank[:, 0:P], src[:, 0:P], ident[:])
                return nc.tensor.transpose(bank[:, P:2 * P], src[:, P:2 * P], ident[:])

            def transpose_z(s, u):
                pe.wait_ge(z_ready, 2 * s + 2)
                wait(pe, qkv_lo, 3 * s)
                transpose_x(bank_w[0], z[u]).then_inc(xt_filled, 1)

            def project(s, u, j):
                w = bank_w[j % 2]
                if j == 0:
                    pe.wait_ge(xt_ready, 2 * s + 2)
                elif j == 1:
                    wait(pe, qkv_lo, 3 * s - 1)
                else:
                    pe.wait_ge(qkv_lo, 3 * s + 1)
                parts = (xt_hi[u][:, 0:P], xt_alo[u][:], xt_b[u][:])
                if j < 2:
                    for c in range(CH):
                        col = slice((CH * j + c) * P, (CH * j + c + 1) * P)
                        dst = w[:, c * P:(c + 1) * P]
                        for k, (x_part, w_part) in enumerate(w_qk.passes(*parts, col)):
                            mm(dst, w_part, x_part, k == 0, False)
                        last = mm(dst, bias_qk[:, col], ones_rows[:], False, True)
                else:
                    for k, (x_part, w_part) in enumerate(w_v.passes(*parts, slice(0, D))):
                        last = mm(w[:, 0:D], x_part, w_part, k == 0, k == 4)
                last.then_inc(qkv_filled, 1)

            def scores(t, u, g):
                if g == 0:
                    pe.wait_ge(qkv_lo, 3 * t + 2)
                wait(pe, pt_lo_ready, 4 * t + g - 3)
                r = slice(32 * g, 32 * g + 32)
                for c in range(GH):
                    col = slice(c * P, (c + 1) * P)
                    mm(bank_st[g][:, col], q_st[u][r, col], k_hi[u][r, col], True, False)
                    last = mm(bank_st[g][:, col], q_st[u][r, col], k_lo[u][r, col], False, True)
                last.then_inc(scores_filled, 1)

            def transpose_prob(t, g):
                pe.wait_ge(prob_ready, 3 * (4 * t + g) + 3)
                for e in range(GH):
                    last = nc.tensor.transpose(bank_st[g][:, e * P:(e + 1) * P], prob[g % 2][:, e, :], ident[:])
                last.then_inc(pt_filled, 1)

            def weigh_values(t, u, g):
                pe.wait_ge(pt_lo_ready, 4 * t + g + 1)
                if g == 0:
                    pe.wait_ge(qkv_lo, 3 * t + 3)
                    wait(pe, o_ready, 2 * t)
                for e in range(GH):
                    h = 4 * e + g
                    o = bank_o[:, h * VW:(h + 1) * VW]
                    col = slice(e * P, (e + 1) * P)
                    mm(o, pt_hi[g % 2][:, col], v_hi[u][:, h, :], True, False)
                    mm(o, pt_lo[g % 2][:, col], v_hi[u][:, h, :], False, False)
                    last = mm(o[:, 0:HD], pt_hi[g % 2][:, col], v_lo[u][:, h, :], False, True)
                last.then_inc(heads_done, 1)

            def transpose_o(t):
                pe.wait_ge(o_ready, 2 * t + 2)
                wait(pe, logits_out, t)
                transpose_x(bank_e, o_norm[:].rearrange("p h d -> p (h d)")).then_inc(ot_filled, 1)

            def project_out(t):
                pe.wait_ge(ot_lo_ready, 2 * t + 2)
                for k, (o_part, w_part) in enumerate(w_p.passes(ot_hi[:, 0:P], ot_alo[:], ot_b[:], slice(0, D))):
                    mm(bank_e[:, 0:D], o_part, w_part, k == 0, False)
                mm(bank_e[:, 0:D], ones_rows[:], bias_out[:], False, True).then_inc(out_filled, 1)

            def transpose_z2(t, u):
                pe.wait_ge(z2_ready, 2 * t + 2)
                transpose_x(bank_e, z2[u]).then_inc(xm_filled, 1)

            def gate_logits(t):
                pe.wait_ge(xm_ready, 2 * t + 2)
                for k, (x_part, w_part) in enumerate(w_g.passes(xm_hi[:, 0:P], xm_alo[:], xm_b[:], slice(0, N_EXP))):
                    last = mm(bank_e[:, 2 * P:2 * P + N_EXP], x_part, w_part, k == 0, k == 4)
                last.then_inc(logits_filled, 1)

            def count(t, u):
                pe.wait_ge(any_ready, t + 1)
                wait(pe, count_out, t)
                at = COUNTS.start
                mm(bank_e[:, at:at + N_EXP], before[:], picked_any[u][:], True, True)
                mm(bank_e[:, at + N_EXP:at + 2 * N_EXP], all_ones[:], picked_any[u][:], True, True).then_inc(count_filled, 1)

            pe.wait_ge(consts_ready, 3)
            transpose_z(0, 0)
            for j in range(3):
                project(0, 0, j)
            transpose_z(1, 1)

            def iteration(t, u, output=True, proj=True, embed=True, queue=True):
                n = 1 - u
                scores(t, u, 0)
                if queue:
                    count(t - 2, u)
                scores(t, u, 1)
                if output:
                    transpose_o(t - 1)
                if proj:
                    project(t + 1, n, 0)
                scores(t, u, 2)
                transpose_prob(t, 0)
                scores(t, u, 3)
                if output:
                    project_out(t - 1)
                transpose_prob(t, 1)
                weigh_values(t, u, 0)
                if proj:
                    project(t + 1, n, 1)
                transpose_prob(t, 2)
                weigh_values(t, u, 1)
                if output:
                    transpose_z2(t - 1, n)
                transpose_prob(t, 3)
                if proj:
                    project(t + 1, n, 2)
                weigh_values(t, u, 2)
                if output:
                    gate_logits(t - 1)
                weigh_values(t, u, 3)
                if embed:
                    transpose_z(t + 2, u)

            iteration(0, 0, output=False, queue=False)
            iteration(1, 1, queue=False)
            with pe.Fori(0, (n_seq - 4) // 2) as i:
                for v in range(2):
                    iteration(2 * i + 2 + v, v)
            iteration(n_seq - 2, 0, embed=False)
            iteration(n_seq - 1, 1, embed=False, proj=False)
            count(n_seq - 2, 0)
            transpose_o(n_seq - 1)
            project_out(n_seq - 1)
            transpose_z2(n_seq - 1, 1)
            gate_logits(n_seq - 1)
            count(n_seq - 1, 1)


class Route:

    def __init__(self, nc, sb, n_seq):
        self.tokens = n_seq * P
        self.stride = self.tokens + TILE
        self.x_queue = nc.dram_tensor("x_queue", [N_EXP * self.stride, 2 * P], F32, kind="Internal").ap()
        self.slots = sb("route_slots", [P, 2 * n_seq], I32)
        self.experts = sb("route_experts", [P, 2 * n_seq], F32)
        self.gates = sb("route_gates", [P, 2 * n_seq], F32)
        self.running = sb("route_running", [P, N_EXP], F32)
        self.tiles = 2 * self.tokens // TILE + N_EXP
        self.y_tiles = nc.dram_tensor("y_tiles", [self.tiles * TILE, D], F32, kind="Internal").ap()


def experts(nc, A, h_all, ident, ones_rows, psum, route, sb, sem, n_seq):
    NT = route.tiles
    A2 = TILE // P
    w1 = Split(sb, "w1", N_EXP * HID)
    w2_hi = sb("w2_hi", [P, N_EXP * HC, D], F16)
    w2_lo = sb("w2_lo", [P, N_EXP * HC, D], F16)
    b1 = sb("b1", [P, N_EXP * HC], F32)
    bias2 = sb("bias2", [P, N_EXP, D], F16)
    stage1 = sb("stage1", [P, 2, HID], F32)
    stage2 = sb("stage2", [P, HC, D], F32)
    stage_b2 = sb("stage_b2", [33, N_EXP, D], F32)
    b2_hi = sb("b2_hi", [33, N_EXP, D], F16)
    norm2 = sb("norm2", [P, 4], F32)
    zeros = sb("zeros", [P, A2, 2 * P], F32)
    consts = sb("consts", [P, 2, N_EXP], F32)
    tile_no = sb("tile_no", [1, NT], F32)
    filled = sb("filled", [P, N_EXP], F32)
    filled_i = sb("filled_i", [P, N_EXP], I32)
    end_i = sb("end_i", [P, N_EXP], I32)
    tiles_i = sb("tiles_i", [P, N_EXP], I32)
    tiles = sb("tiles", [P, N_EXP], F32)
    upto = [sb(f"upto{k}", [P, N_EXP], F32) for k in range(4)]
    first = sb("first", [P, N_EXP], F32)
    last_row = sb("last_row", [P, N_EXP], F32)
    shift = sb("shift", [P, N_EXP], F32)
    moved = [sb(f"moved{k}", [P, 2 * n_seq], F32) for k in range(3)]
    t_a = sb("t_a", [1, NT, N_EXP], F32)
    t_b = sb("t_b", [1, NT, N_EXP], F32)
    t_q = sb("t_q", [1, NT, N_EXP], F32)
    t_e = sb("t_e", [1, NT], F32)
    t_r = sb("t_r", [1, NT], F32)
    tile_expert = sb("tile_expert", [1, NT], I32)
    tile_row = sb("tile_row", [1, NT], I32)
    t_c = sb("t_c", [1, NT, N_EXP], F32)

    def pair(name, shape, dt):
        return [sb(f"{name}{u}", shape, dt) for u in range(2)]

    x_rows = pair("x_rows", [P, A2, 2 * P], F32)
    xf = sb("c_xf", [P, 2, TILE], F32)
    x_hi = pair("c_x_hi", [P, 2, TILE], F16)
    x_alo = pair("c_x_alo", [P, TILE], F16)
    x_b = pair("c_x_b", [P, TILE], F16)
    sel = sb("c_sel", [P, 2], F32)
    hf = pair("hf", [P, TILE], F32)
    h_hi = pair("h_hi", [P, TILE], F16)
    h_lo = pair("h_lo", [P, TILE], F16)
    y_out = pair("y_out", [P, A2, D], F32)
    bank_x, bank_h, bank_y = psum[0:2], psum[2:6], psum[6:8]

    loaded = sem("c_loaded")
    weights_loaded = sem("c_weights_loaded")
    hi_ready = sem("c_hi_ready")
    split_ready = sem("c_split_ready")
    zeroed = sem("c_zeroed")
    table_step = sem("c_table_step")
    padded = sem("c_padded")
    x_loaded = [sem(f"c_x_loaded{u}") for u in range(2)]
    x_filled = sem("c_x_filled")
    xf_ready = sem("c_xf_ready")
    x_hi_ready = sem("c_x_hi_ready")
    x_ready = sem("c_x_ready")
    h_filled = sem("c_h_filled")
    gelu_ready = sem("c_gelu_ready")
    h_hi_ready = sem("c_h_hi_ready")
    h_lo_ready = sem("c_h_lo_ready")
    chunk_used = sem("c_chunk_used")
    y_ready = sem("c_y_ready")
    y_stored = [sem(f"c_y_stored{u}") for u in range(2)]
    TABLE_STEPS = 20

    block = nc.Block()
    with block:
        @block.sync
        def _(sp):
            sp.dma_start(sel[:], A["sel"]).then_inc(loaded, 16)
            sp.dma_start(consts[:, 0, :], A["expert_no"].partition_broadcast(P)).then_inc(loaded, 16)
            sp.dma_start(consts[:, 1, :], A["queue_start"].partition_broadcast(P)).then_inc(loaded, 16)
            sp.dma_start(tile_no[:], A["tile_no"]).then_inc(loaded, 16)
            with nc.allow_non_contiguous_dma(reason="bias columns, once"):
                sp.dma_start(b1[:], A["L0_ffn_b1"].rearrange("e (c p) -> p (e c)", p=P)).then_inc(loaded, 16)
                for k, n in enumerate(("L0_ffn_ln2_g", "L0_ffn_ln2_b")):
                    sp.dma_start(norm2[:, k:k + 1], A[n][0, 0:P].unsqueeze(1)).then_inc(loaded, 16)
                    for r in (0, DB):
                        sp.dma_start(norm2[r:r + DB, 2 + k:3 + k], A[n][0, P:D].unsqueeze(1)).then_inc(loaded, 16)
            for r in (0, 32):
                sp.dma_start(stage_b2[r:r + 1, :, :], A["L0_ffn_b2"].unsqueeze(0)).then_inc(loaded, 16)
            for e in range(N_EXP):
                wait(sp, split_ready, 2 + 3 * e if e else 0)
                load_split(sp, weights_loaded, stage1, A["L0_ffn_w1"][e], HID)
                sp.dma_start(stage2[:], A["L0_ffn_w2"][e].rearrange("(c p) d -> p c d", p=P)).then_inc(weights_loaded, 16)

            with sp.Fori(0, NT // 2) as i:
                for u in range(2):
                    j = 2 * i + u
                    sp.wait_ge(y_ready, j + 1)
                    sp.dma_start(route.y_tiles[bass.ts(j, TILE), :].rearrange("(a p) d -> p a d", p=P), y_out[u][:]
                                 ).then_inc(y_stored[u], 16)
            for u in range(2):
                sp.wait_ge(y_stored[u], 8 * NT)
        LOADS = 16 * 13

        @block.gpsimd
        def _(pool):
            nc.gpsimd.memset(zeros[:], 0.0).then_inc(zeroed, 1)
            pool.wait_ge(zeroed, 1)
            pool.wait_ge(table_step, TABLE_STEPS)
            for e in range(N_EXP):
                end = pool.value_load(end_i[0:1, e:e + 1], min_val=0, max_val=N_EXP * route.stride - TILE)
                pool.dma_start(route.x_queue[bass.ds(end, TILE), :].rearrange("(a p) d -> p a d", p=P), zeros[:]).then_inc(padded, 16)
            pool.wait_ge(padded, 16 * N_EXP)

            def load(j, u):
                wait(pool, x_filled, j - 1)
                row = pool.value_load(tile_row[0:1, bass.ds(j, 1)], min_val=0, max_val=N_EXP * route.stride - TILE)
                pool.dma_start(x_rows[u][:], route.x_queue[bass.ds(row, TILE), :].rearrange("(a p) d -> p a d", p=P)
                               ).then_inc(x_loaded[u], 16)

            load(0, 0)
            load(1, 1)
            with pool.Fori(0, NT // 2 - 1) as i:
                for u in range(2):
                    load(2 * i + 2 + u, u)

        @block.scalar
        def _(act):
            act.wait_ge(loaded, LOADS)
            for r in (0, 32):
                nc.scalar.activation(b2_hi[r:r + 1, :, :], stage_b2[r:r + 1, :, :], ACT.Copy, scale=W_SCALE).then_inc(hi_ready, 1)
            for e in range(N_EXP):
                act.wait_ge(weights_loaded, 64 * e + 64)
                c = slice(e * HID, (e + 1) * HID)
                for dst, src in ((w1.a_hi[:, c], stage1[:, 0, :]), (w1.b_hi[:, c], stage1[:, 1, :]),
                                 (w2_hi[:, e * HC:(e + 1) * HC, :], stage2[:])):
                    nc.scalar.activation(dst, src, ACT.Copy, scale=W_SCALE).then_inc(hi_ready, 1)
            act.wait_ge(table_step, TABLE_STEPS)

            def x_high(j, u):
                act.wait_ge(x_filled, j + 1)
                wait(act, x_ready, 2 * j)
                for k in range(2):
                    nc.scalar.activation(xf[:, k, :], bank_x[u][:, k * TILE:(k + 1) * TILE], ACT.Identity,
                                         bias=norm2[:, 2 * k + 1:2 * k + 2], scale=norm2[:, 2 * k:2 * k + 1]).then_inc(xf_ready, 1)
                act.wait_ge(xf_ready, 2 * j + 2)
                wait(act, h_filled, HC * (j - 1))
                nc.scalar.copy(x_hi[u][:], xf[:]).then_inc(x_hi_ready, 1)

            def tile(j, u, more=True):
                e = act.value_load(tile_expert[0:1, bass.ds(j, 1)], min_val=0, max_val=N_EXP - 1)
                for c in range(HC):
                    k = j * HC + c
                    act.wait_ge(h_filled, k + 1)
                    wait(act, h_lo_ready, k - 1)
                    nc.scalar.activation(hf[c % 2][:], bank_h[c % 4][:, 0:TILE], ACT.Gelu, bias=b1[:, bass.ds(e * HC + c, 1)],
                                         scale=1.0 / W_SCALE).then_inc(gelu_ready, 1)
                    if c == 2 and more:
                        x_high(j + 1, 1 - u)

            x_high(0, 0)
            tile(0, 0)
            with act.Fori(0, NT // 2 - 1) as i:
                for v in range(2):
                    tile(2 * i + 1 + v, 1 - v)
            tile(NT - 1, 1, more=False)

        @block.vector
        def _(dve):
            n = 0
            ops = [
                lambda: nc.vector.tensor_tensor(filled[:], route.running[:], consts[:, 1, :], ALU.subtract),
                lambda: nc.vector.tensor_copy(end_i[:], route.running[:]),
                lambda: nc.vector.tensor_scalar(filled[:], filled[:], float(TILE - 1), None, ALU.add),
                lambda: nc.vector.tensor_copy(filled_i[:], filled[:]),
                lambda: nc.vector.tensor_scalar(tiles_i[:], filled_i[:], TILE.bit_length() - 1, None, ALU.logical_shift_right),
                lambda: nc.vector.tensor_copy(tiles[:], tiles_i[:]),
                lambda: nc.vector.tensor_scalar(upto[0][:], tiles[:], 1.0, None, ALU.max),
                lambda: nc.vector.tensor_copy(tiles[:], upto[0][:]),
            ]
            for k in range(3):
                ops.append(lambda k=k: nc.vector.tensor_copy(upto[k + 1][:], upto[k][:]))
                ops.append(lambda k=k: nc.vector.tensor_tensor(upto[k + 1][:, 1 << k:N_EXP], upto[k][:, 1 << k:N_EXP],
                                                               upto[k][:, 0:N_EXP - (1 << k)], ALU.add))
            whole = [1, NT, N_EXP]
            j_of = tile_no[:].unsqueeze(2).to_broadcast(whole)

            def per_queue(t):
                return t[0:1].unsqueeze(1).to_broadcast(whole)
            ops += [
                lambda: nc.vector.tensor_tensor(first[:], upto[3][:], tiles[:], ALU.subtract),
                lambda: nc.vector.tensor_tensor(t_a[:], j_of, per_queue(upto[3][:]), ALU.is_ge),
                lambda: nc.vector.tensor_reduce(t_e[:], t_a[:], AX, ALU.add),
                lambda: nc.vector.tensor_scalar(t_e[:], t_e[:], float(N_EXP - 1), None, ALU.min),
                lambda: nc.vector.tensor_tensor(t_a[:], j_of, per_queue(first[:]), ALU.subtract),
                lambda: nc.vector.tensor_scalar(last_row[:], tiles[:], -1.0, None, ALU.add),
            ]
            def rows_of(number, dst):
                return [
                    lambda: nc.vector.tensor_scalar(t_c[:], number[:], float(TILE), None, ALU.mult),
                    lambda: nc.vector.tensor_tensor(t_c[:], t_c[:], per_queue(consts[:, 1, :]), ALU.add),
                    lambda: nc.vector.tensor_tensor(t_c[:], t_c[:], t_q[:], ALU.mult),
                    lambda: nc.vector.tensor_reduce(t_r[:], t_c[:], AX, ALU.add),
                    lambda: nc.vector.tensor_copy(dst[:], t_r[:]),
                ]
            ops += [lambda: nc.vector.tensor_tensor(t_q[:], per_queue(consts[:, 0, :]), t_e[:].unsqueeze(2).to_broadcast(whole), ALU.is_equal)]
            ops += [lambda: nc.vector.tensor_tensor(t_b[:], t_a[:], per_queue(last_row[:]), ALU.min)]
            ops += rows_of(t_b, tile_row)
            ops += [lambda: nc.vector.tensor_copy(tile_expert[:], t_e[:])]
            ops += [
                lambda: nc.vector.scalar_tensor_tensor(shift[:], first[:], float(TILE), consts[:, 1, :], ALU.mult, ALU.subtract),
                lambda: nc.vector.tensor_copy(moved[0][:], route.slots[:]),
            ]
            for e in range(N_EXP):
                ops += [
                    lambda e=e: nc.vector.tensor_scalar(moved[2][:], route.experts[:], float(e), shift[:, e:e + 1], ALU.is_equal, ALU.mult),
                    lambda e=e: nc.vector.tensor_tensor(moved[(e + 1) % 2][:], moved[e % 2][:], moved[2][:], ALU.add),
                ]
            ops += [lambda: nc.vector.tensor_copy(route.slots[:], moved[0][:])]
            dve.wait_ge(loaded, LOADS)
            made = sem("c_table_part_made")
            for k, op in enumerate(ops):
                op().then_inc(made, 1)
                dve.wait_ge(made, k + 1)
            nc.vector.memset(bias2[:], 0.0).then_inc(table_step, TABLE_STEPS)
            dve.wait_ge(table_step, TABLE_STEPS)

            dve.wait_ge(hi_ready, 2)
            nc.vector.tensor_copy(bias2[0:1, :, :], b2_hi[0:1, :, :]).then_inc(split_ready, 1)
            nc.vector.scalar_tensor_tensor(bias2[32:33, :, :], stage_b2[32:33, :, :], W_SCALE, b2_hi[32:33, :, :], ALU.mult,
                                           ALU.subtract).then_inc(split_ready, 1)
            for e in range(N_EXP):
                dve.wait_ge(hi_ready, 2 + 3 * e + 3)
                c, cc = slice(e * HID, (e + 1) * HID), slice(e * HC, (e + 1) * HC)
                for dst, src, hi in ((w1.a_lo[:, c], stage1[:, 0, :], w1.a_hi[:, c]), (w1.b_lo[:, c], stage1[:, 1, :], w1.b_hi[:, c]),
                                     (w2_lo[:, cc, :], stage2[:], w2_hi[:, cc, :])):
                    nc.vector.scalar_tensor_tensor(dst, src, W_SCALE, hi, ALU.mult, ALU.subtract).then_inc(split_ready, 1)

            def x_low(j, u):
                dve.wait_ge(x_hi_ready, j + 1)
                nc.vector.tensor_tensor(x_alo[u][:], xf[:, 0, :], x_hi[u][:, 0, :], ALU.subtract).then_inc(x_ready, 1)
                nc.vector.scalar_tensor_tensor(x_b[u][:], x_hi[u][:, 1, :], sel[:, 0:1], xf[:, 1, :], ALU.mult, ALU.add
                                               ).then_inc(x_ready, 1)

            def y_part(j, u):
                dve.wait_ge(chunk_used, HC * j + HC)
                wait(dve, y_stored[u], 8 * (j - u))
                nc.vector.tensor_scalar(y_out[u][:].rearrange("p a d -> p (a d)"), bank_y[u][:, 0:A2 * D], 1.0 / W_SCALE, None,
                                        ALU.mult).then_inc(y_ready, 1)

            def tile(j, u, more=True, before=True):
                for c in range(HC):
                    k = j * HC + c
                    dve.wait_ge(gelu_ready, k + 1)
                    wait(dve, chunk_used, k - 1)
                    nc.vector.tensor_copy(h_hi[c % 2][:], hf[c % 2][:]).then_inc(h_hi_ready, 1)
                    dve.wait_ge(h_hi_ready, k + 1)
                    nc.vector.tensor_tensor(h_lo[c % 2][:], hf[c % 2][:], h_hi[c % 2][:], ALU.subtract).then_inc(h_lo_ready, 1)
                    if c == 1 and before:
                        y_part(j - 1, 1 - u)
                    if c == 3 and more:
                        x_low(j + 1, 1 - u)

            x_low(0, 0)
            tile(0, 0, before=False)
            with dve.Fori(0, NT // 2 - 1) as i:
                for v in range(2):
                    tile(2 * i + 1 + v, 1 - v)
            tile(NT - 1, 1, more=False)
            y_part(NT - 1, 1)

        @block.tensor
        def _(pe):
            def mm(dst, lhsT, rhs, start, stop, **k):
                return nc.tensor.matmul(dst, lhsT, rhs, start=start, stop=stop, **k)

            pe.wait_ge(split_ready, 2 + 3 * N_EXP)
            pe.wait_ge(table_step, TABLE_STEPS)

            def transpose_x(j, u):
                pe.wait_ge(x_loaded[u], 8 * (j - u) + 16)
                wait(pe, xf_ready, 2 * (j - 1))
                for a in range(A2):
                    c = slice(a * P, (a + 1) * P)
                    d = slice(TILE + a * P, TILE + (a + 1) * P)
                    nc.tensor.transpose(bank_x[u][:, c], x_rows[u][:, a, 0:P], ident[:])
                    last = nc.tensor.transpose(bank_x[u][:, d], x_rows[u][:, a, P:2 * P], ident[:])
                last.then_inc(x_filled, 1)

            def up(j, u, e, c):
                k = j * HC + c
                wait(pe, gelu_ready, k - 3)
                if c == 0:
                    pe.wait_ge(x_ready, 2 * j + 2)
                dst = bank_h[c % 4][:, 0:TILE]
                for i, (x_part, w_part) in enumerate(w1.passes(x_hi[u][:, 0, :], x_alo[u][:], x_b[u][:], bass.ds(e * HID + c * P, P))):
                    last = mm(dst, w_part, x_part, i == 0, i == 4)
                last.then_inc(h_filled, 1)

            def down(j, u, e, c):
                k = j * HC + c
                if c == 0:
                    wait(pe, y_ready, j - 1)
                pe.wait_ge(h_lo_ready, k + 1)
                row = bass.ds(e * HC + c, 1)
                wh, wl = (w[:, row, :].rearrange("p o d -> p (o d)") for w in (w2_hi, w2_lo))
                for a in range(A2):
                    dst = bank_y[u][:, a * D:(a + 1) * D]
                    tok = slice(a * P, (a + 1) * P)
                    if c == 0:
                        mm(dst, ones_rows[:], bias2[:, bass.ds(e, 1), :].rearrange("p o d -> p (o d)"), a == 0, False,
                           skip_group_check=True)
                    mm(dst, h_hi[c % 2][:, tok], wh, False, False, skip_group_check=True)
                    mm(dst, h_hi[c % 2][:, tok], wl, False, False, skip_group_check=True)
                    last = mm(dst, h_lo[c % 2][:, tok], wh, False, c == HC - 1, skip_group_check=True)
                last.then_inc(chunk_used, 1)

            def expert_of(j):
                return pe.value_load(tile_expert[0:1, bass.ds(j, 1)], min_val=0, max_val=N_EXP - 1)

            def tile(j, u, more=True):
                e = expert_of(j)
                for c in range(HC):
                    up(j, u, e, c)
                    if c >= 2:
                        down(j, u, e, c - 2)
                    if c == 0 and more:
                        transpose_x(j + 1, 1 - u)
                down(j, u, e, HC - 2)
                down(j, u, e, HC - 1)

            transpose_x(0, 0)
            tile(0, 0)
            with pe.Fori(0, NT // 2 - 1) as i:
                for v in range(2):
                    tile(2 * i + 1 + v, 1 - v)
            tile(NT - 1, 1, more=False)


def combine(nc, A, h_all, route, out, sb, sem, n_seq):
    DEPTH = 4
    y_rows = [[sb(f"y_rows{k}_{u}", [P, D], F32) for k in range(2)] for u in range(DEPTH)]
    slot_now = [sb(f"d_slot_now{u}", [P, 2], I32) for u in range(DEPTH)]
    slot_at_hand = sem("d_slot_at_hand")
    fetched = [sem(f"d_fetched{u}") for u in range(DEPTH)]
    added = sem("d_added")
    stored = sem("d_stored")

    def seq(s):
        return bass.ts(s, D)

    block = nc.Block()
    with block:
        @block.gpsimd
        def _(pool):
            def fetch(s, u):
                nc.gpsimd.tensor_copy(slot_now[u][:], route.slots[:, bass.ds(2 * s, 2)]).then_inc(slot_at_hand, 1)
                waits_apart(pool, (slot_at_hand, 1), (slot_at_hand, s + 1))
                for k in range(2):
                    nc.gpsimd.indirect_dma_start(
                        out=y_rows[u][k][:, :], out_offset=None, in_=route.y_tiles,
                        in_offset=bass.IndirectOffsetOnAxis(ap=slot_now[u][:, k:k + 1].bitcast(U32), axis=0),
                    ).then_inc(fetched[u], 16)

            for u in range(DEPTH):
                fetch(u, u)
            with pool.Fori(1, n_seq // DEPTH) as i:
                for u in range(DEPTH):
                    s = DEPTH * i + u
                    waits_apart(pool, (slot_at_hand, 1), (added, 2 * s - 2 * DEPTH + 2))
                    fetch(s, u)

        @block.vector
        def _(dve):
            with dve.Fori(0, n_seq // DEPTH) as i:
                for u in range(DEPTH):
                    s = DEPTH * i + u
                    dve.wait_ge(fetched[u], 32 * i + 32)
                    for k in range(2):
                        dve.wait_ge(added, 2 * s + k)
                        nc.vector.scalar_tensor_tensor(h_all[:, seq(s)], y_rows[u][k][:], route.gates[:, bass.ds(2 * s + k, 1)],
                                                       h_all[:, seq(s)], ALU.mult, ALU.add).then_inc(added, 1)

        @block.sync
        def _(sp):
            with sp.Fori(0, n_seq) as s:
                sp.wait_ge(added, 2 * s + 2)
                sp.dma_start(out[bass.ds(s, 1), :, :].rearrange("b s d -> s (b d)"), h_all[:, seq(s)]).then_inc(stored, 16)
            sp.wait_ge(stored, 16 * n_seq)


def kernel(**inputs):
    import numpy as np
    import concourse.bacc as bacc
    from concourse.bass_utils import run_bass_kernel_spmd

    a = {k: np.asarray(v) for k, v in inputs.items()}
    n_seq, n_tok = a["x"].shape
    for k in ("x", "itok_BS_0_1003", "itok_BS_0_5", "mask_BS_i1_0"):
        a[k] = a[k].T
    a["L0_attn_qkv_wT"] = a.pop("L0_attn_qkv_w").T
    a["L0_attn_proj_wT"] = a.pop("L0_attn_proj_w").T

    w, b = a["L0_ffn_qkv_w"], a["L0_ffn_qkv_b"]
    twice = np.concatenate([np.arange(16 * h, 16 * h + 16) for h in range(2 * HEADS) for _ in range(2)])
    a["qk_dup_wT"], a["qk_dup_b"] = w[:, twice], b[twice]

    p = np.arange(P)
    a["sel"] = np.stack([-(p >= DB).astype(np.float32), -(p % 32 >= 16).astype(np.float32)], axis=1)
    a["expert_no"] = np.arange(N_EXP, dtype=np.float32)
    a["queue_start"] = (np.arange(N_EXP) * (n_seq * n_tok + TILE)).astype(np.float32)
    a["tile_no"] = np.arange(2 * n_seq * n_tok // TILE + N_EXP, dtype=np.float32)

    nc = bacc.Bacc("TRN2", target_bir_lowering=False, num_devices=1)
    arrays, aps = {}, {}
    for name, v in a.items():
        v = np.ascontiguousarray(v if v.ndim > 1 else v[None])
        arrays[f"in_{name}"] = v
        aps[name] = nc.dram_tensor(f"in_{name}", v.shape, mybir.dt.from_np(v.dtype), kind="ExternalInput").ap()
    out = nc.dram_tensor("out", [n_seq, n_tok, D], F32, kind="ExternalOutput").ap()
    build(nc, aps, out)
    return run_bass_kernel_spmd(nc, [arrays], core_ids=[0]).results[0]["out"]
```

```python
from contextlib import ExitStack

import numpy as np

import concourse.bass as bass
from concourse import mybir

F32 = mybir.dt.float32
F16 = mybir.dt.float16
I32 = mybir.dt.int32
U32 = mybir.dt.uint32
ALU = mybir.AluOpType
ACT = mybir.ActivationFunctionType
AX = mybir.AxisListType.X

P = 128
D = 192
DB = D - P
HEADS = 12
HALF = 384
W_SCALE = 64.0
LN_EPS = 1e-5
N_EXP = 8
HID = 768
HC = HID // P
TILE = 256
GROUP = 4
N_GROUPS = HEADS // GROUP


def wait(eng, sem, value):
    if not (isinstance(value, int) and value <= 0):
        eng.wait_ge(sem, value)


def waits_apart(eng, over, *waits):
    waits = [(sem, value if isinstance(value, int) else eng.to_reg(value)) for sem, value in waits]
    eng.wait_ge(*over)
    for sem, value in waits:
        wait(eng, sem, value)


def pipeline(eng, n_seq, turn):
    def one_turn(t, parity):
        def run(step, behind, *args):
            s = t - behind
            if not isinstance(t, int) or 0 <= s < n_seq:
                step(s, (parity - behind) % 2, *args)
        turn(run)

    distances = []
    turn(lambda step, behind, *args: distances.append(behind))
    nearest, farthest = min(distances), max(distances)
    first = farthest + 1
    pairs = (n_seq + nearest - first) // 2
    for t in range(nearest, first):
        one_turn(t, t % 2)
    with eng.Fori(0, pairs) as i:
        for v in range(2):
            one_turn(2 * i + first + v, (first + v) % 2)
    for t in range(first + 2 * pairs, n_seq + farthest):
        one_turn(t, t % 2)


class Split:

    def __init__(self, sb, name, cols):
        self.cols = cols
        self.a_hi, self.a_lo, self.b_hi, self.b_lo = (
            sb(f"{name}_{part}", [P, cols], F16) for part in ("a_hi", "a_lo", "b_hi", "b_lo"))

    def passes(self, act_a_hi, act_a_lo, act_b, cols):
        return [(act_a_hi, self.a_hi[:, cols]), (act_a_lo, self.a_hi[:, cols]),
                (act_a_hi, self.a_lo[:, cols]), (act_b, self.b_hi[:, cols]), (act_b, self.b_lo[:, cols])]


def build(nc, A, out):
    n_seq = A["x"].shape[1]
    S_ALL = n_seq * D
    with ExitStack() as whole:
        def sb(name, shape, dt, ctx=whole):
            return ctx.enter_context(nc.sbuf_tensor(name, shape, dt))

        def sem(name):
            return whole.enter_context(nc.semaphore(name))

        h_all = sb("h_all", [P, S_ALL], F32)
        ident = sb("ident", [P, P], F32)
        ones_rows = sb("ones_rows", [P, P], F16)
        neg_low = sb("neg_low", [P, 1], F32)
        half_pow = sb("half_pow", [P, 1], F32)
        psum = [whole.enter_context(nc.psum_tensor(f"bank{i}", [P, 512], F32)) for i in range(8)]

        phases(nc, A, out, h_all, ident, ones_rows, neg_low, half_pow, psum, sb, sem, n_seq)


def load_split(eng, sems, stage, src, cols):
    eng.dma_start(stage[:, 0, 0:cols], src[0:P, :]).then_inc(sems, 16)
    eng.dma_start(stage[0:DB, 1, 0:cols], src[P:D, :]).then_inc(sems, 16)
    eng.dma_start(stage[DB:P, 1, 0:cols], src[P:D, :]).then_inc(sems, 16)


def phases(nc, A, out, h_all, ident, ones_rows, neg_low, half_pow, psum, sb, sem, n_seq):
    with ExitStack() as ctx:
        first_attention(nc, A, h_all, ident, ones_rows, neg_low, half_pow, psum,
                        lambda n, s, d: sb(n, s, d, ctx), sem, n_seq)
    with ExitStack() as routed:
        route = Route(nc, lambda n, s, d: sb(n, s, d, routed), n_seq)
        with ExitStack() as ctx:
            second_attention(nc, A, h_all, ident, ones_rows, half_pow, psum, route,
                             lambda n, s, d: sb(n, s, d, ctx), sem, n_seq)
        with ExitStack() as ctx:
            experts(nc, A, h_all, ident, ones_rows, psum, route, lambda n, s, d: sb(n, s, d, ctx), sem, n_seq)
        with ExitStack() as ctx:
            combine(nc, A, h_all, route, out, lambda n, s, d: sb(n, s, d, ctx), sem, n_seq)


def first_attention(nc, A, h_all, ident, ones_rows, neg_low, half_pow, psum, sb, sem, n_seq):
    HD = 64
    CH = 6
    QK = 2 * CH * P
    SCALE = float(HD) ** -0.5 / (W_SCALE * W_SCALE)
    VW = HD + 1

    w_qk = Split(sb, "w_qk", QK)
    w_v = Split(sb, "w_v", CH * P)
    wp_hi = sb("wp_hi", [P, CH, D], F16)
    wp_lo = sb("wp_lo", [P, CH, D], F16)
    bias_qk = sb("bias_qk", [P, QK], F16)
    bias_out = sb("bias_out", [P, D], F16)
    pe_base = sb("pe_base", [P, D], F32)
    names = ("problem", "skill", "correct", "segment")
    tables = [A[f"L0_tok_{n}_table"] for n in names]
    sizes = [t.shape[0] for t in tables]
    ids_all = sb("ids_all", [P, 4, n_seq], I32)
    ids_i = [ids_all[:, n, :] for n in range(4)]
    ids_now = [sb(f"ids_now{u}", [P, 4], I32) for u in range(2)]
    coef = [sb(f"{n}_coef", [P, n_seq], F32) for n in names]
    rows = [[sb(f"{n}_rows{u}", [P, D], F32) for u in range(2)] for n in names]

    stats = [sb(f"stats{u}", [P, 6], F32) for u in range(2)]
    moments = [sb(f"moments{u}", [P, 2], F32) for u in range(2)]
    var_eps = [sb(f"var_eps{u}", [P, 1], F32) for u in range(2)]
    rstd = [sb(f"rstd{u}", [P, 1], F32) for u in range(2)]
    y = [sb(f"y{u}", [P, 2 * P], F32) for u in range(2)]
    xt_hi = [sb(f"xt_hi{u}", [P, 2 * P], F16) for u in range(2)]
    xt_alo = [sb(f"xt_alo{u}", [P, P], F16) for u in range(2)]
    xt_b = [sb(f"xt_b{u}", [P, P], F16) for u in range(2)]
    q_hi = [sb(f"q_hi{u}", [P, CH * P], F16) for u in range(2)]
    q_lo = [sb(f"q_lo{u}", [P, CH * P], F16) for u in range(2)]
    kp_hi = [sb(f"kp_hi{u}", [P, CH, 2, P], F16) for u in range(2)]
    kp_lo = [sb(f"kp_lo{u}", [P, CH, 2, P], F16) for u in range(2)]
    v_hi = [sb(f"v_hi{u}", [P, HEADS, VW], F16) for u in range(2)]
    v_lo = [sb(f"v_lo{u}", [P, HEADS, HD], F16) for u in range(2)]
    row_max = [sb(f"row_max{u}", [P, GROUP], F32) for u in range(2)]
    neg_max = [sb(f"neg_max{u}", [P, GROUP], F32) for u in range(2)]
    prob = [sb(f"prob{u}", [P, GROUP, P], F32) for u in range(2)]
    pt_hi = [sb(f"pt_hi{u}", [P, GROUP, P], F16) for u in range(2)]
    pt_lo = [sb(f"pt_lo{u}", [P, GROUP, P], F16) for u in range(2)]
    recip = sb("recip", [P, HEADS], F32)
    o_norm = sb("o_norm", [P, HEADS, HD], F32)
    ot_hi = sb("ot_hi", [P, CH, P], F16)
    ot_lo = sb("ot_lo", [P, CH, P], F16)
    stage = sb("stage", [P, 2, QK], F32)
    stage_p = sb("stage_p", [P, CH, D], F32)
    stage_bias = sb("stage_bias", [33, QK], F32)
    stage_bout = sb("stage_bout", [33, D], F32)
    bout_hi = sb("bout_hi", [33, D], F16)
    bqk_hi = sb("bqk_hi", [33, QK], F16)
    bv_col = sb("bv_col", [P, CH], F32)
    wvec = sb("wvec", [P, 6], F32)
    idf = sb("idf", [P, n_seq], F32)
    idn = sb("idn", [P, n_seq], F32)

    bank_s, bank_t, bank_o, bank_w = psum[0:2], psum[2:4], psum[4:6], psum[6:8]

    loaded = sem("a_loaded")
    const_done = sem("a_const_done")
    wide_loaded = sem("a_wide_loaded")
    v_loaded = sem("a_v_loaded")
    split_step = sem("a_split_step")
    bias_sum = sem("a_bias_sum")
    masks_ready = sem("a_masks_ready")
    ids_ready = sem("a_ids_ready")
    ids_at_hand = sem("a_ids_at_hand")
    id_step = sem("a_id_step")
    weights_ready = sem("a_weights_ready")
    rows_loaded = [sem(f"a_rows_loaded{u}") for u in range(2)]
    embedded = sem("a_embedded")
    ln_step = sem("a_ln_step")
    rstd_ready = sem("a_rstd_ready")
    y_ready = sem("a_y_ready")
    xt_filled = sem("a_xt_filled")
    xt_hi_ready = sem("a_xt_hi_ready")
    xt_ready = sem("a_xt_ready")
    qkv_filled = sem("a_qkv_filled")
    qkv_hi = sem("a_qkv_hi")
    qkv_lo = sem("a_qkv_lo")
    scores_filled = sem("a_scores_filled")
    max_ready = sem("a_max_ready")
    neg_ready = sem("a_neg_ready")
    prob_ready = sem("a_prob_ready")
    pt_filled = sem("a_pt_filled")
    pt_hi_ready = sem("a_pt_hi_ready")
    pt_lo_ready = sem("a_pt_lo_ready")
    heads_done = sem("a_heads_done")
    recip_ready = sem("a_recip_ready")
    o_ready = sem("a_o_ready")
    ot_filled = sem("a_ot_filled")
    ot_hi_ready = sem("a_ot_hi_ready")
    ot_lo_ready = sem("a_ot_lo_ready")
    out_filled = sem("a_out_filled")
    h_ready = sem("a_h_ready")
    HI_AT = [1, 2, 4, 6, 7, 8]

    def seq(s):
        return bass.ts(s, D)

    wq_src, wv_src = A["L0_attn_qkv_wT"][:, 0:QK], A["L0_attn_qkv_wT"][:, QK:QK + CH * P]
    block = nc.Block()
    with block:
        @block.sync
        def _(sp):
            for n, ids in zip(("x", "itok_BS_0_1003", "itok_BS_0_5", "mask_BS_i1_0"), ids_i):
                sp.dma_start(ids, A[n]).then_inc(loaded, 16)
            sp.dma_start(wvec[:, 0:5], A["L0_tok_combine_w"].partition_broadcast(P)).then_inc(loaded, 16)
            sp.dma_start(wvec[:, 5:6], A["L0_tok_combine_b"].partition_broadcast(P)).then_inc(loaded, 16)
            sp.dma_start(pe_base[:], A["L0_tok_pe"]).then_inc(loaded, 16)
            load_split(sp, wide_loaded, stage, wq_src, QK)
            for r in (0, 32):
                sp.dma_start(stage_bias[r:r + 1, :], A["L0_attn_qkv_b"][:, 0:QK]).then_inc(wide_loaded, 16)
                sp.dma_start(stage_bout[r:r + 1, :], A["L0_attn_proj_b"]).then_inc(wide_loaded, 16)
            sp.dma_start(bv_col[:], A["L0_attn_qkv_b"][0, QK:QK + CH * P].rearrange("(c p) -> p c", p=P),
                         allow_slow_non_contiguous=True).then_inc(wide_loaded, 16)
            sp.dma_start(stage_p[:], A["L0_attn_proj_wT"].rearrange("(c p) d -> p c d", p=P)).then_inc(wide_loaded, 16)
            sp.wait_ge(split_step, 4)
            load_split(sp, v_loaded, stage, wv_src, CH * P)

        @block.gpsimd
        def _(pool):
            nc.gpsimd.memset(ident[:], 1.0).then_inc(masks_ready, 1)
            nc.gpsimd.memset(half_pow[:], -0.5).then_inc(masks_ready, 1)
            pool.wait_ge(masks_ready, 1)
            nc.gpsimd.affine_select(out=ident[:], in_=ident[:], compare_op=ALU.is_equal, fill=0.0, base=0,
                                    pattern=[[-1, P]], channel_multiplier=1).then_inc(masks_ready, 1)
            pool.wait_ge(masks_ready, 3)
            pool.wait_ge(ids_ready, 4)

            def gather(s, u):
                waits_apart(pool, (masks_ready, 3), (embedded, 4 * s - 4))
                nc.gpsimd.tensor_copy(ids_now[u][:], ids_all[:, :, bass.ds(s, 1)].rearrange("p n o -> p (n o)")).then_inc(ids_at_hand, 1)
                waits_apart(pool, (masks_ready, 3), (ids_at_hand, s + 1))
                for n in range(4):
                    nc.gpsimd.indirect_dma_start(
                        out=rows[n][u][:, :], out_offset=None, in_=tables[n],
                        in_offset=bass.IndirectOffsetOnAxis(ap=ids_now[u][:, n:n + 1].bitcast(U32), axis=0),
                    ).then_inc(rows_loaded[u], 16)

            def rsqrt(s, u):
                pool.wait_ge(ln_step, 3 * s + 3)
                nc.gpsimd.tensor_tensor(rstd[u][:], var_eps[u][:], half_pow[:], ALU.pow).then_inc(rstd_ready, 1)

            def turn(run):
                run(gather, -4)
                run(rsqrt, -3)

            pipeline(pool, n_seq, turn)

        @block.scalar
        def _(act):
            def to_hi(dst, src):
                return nc.scalar.activation(dst, src, ACT.Copy, scale=W_SCALE)

            act.wait_ge(wide_loaded, 16 * 9)
            to_hi(w_qk.a_hi[:], stage[:, 0, :]).then_inc(weights_ready, 1)
            to_hi(w_qk.b_hi[:], stage[:, 1, :]).then_inc(weights_ready, 1)
            to_hi(wp_hi[:], stage_p[:]).then_inc(weights_ready, 1)
            to_hi(bqk_hi[0:1, :], stage_bias[0:1, :]).then_inc(weights_ready, 1)
            to_hi(bqk_hi[32:33, :], stage_bias[32:33, :]).then_inc(weights_ready, 1)
            act.wait_ge(v_loaded, 48)
            to_hi(w_v.a_hi[:], stage[:, 0, 0:CH * P]).then_inc(weights_ready, 1)
            to_hi(w_v.b_hi[:], stage[:, 1, 0:CH * P]).then_inc(weights_ready, 1)

            def xt_high(s, u):
                act.wait_ge(xt_filled, s + 1)
                wait(act, qkv_filled, 6 * s - 6)
                nc.scalar.copy(xt_hi[u][:], bank_w[0][:, 0:2 * P]).then_inc(xt_hi_ready, 1)

            def qkv_high(s, u, j):
                w = bank_w[j % 2]
                act.wait_ge(qkv_filled, 6 * s + j + 1)
                if j < 2:
                    wait(act, scores_filled, 3 * s - 3)
                    nc.scalar.copy(q_hi[u][:, j * HALF:(j + 1) * HALF], w[:, 0:HALF]).then_inc(qkv_hi, 1)
                elif j < 4:
                    for g in range(2):
                        r = slice(64 * g, 64 * g + 64)
                        nc.scalar.copy(kp_hi[u][r, 3 * (j - 2):3 * (j - 1), g, :],
                                       w[r, 0:HALF].rearrange("p (c k) -> p c k", k=P)).then_inc(qkv_hi, 1)
                else:
                    wait(act, heads_done, 3 * s - 3)
                    nc.scalar.copy(v_hi[u][:, 6 * (j - 4):6 * (j - 3), 0:HD],
                                   w[:, 0:HALF].rearrange("p (h d) -> p h d", d=HD)).then_inc(qkv_hi, 1)

            def exps(t, u, g):
                b = (u + g) % 2
                act.wait_ge(neg_ready, 3 * t + g + 1)
                wait(act, pt_filled, 3 * t + g - 1)
                for e in range(GROUP):
                    nc.scalar.activation(prob[b][:, e, :], bank_s[b][:, e * P:(e + 1) * P], ACT.Exp,
                                         bias=neg_max[b][:, e:e + 1], scale=SCALE).then_inc(prob_ready, 1)

            def pt_high(t, u, g):
                b = (u + g) % 2
                act.wait_ge(pt_filled, 3 * t + g + 1)
                wait(act, heads_done, 3 * t + g - 1)
                nc.scalar.copy(pt_hi[b][:].rearrange("p e k -> p (e k)"), bank_t[b][:]).then_inc(pt_hi_ready, 1)

            def ot_high(t, u, half):
                act.wait_ge(ot_filled, 2 * t + half + 1)
                wait(act, out_filled, t)
                nc.scalar.copy(ot_hi[:, 3 * half:3 * half + 3, :].rearrange("p c k -> p (c k)"),
                               bank_o[half][:, 0:HALF]).then_inc(ot_hi_ready, 1)

            act.wait_ge(const_done, 1)
            def turn(run):
                run(xt_high, -2)
                run(qkv_high, -1, 5)
                run(exps, -1, 0)
                run(qkv_high, -2, 0)
                run(qkv_high, -2, 1)
                run(ot_high, 0, 0)
                run(qkv_high, -2, 2)
                run(ot_high, 0, 1)
                run(pt_high, -1, 0)
                run(qkv_high, -2, 3)
                run(exps, -1, 1)
                run(qkv_high, -2, 4)
                run(exps, -1, 2)
                run(pt_high, -1, 1)
                run(pt_high, -1, 2)

            pipeline(act, n_seq, turn)

        @block.vector
        def _(dve):
            nc.vector.memset(ones_rows[:], 0.0).then_inc(id_step, 1)
            nc.vector.memset(bias_qk[:], 0.0).then_inc(id_step, 1)
            nc.vector.memset(bias_out[:], 0.0).then_inc(id_step, 1)
            nc.vector.memset(neg_low[0:64, :], 0.0).then_inc(id_step, 1)
            nc.vector.memset(neg_low[64:P, :], -1.0).then_inc(id_step, 1)
            for u in range(2):
                for kp in (kp_hi[u], kp_lo[u]):
                    nc.vector.memset(kp[:], 0.0).then_inc(id_step, 1)
                nc.vector.memset(v_hi[u][:, :, HD:VW], 1.0).then_inc(id_step, 1)
            dve.wait_ge(id_step, 11)
            nc.vector.memset(ones_rows[0:1, :], 1.0).then_inc(id_step, 1)
            nc.vector.memset(ones_rows[32:33, :], 1.0).then_inc(id_step, 1)
            dve.wait_ge(loaded, 16 * 7)
            nc.vector.tensor_scalar(pe_base[:], pe_base[:], wvec[:, 0:1], wvec[:, 5:6], ALU.mult, ALU.add).then_inc(id_step, 1)
            done = 14
            for n, w_at in zip(range(4), (2, 3, 4, 1)):
                v_n = float(sizes[n])
                steps = [
                    lambda: nc.vector.tensor_copy(idf[:], ids_i[n]),
                    lambda: nc.vector.tensor_scalar(idn[:], idf[:], 0.0, v_n, ALU.is_lt, ALU.mult),
                    lambda: nc.vector.tensor_tensor(idf[:], idf[:], idn[:], ALU.add),
                    lambda: nc.vector.tensor_scalar(idf[:], idf[:], 0.0, v_n - 1.0, ALU.max, ALU.min),
                    lambda: nc.vector.tensor_scalar(coef[n][:], idf[:], 0.0, wvec[:, w_at:w_at + 1], ALU.not_equal, ALU.mult),
                ]
                for step in steps:
                    dve.wait_ge(id_step, done)
                    step().then_inc(id_step, 1)
                    done += 1
                nc.vector.tensor_copy(ids_i[n], idf[:]).then_inc(ids_ready, 1)
                dve.wait_ge(ids_ready, n + 1)
                dve.wait_ge(id_step, done)

            def embed(s, u, n):
                dve.wait_ge(rows_loaded[u], 32 * (s - u) + 64)
                wait(dve, embedded, 4 * s + n)
                base = pe_base[:] if n == 0 else h_all[:, seq(s)]
                nc.vector.scalar_tensor_tensor(h_all[:, seq(s)], rows[n][u][:], coef[n][:, bass.ds(s, 1)], base,
                                               ALU.mult, ALU.add).then_inc(embedded, 1)

            def ln_stats(s, u):
                waits_apart(dve, (const_done, 1), (embedded, 4 * s + 4))
                nc.vector.bn_stats(stats[u][:], h_all[:, seq(s)]).then_inc(ln_step, 1)

            def ln_aggr(s, u):
                waits_apart(dve, (const_done, 1), (ln_step, 3 * s + 1), (y_ready, 2 * s - 2))
                nc.vector.bn_aggr(moments[u][:], stats[u][:]).then_inc(ln_step, 1)

            def ln_eps(s, u):
                dve.wait_ge(ln_step, 3 * s + 2)
                nc.vector.tensor_scalar(var_eps[u][:], moments[u][:, 1:2], LN_EPS, None, ALU.add).then_inc(ln_step, 1)

            def ln_apply(s, u):
                dve.wait_ge(rstd_ready, s + 1)
                wait(dve, xt_filled, s - 1)
                for dst, src in ((y[u][:, 0:D], h_all[:, seq(s)]), (y[u][:, D:2 * P], h_all[:, bass.ds(s * D + P, DB)])):
                    nc.vector.tensor_scalar(dst, src, moments[u][:, 0:1], rstd[u][:, 0:1],
                                            ALU.subtract, ALU.mult).then_inc(y_ready, 1)

            def xt_low(s, u):
                dve.wait_ge(xt_hi_ready, s + 1)
                nc.vector.tensor_tensor(xt_alo[u][:], bank_w[0][:, 0:P], xt_hi[u][:, 0:P], ALU.subtract).then_inc(xt_ready, 1)
                nc.vector.scalar_tensor_tensor(xt_b[u][:], xt_hi[u][:, P:2 * P], neg_low[:, 0:1], bank_w[0][:, P:2 * P],
                                               ALU.mult, ALU.add).then_inc(xt_ready, 1)

            def qkv_low(s, u, j):
                w = bank_w[j % 2]
                dve.wait_ge(qkv_hi, 8 * s + HI_AT[j])
                if j < 2:
                    c = slice(j * HALF, (j + 1) * HALF)
                    nc.vector.tensor_tensor(q_lo[u][:, c], w[:, 0:HALF], q_hi[u][:, c], ALU.subtract).then_inc(qkv_lo, 1)
                elif j < 4:
                    for g in range(2):
                        r = slice(64 * g, 64 * g + 64)
                        c = slice(3 * (j - 2), 3 * (j - 1))
                        nc.vector.tensor_tensor(kp_lo[u][r, c, g, :], w[r, 0:HALF].rearrange("p (c k) -> p c k", k=P),
                                                kp_hi[u][r, c, g, :], ALU.subtract).then_inc(qkv_lo, 1)
                else:
                    c = slice(6 * (j - 4), 6 * (j - 3))
                    nc.vector.tensor_tensor(v_lo[u][:, c, :], w[:, 0:HALF].rearrange("p (h d) -> p h d", d=HD),
                                            v_hi[u][:, c, 0:HD], ALU.subtract).then_inc(qkv_lo, 1)

            def maxima(t, u, g):
                b = (u + g) % 2
                dve.wait_ge(scores_filled, 3 * t + g + 1)
                wait(dve, neg_ready, 3 * t + g - 1)
                nc.vector.tensor_reduce(row_max[b][:], bank_s[b][:].rearrange("p (e k) -> p e k", k=P), AX, ALU.max
                                        ).then_inc(max_ready, 1)

            def neg_maxima(t, u, g):
                b = (u + g) % 2
                dve.wait_ge(max_ready, 3 * t + g + 1)
                wait(dve, prob_ready, 4 * (3 * t + g - 1))
                nc.vector.tensor_scalar(neg_max[b][:], row_max[b][:], -SCALE, None, ALU.mult).then_inc(neg_ready, 1)

            def pt_low(t, u, g):
                b = (u + g) % 2
                dve.wait_ge(pt_hi_ready, 3 * t + g + 1)
                nc.vector.tensor_tensor(pt_lo[b][:].rearrange("p e k -> p (e k)"), bank_t[b][:],
                                        pt_hi[b][:].rearrange("p e k -> p (e k)"), ALU.subtract).then_inc(pt_lo_ready, 1)

            def o_view(half):
                return bank_o[half][:, 0:6 * VW].rearrange("p (h d) -> p h d", d=VW)

            def row_sums(t, u, half):
                dve.wait_ge(heads_done, 3 * t + 2 + half)
                wait(dve, o_ready, 2 * t)
                nc.vector.reciprocal(recip[:, 6 * half:6 * half + 6], o_view(half)[:, :, HD]).then_inc(recip_ready, 1)

            def normalise(t, u, half):
                dve.wait_ge(recip_ready, 2 * t + half + 1)
                wait(dve, ot_filled, 2 * t)
                nc.vector.tensor_tensor(o_norm[:, 6 * half:6 * half + 6, :], o_view(half)[:, :, 0:HD],
                                        recip[:, 6 * half:6 * half + 6].unsqueeze(2).to_broadcast([P, 6, HD]),
                                        ALU.mult).then_inc(o_ready, 1)

            def ot_low(t, u, half):
                dve.wait_ge(ot_hi_ready, 2 * t + half + 1)
                nc.vector.tensor_tensor(ot_lo[:, 3 * half:3 * half + 3, :].rearrange("p c k -> p (c k)"), bank_o[half][:, 0:HALF],
                                        ot_hi[:, 3 * half:3 * half + 3, :].rearrange("p c k -> p (c k)"),
                                        ALU.subtract).then_inc(ot_lo_ready, 1)

            def add_output(t, u):
                dve.wait_ge(out_filled, t + 1)
                nc.vector.scalar_tensor_tensor(h_all[:, seq(t)], bank_o[0][:, 0:D], 1.0 / (W_SCALE * W_SCALE), h_all[:, seq(t)],
                                               ALU.mult, ALU.add).then_inc(h_ready, 1)

            def to_lo(dst, src, hi):
                return nc.vector.scalar_tensor_tensor(dst, src, W_SCALE, hi, ALU.mult, ALU.subtract)

            dve.wait_ge(weights_ready, 1)
            to_lo(w_qk.a_lo[:], stage[:, 0, :], w_qk.a_hi[:]).then_inc(split_step, 1)
            dve.wait_ge(weights_ready, 2)
            to_lo(w_qk.b_lo[:], stage[:, 1, :], w_qk.b_hi[:]).then_inc(split_step, 1)
            dve.wait_ge(weights_ready, 5)
            to_lo(wp_lo[:], stage_p[:], wp_hi[:]).then_inc(split_step, 1)
            nc.vector.tensor_copy(bias_qk[0:1, :], bqk_hi[0:1, :]).then_inc(split_step, 1)
            to_lo(bias_qk[32:33, :], stage_bias[32:33, :], bqk_hi[32:33, :]).then_inc(split_step, 1)
            dve.wait_ge(bias_sum, 1)
            for r in (0, 32):
                nc.vector.tensor_tensor(stage_bout[r:r + 1, :], bank_t[0][r:r + 1, 0:D], stage_bout[r:r + 1, :], ALU.add
                                        ).then_inc(split_step, 1)
            dve.wait_ge(split_step, 7)
            for r in (0, 32):
                nc.vector.tensor_scalar(bout_hi[r:r + 1, :], stage_bout[r:r + 1, :], W_SCALE * W_SCALE, None, ALU.mult
                                        ).then_inc(split_step, 1)
            dve.wait_ge(split_step, 9)
            nc.vector.tensor_copy(bias_out[0:1, :], bout_hi[0:1, :]).then_inc(split_step, 1)
            nc.vector.scalar_tensor_tensor(bias_out[32:33, :], stage_bout[32:33, :], W_SCALE * W_SCALE, bout_hi[32:33, :],
                                           ALU.mult, ALU.subtract).then_inc(split_step, 1)
            dve.wait_ge(weights_ready, 7)
            to_lo(w_v.a_lo[:], stage[:, 0, 0:CH * P], w_v.a_hi[:]).then_inc(split_step, 1)
            to_lo(w_v.b_lo[:], stage[:, 1, 0:CH * P], w_v.b_hi[:]).then_inc(split_step, 1)
            dve.wait_ge(split_step, 13)
            nc.vector.memset(stats[0][:], 0.0).then_inc(const_done, 1)
            dve.wait_ge(const_done, 1)

            def turn(run):
                run(pt_low, 1, 2)
                run(xt_low, -1)
                run(row_sums, 1, 0)
                run(embed, -2, 2)
                run(qkv_low, 0, 5)
                run(embed, -2, 3)
                run(normalise, 1, 0)
                run(row_sums, 1, 1)
                run(ln_stats, -2)
                run(qkv_low, -1, 0)
                run(normalise, 1, 1)
                run(ln_aggr, -2)
                run(maxima, 0, 1)
                run(ln_eps, -2)
                run(qkv_low, -1, 1)
                run(neg_maxima, 0, 1)
                run(ln_apply, -2)
                run(ot_low, 1, 0)
                run(qkv_low, -1, 2)
                run(ot_low, 1, 1)
                run(maxima, 0, 2)
                run(embed, -3, 0)
                run(neg_maxima, 0, 2)
                run(qkv_low, -1, 3)
                run(pt_low, 0, 0)
                run(add_output, 1)
                run(qkv_low, -1, 4)
                run(embed, -3, 1)
                run(maxima, -1, 0)
                run(pt_low, 0, 1)
                run(neg_maxima, -1, 0)

            pipeline(dve, n_seq, turn)

        @block.tensor
        def _(pe):
            def mm(dst, lhsT, rhs, start, stop):
                return nc.tensor.matmul(dst, lhsT, rhs, start=start, stop=stop)

            pe.wait_ge(wide_loaded, 16 * 9)
            for r in (0, 32):
                for c in range(CH):
                    last = mm(bank_t[0][r:r + 1, 0:D], bv_col[:, c:c + 1], stage_p[:, c, :], c == 0, c == CH - 1)
            last.then_inc(bias_sum, 1)
            pe.wait_ge(masks_ready, 3)
            pe.wait_ge(const_done, 1)

            def transpose_y(s, u):
                pe.wait_ge(y_ready, 2 * s + 2)
                wait(pe, qkv_lo, 8 * s + HI_AT[4] - 8)
                nc.tensor.transpose(bank_w[0][:, 0:P], y[u][:, 0:P], ident[:])
                nc.tensor.transpose(bank_w[0][:, P:2 * P], y[u][:, P:2 * P], ident[:]).then_inc(xt_filled, 1)

            def project(s, u, j):
                w = bank_w[j % 2]
                if j == 0:
                    pe.wait_ge(xt_ready, 2 * s + 2)
                elif j == 1:
                    wait(pe, qkv_lo, 8 * s)
                else:
                    pe.wait_ge(qkv_lo, 8 * s + HI_AT[j - 2])
                parts = (xt_hi[u][:, 0:P], xt_alo[u][:], xt_b[u][:])
                if j < 4:
                    for c in range(3):
                        col = slice((3 * j + c) * P, (3 * j + c + 1) * P)
                        dst = w[:, c * P:(c + 1) * P]
                        for k, (x_part, w_part) in enumerate(w_qk.passes(*parts, col)):
                            mm(dst, w_part, x_part, k == 0, False)
                        last = mm(dst, bias_qk[:, col], ones_rows[:], False, True)
                else:
                    col = slice((j - 4) * HALF, (j - 3) * HALF)
                    for k, (x_part, w_part) in enumerate(w_v.passes(*parts, col)):
                        last = mm(w[:, 0:HALF], x_part, w_part, k == 0, k == 4)
                last.then_inc(qkv_filled, 1)

            def scores(t, u, g):
                b = (u + g) % 2
                if g == 0:
                    pe.wait_ge(qkv_lo, 8 * t + HI_AT[3])
                wait(pe, prob_ready, 4 * (3 * t + g - 1))
                for c in range(2 * g, 2 * g + 2):
                    dst = bank_s[b][:, (c - 2 * g) * 256:(c - 2 * g + 1) * 256]
                    col = slice(c * P, (c + 1) * P)
                    kh, kl = (kp[u][:, c, :, :].rearrange("p g k -> p (g k)") for kp in (kp_hi, kp_lo))
                    mm(dst, q_hi[u][:, col], kh, True, False)
                    mm(dst, q_hi[u][:, col], kl, False, False)
                    last = mm(dst, q_lo[u][:, col], kh, False, True)
                last.then_inc(scores_filled, 1)

            def transpose_prob(t, u, g):
                b = (u + g) % 2
                pe.wait_ge(prob_ready, 4 * (3 * t + g) + 4)
                wait(pe, pt_lo_ready, 3 * t + g - 1)
                for e in range(GROUP):
                    last = nc.tensor.transpose(bank_t[b][:, e * P:(e + 1) * P], prob[b][:, e, :], ident[:])
                last.then_inc(pt_filled, 1)

            def weigh_values(t, u, g):
                b = (u + g) % 2
                pe.wait_ge(pt_lo_ready, 3 * t + g + 1)
                if g == 0:
                    pe.wait_ge(qkv_lo, 8 * t + 8)
                    wait(pe, h_ready, t)
                for e in range(GROUP):
                    h = GROUP * g + e
                    o = bank_o[h // 6][:, (h % 6) * VW:(h % 6 + 1) * VW]
                    mm(o, pt_hi[b][:, e, :], v_hi[u][:, h, :], True, False)
                    mm(o, pt_lo[b][:, e, :], v_hi[u][:, h, :], False, False)
                    last = mm(o[:, 0:HD], pt_hi[b][:, e, :], v_lo[u][:, h, :], False, True)
                last.then_inc(heads_done, 1)

            def transpose_o(t, u, half):
                pe.wait_ge(o_ready, 2 * t + half + 1)
                for c in range(3):
                    last = nc.tensor.transpose(bank_o[half][:, c * P:(c + 1) * P],
                                               o_norm[:, 6 * half + 2 * c:6 * half + 2 * c + 2, :].rearrange("p h d -> p (h d)"),
                                               ident[:])
                last.then_inc(ot_filled, 1)

            def project_out(t, u):
                pe.wait_ge(ot_lo_ready, 2 * t + 2)
                dst = bank_o[0][:, 0:D]
                for c in range(CH):
                    mm(dst, ot_hi[:, c, :], wp_hi[:, c, :], c == 0, False)
                    mm(dst, ot_hi[:, c, :], wp_lo[:, c, :], False, False)
                    mm(dst, ot_lo[:, c, :], wp_hi[:, c, :], False, False)
                mm(dst, ones_rows[:], bias_out[:], False, True).then_inc(out_filled, 1)

            def turn(run):
                run(scores, 1, 1)
                run(project, 0, 0)
                run(weigh_values, 2, 2)
                run(project, 0, 1)
                run(transpose_o, 2, 0)
                run(project, 0, 2)
                run(transpose_o, 2, 1)
                run(transpose_prob, 1, 0)
                run(project, 0, 3)
                run(scores, 1, 2)
                run(project, 0, 4)
                run(project_out, 2)
                run(transpose_prob, 1, 1)
                run(scores, 0, 0)
                run(weigh_values, 1, 0)
                run(transpose_prob, 1, 2)
                run(transpose_y, -1)
                run(project, 0, 5)
                run(weigh_values, 1, 1)

            pipeline(pe, n_seq, turn)




def second_attention(nc, A, h_all, ident, ones_rows, half_pow, psum, route, sb, sem, n_seq):
    HD = 16
    CH = 3
    QK = 2 * CH * P
    NG, GH = 4, 3
    VW = HD + 1
    SCALE = float(HD) ** -0.5 / (W_SCALE * W_SCALE)

    w_qk = Split(sb, "u_qk", QK)
    w_v = Split(sb, "u_v", D)
    w_p = Split(sb, "u_p", D)
    w_g = Split(sb, "u_g", N_EXP)
    bias_qk = sb("u_bias_qk", [P, QK], F16)
    bias_out = sb("u_bias_out", [P, D], F16)
    sel = sb("u_sel", [P, 2], F32)
    norm1 = sb("u_norm1", [P, 4], F32)
    norm2 = sb("u_norm2", [P, 4], F32)
    y_all = sb("u_y_all", [P, n_seq * D], F32)

    def pair(name, shape, dt):
        return [sb(f"{name}{u}", shape, dt) for u in range(2)]

    stats = [pair(f"u_stats_{k}", [P, 6], F32) for k in range(3)]
    moments = [pair(f"u_moments_{k}", [P, 2], F32) for k in range(3)]
    var_eps = [pair(f"u_var_eps_{k}", [P, 1], F32) for k in range(3)]
    rstd = [pair(f"u_rstd_{k}", [P, 1], F32) for k in range(3)]
    z = pair("u_z", [P, 2 * P], F32)
    xf = pair("u_xf", [P, 2 * P], F32)
    xt_hi = pair("u_xt_hi", [P, 2 * P], F16)
    xt_alo = pair("u_xt_alo", [P, P], F16)
    xt_b = pair("u_xt_b", [P, P], F16)
    q_hi = sb("u_q_hi", [P, CH * P], F16)
    q_st = pair("u_q_st", [P, CH * P], F16)
    k_hi = pair("u_k_hi", [P, CH * P], F16)
    k_lo = pair("u_k_lo", [P, CH * P], F16)
    v_hi = pair("u_v_hi", [P, HEADS, VW], F16)
    v_lo = pair("u_v_lo", [P, HEADS, HD], F16)
    row_max = pair("u_row_max", [P, GH], F32)
    neg_max = pair("u_neg_max", [P, GH], F32)
    prob = pair("u_prob", [P, GH, P], F32)
    pt_hi = pair("u_pt_hi", [P, GH * P], F16)
    pt_lo = pair("u_pt_lo", [P, GH * P], F16)
    recip = sb("u_recip", [P, HEADS], F32)
    o_norm = sb("u_o_norm", [P, HEADS + 4, HD], F32)
    ot_hi = sb("u_ot_hi", [P, 2 * P], F16)
    ot_alo = sb("u_ot_alo", [P, P], F16)
    ot_b = sb("u_ot_b", [P, P], F16)
    z2 = pair("u_z2", [P, 2 * P], F32)
    xf2 = sb("u_xf2", [P, 2 * P], F32)
    xm_hi = sb("u_xm_hi", [P, 2 * P], F16)
    xm_alo = sb("u_xm_alo", [P, P], F16)
    xm_b = sb("u_xm_b", [P, P], F16)
    logits = sb("u_logits", [P, N_EXP], F32)
    top = sb("u_top", [P, 8], F32)
    at = sb("u_at", [P, 8], U32)
    atf = sb("u_atf", [P, 2], F32)
    gap = sb("u_gap", [P, 1], F32)
    e2 = sb("u_e2", [P, 1], F32)
    den = sb("u_den", [P, 1], F32)
    minus_one = sb("u_minus_one", [P, 1], F32)
    picked = pair("u_picked", [P, 2, N_EXP], F32)
    picked_any = pair("u_picked_any", [P, N_EXP], F16)
    before = sb("u_before", [P, P], F16)
    all_ones = sb("u_all_ones", [P, P], F16)
    counted = pair("u_counted", [P, 2, N_EXP], F32)
    place = pair("u_place", [P, N_EXP], F32)
    picked_place = sb("u_picked_place", [P, N_EXP], F32)
    slot_f = pair("u_slot_f", [P, 2], F32)
    slot_now = pair("u_slot_now", [P, 2], I32)
    expert_no = sb("u_expert_no", [P, N_EXP], F32)
    stage = sb("u_stage", [P, 2, QK], F32)
    stage_v = sb("u_stage_v", [P, 2, D], F32)
    stage_p = sb("u_stage_p", [P, 2, D], F32)
    stage_g = sb("u_stage_g", [P, 2, N_EXP], F32)
    stage_bias = sb("u_stage_bias", [33, QK], F32)
    bqk_hi = sb("u_bqk_hi", [33, QK], F16)
    stage_bout = sb("u_stage_bout", [33, D], F32)
    bout_hi = sb("u_bout_hi", [33, D], F16)
    bv_col = sb("u_bv_col", [P, 2], F32)

    bank_st, bank_o, bank_w, bank_e = psum[0:4], psum[4], psum[5:7], psum[7]

    loaded = sem("b_loaded")
    weights_ready = sem("b_weights_ready")
    split_step = sem("b_split_step")
    bias_sum = sem("b_bias_sum")
    ln_step = [sem(f"b_ln{k}_step") for k in range(3)]
    rstd_ready = [sem(f"b_rstd{k}_ready") for k in range(3)]
    y_ready = sem("b_y_ready")
    z_ready = sem("b_z_ready")
    xt_filled = sem("b_xt_filled")
    xf_ready = sem("b_xf_ready")
    xt_hi_ready = sem("b_xt_hi_ready")
    xt_ready = sem("b_xt_ready")
    qkv_filled = sem("b_qkv_filled")
    qkv_hi = sem("b_qkv_hi")
    qkv_lo = sem("b_qkv_lo")
    scores_filled = sem("b_scores_filled")
    max_ready = sem("b_max_ready")
    neg_ready = sem("b_neg_ready")
    prob_ready = sem("b_prob_ready")
    pt_filled = sem("b_pt_filled")
    pt_hi_ready = sem("b_pt_hi_ready")
    pt_lo_ready = sem("b_pt_lo_ready")
    heads_done = sem("b_heads_done")
    recip_ready = sem("b_recip_ready")
    o_ready = sem("b_o_ready")
    ot_filled = sem("b_ot_filled")
    ot_hi_ready = sem("b_ot_hi_ready")
    ot_lo_ready = sem("b_ot_lo_ready")
    out_filled = sem("b_out_filled")
    x1_ready = sem("b_x1_ready")
    h_ready = sem("b_h_ready")
    z2_ready = sem("b_z2_ready")
    xm_filled = sem("b_xm_filled")
    xf2_ready = sem("b_xf2_ready")
    xm_hi_ready = sem("b_xm_hi_ready")
    xm_ready = sem("b_xm_ready")
    logits_filled = sem("b_logits_filled")
    logits_out = sem("b_logits_out")
    top_ready = sem("b_top_ready")
    at_ready = sem("b_at_ready")
    gap_ready = sem("b_gap_ready")
    e2_ready = sem("b_e2_ready")
    den_ready = sem("b_den_ready")
    gate_ready = sem("b_gate_ready")
    experts_kept = sem("b_experts_kept")
    atf_ready = sem("b_atf_ready")
    picked_ready = sem("b_picked_ready")
    any_ready = sem("b_any_ready")
    count_filled = sem("b_count_filled")
    count_out = sem("b_count_out")
    place_ready = sem("b_place_ready")
    running_ready = sem("b_running_ready")
    slot_ready = sem("b_slot_ready")
    slot_now_ready = sem("b_slot_now_ready")
    slot_kept = sem("b_slot_kept")
    queued = [sem(f"b_queued{u}") for u in range(2)]
    consts_ready = sem("b_consts_ready")

    def seq(s):
        return bass.ts(s, D)

    COUNTS = slice(2 * P + 2 * N_EXP, 2 * P + 4 * N_EXP)
    block = nc.Block()
    with block:
        @block.sync
        def _(sp):
            load_split(sp, loaded, stage, A["qk_dup_wT"], QK)
            load_split(sp, loaded, stage_v, A["L0_ffn_qkv_w"][:, 2 * D:3 * D], D)
            load_split(sp, loaded, stage_p, A["L0_ffn_proj_w"], D)
            load_split(sp, loaded, stage_g, A["L0_ffn_gate_w"], N_EXP)
            for r in (0, 32):
                sp.dma_start(stage_bias[r:r + 1, :], A["qk_dup_b"]).then_inc(loaded, 16)
                sp.dma_start(stage_bout[r:r + 1, :], A["L0_ffn_proj_b"]).then_inc(loaded, 16)
            with nc.allow_non_contiguous_dma(reason="columns of 192 numbers, once"):
                v_b = A["L0_ffn_qkv_b"][0, 2 * D:3 * D]
                sp.dma_start(bv_col[:, 0:1], v_b[0:P].unsqueeze(1)).then_inc(loaded, 16)
                sp.dma_start(bv_col[0:DB, 1:2], v_b[P:D].unsqueeze(1)).then_inc(loaded, 16)
                for tile, names in ((norm1, ("L0_ffn_ln1_g", "L0_ffn_ln1_b")), (norm2, ("L0_ffn_ln2_g", "L0_ffn_ln2_b"))):
                    for k, n in enumerate(names):
                        sp.dma_start(tile[:, k:k + 1], A[n][0, 0:P].unsqueeze(1)).then_inc(loaded, 16)
                        for r in (0, DB):
                            sp.dma_start(tile[r:r + DB, 2 + k:3 + k], A[n][0, P:D].unsqueeze(1)).then_inc(loaded, 16)
            sp.dma_start(sel[:], A["sel"]).then_inc(loaded, 16)
            sp.dma_start(expert_no[:], A["expert_no"].partition_broadcast(P)).then_inc(loaded, 16)
            sp.dma_start(route.running[:], A["queue_start"].partition_broadcast(P)).then_inc(loaded, 16)
        LOADS = 16 * (12 + 4 + 2 + 12 + 3)

        @block.gpsimd
        def _(pool):
            def rsqrt(s, u, k):
                pool.wait_ge(ln_step[k], 3 * s + 3)
                nc.gpsimd.tensor_tensor(rstd[k][u][:], var_eps[k][u][:], half_pow[:], ALU.pow).then_inc(rstd_ready[k], 1)

            def gap_of(s, u):
                pool.wait_ge(top_ready, s + 1)
                wait(pool, e2_ready, s)
                nc.gpsimd.tensor_tensor(gap[:], top[:, 1:2], top[:, 0:1], ALU.subtract).then_inc(gap_ready, 1)

            def expert_numbers(s, u):
                waits_apart(pool, (loaded, LOADS), (at_ready, s + 1), (picked_ready, 2 * s))
                nc.gpsimd.tensor_copy(atf[:], at[:, 0:2]).then_inc(atf_ready, 1)

            def one_hot(s, u):
                waits_apart(pool, (loaded, LOADS), (atf_ready, s + 1), (slot_ready, 2 * s - 2))
                nc.gpsimd.tensor_copy(route.experts[:, bass.ds(2 * s, 2)], atf[:]).then_inc(experts_kept, 1)
                for k in range(2):
                    nc.gpsimd.tensor_scalar(picked[u][:, k, :], expert_no[:], atf[:, k:k + 1], None, ALU.is_equal
                                            ).then_inc(picked_ready, 1)

            def either(s, u):
                pool.wait_ge(picked_ready, 2 * s + 2)
                wait(pool, count_filled, s - 1)
                nc.gpsimd.tensor_tensor(picked_any[u][:], picked[u][:, 0, :], picked[u][:, 1, :], ALU.add).then_inc(any_ready, 1)

            def denominator(s, u):
                waits_apart(pool, (loaded, LOADS), (e2_ready, s + 1), (gate_ready, 2 * s))
                nc.gpsimd.tensor_scalar(den[:], e2[:], 1.0, None, ALU.add).then_inc(den_ready, 1)

            def first_gate(s, u):
                pool.wait_ge(den_ready, s + 1)
                nc.gpsimd.tensor_tensor(route.gates[:, bass.ds(2 * s, 1)], den[:], minus_one[:], ALU.pow).then_inc(gate_ready, 1)

            def second_gate(s, u):
                pool.wait_ge(gate_ready, 2 * s + 1)
                nc.gpsimd.tensor_tensor(route.gates[:, bass.ds(2 * s + 1, 1)], route.gates[:, bass.ds(2 * s, 1)], e2[:], ALU.mult
                                        ).then_inc(gate_ready, 1)

            def places(s, u):
                pool.wait_ge(count_out, s + 1)
                wait(pool, running_ready, s)
                wait(pool, slot_ready, 2 * s)
                nc.gpsimd.tensor_tensor(place[u][:], counted[u][:, 0, :], route.running[:], ALU.add).then_inc(place_ready, 1)
                pool.wait_ge(place_ready, s + 1)
                nc.gpsimd.tensor_tensor(route.running[:], route.running[:], counted[u][:, 1, :], ALU.add).then_inc(running_ready, 1)

            def enqueue(s, u):
                waits_apart(pool, (loaded, LOADS), (slot_ready, 2 * s + 2), (queued[u], 16 * (s - u)))
                nc.gpsimd.tensor_copy(slot_now[u][:], slot_f[u][:]).then_inc(slot_now_ready, 1)
                waits_apart(pool, (loaded, LOADS), (slot_now_ready, s + 1))
                nc.gpsimd.tensor_copy(route.slots[:, bass.ds(2 * s, 2)], slot_now[u][:]).then_inc(slot_kept, 1)
                for k in range(2):
                    nc.gpsimd.indirect_dma_start(
                        out=route.x_queue, out_offset=bass.IndirectOffsetOnAxis(ap=slot_now[u][:, k:k + 1].bitcast(U32), axis=0),
                        in_=z2[u][:, :], in_offset=None).then_inc(queued[u], 16)

            nc.gpsimd.memset(minus_one[:], -1.0).then_inc(consts_ready, 1)
            nc.gpsimd.memset(all_ones[:], 1.0).then_inc(consts_ready, 1)
            pool.wait_ge(consts_ready, 2)
            nc.gpsimd.affine_select(out=before[:], in_=all_ones[:], compare_op=ALU.is_gt, fill=0.0, base=0,
                                    pattern=[[1, P]], channel_multiplier=-1).then_inc(consts_ready, 1)
            pool.wait_ge(loaded, LOADS)
            def turn(run):
                run(second_gate, 2)
                run(gap_of, 1)
                run(places, 2)
                run(enqueue, 2)
                run(expert_numbers, 1)
                run(denominator, 1)
                run(one_hot, 1)
                run(rsqrt, -3, 1)
                run(rsqrt, 0, 2)
                run(either, 1)
                run(rsqrt, -4, 0)
                run(first_gate, 1)

            pipeline(pool, n_seq, turn)
            for u in range(2):
                pool.wait_ge(queued[u], 16 * n_seq)

        @block.scalar
        def _(act):
            def to_hi(dst, src):
                return nc.scalar.activation(dst, src, ACT.Copy, scale=W_SCALE)

            act.wait_ge(loaded, LOADS)
            for w, st in ((w_qk, stage), (w_v, stage_v), (w_p, stage_p), (w_g, stage_g)):
                to_hi(w.a_hi[:], st[:, 0, :]).then_inc(weights_ready, 1)
                to_hi(w.b_hi[:], st[:, 1, :]).then_inc(weights_ready, 1)
            to_hi(bqk_hi[0:1, :], stage_bias[0:1, :]).then_inc(weights_ready, 1)
            to_hi(bqk_hi[32:33, :], stage_bias[32:33, :]).then_inc(weights_ready, 1)

            def affine(dst, bank, norm, sems, first_wait):
                first_wait()
                for k in range(2):
                    nc.scalar.activation(dst[:, k * P:(k + 1) * P], bank[:, k * P:(k + 1) * P], ACT.Identity,
                                         bias=norm[:, 2 * k + 1:2 * k + 2], scale=norm[:, 2 * k:2 * k + 1]).then_inc(sems, 1)

            def xt_affine(s, u):
                act.wait_ge(xt_filled, s + 1)
                affine(xf[u], bank_w[0], norm1, xf_ready, lambda: wait(act, xt_ready, 2 * s - 2))

            def xt_high(s, u):
                act.wait_ge(xf_ready, 2 * s + 2)
                wait(act, qkv_filled, 3 * s - 3)
                nc.scalar.copy(xt_hi[u][:], xf[u][:]).then_inc(xt_hi_ready, 1)

            def qkv_high(s, u, j):
                act.wait_ge(qkv_filled, 3 * s + j + 1)
                w = bank_w[j % 2]
                if j == 0:
                    wait(act, qkv_lo, 3 * s - 2)
                    nc.scalar.copy(q_hi[:], w[:, 0:HALF]).then_inc(qkv_hi, 1)
                elif j == 1:
                    wait(act, scores_filled, 4 * s - 4)
                    nc.scalar.copy(k_hi[u][:], w[:, 0:HALF]).then_inc(qkv_hi, 1)
                else:
                    wait(act, heads_done, 4 * s - 4)
                    nc.scalar.copy(v_hi[u][:, :, 0:HD], w[:, 0:D].rearrange("p (h d) -> p h d", d=HD)).then_inc(qkv_hi, 1)

            def exps(t, u, g):
                act.wait_ge(neg_ready, 4 * t + g + 1)
                wait(act, pt_filled, 4 * t + g - 1)
                for e in range(GH):
                    nc.scalar.activation(prob[g % 2][:, e, :], bank_st[g][:, e * P:(e + 1) * P], ACT.Exp,
                                         bias=neg_max[g % 2][:, e:e + 1], scale=SCALE).then_inc(prob_ready, 1)

            def pt_high(t, u, g):
                act.wait_ge(pt_filled, 4 * t + g + 1)
                wait(act, heads_done, 4 * t + g - 1)
                nc.scalar.copy(pt_hi[g % 2][:], bank_st[g][:, 0:HALF]).then_inc(pt_hi_ready, 1)

            def ot_high(t, u):
                act.wait_ge(ot_filled, t + 1)
                wait(act, out_filled, t)
                nc.scalar.copy(ot_hi[:], bank_e[:, 0:2 * P]).then_inc(ot_hi_ready, 1)

            def xm_affine(t, u):
                act.wait_ge(xm_filled, t + 1)
                affine(xf2, bank_e, norm2, xf2_ready, lambda: wait(act, xm_ready, 2 * t))

            def xm_high(t, u):
                act.wait_ge(xf2_ready, 2 * t + 2)
                wait(act, logits_filled, t)
                nc.scalar.copy(xm_hi[:], xf2[:]).then_inc(xm_hi_ready, 1)

            def second_exp(t, u):
                act.wait_ge(gap_ready, t + 1)
                wait(act, gate_ready, 2 * t)
                nc.scalar.activation(e2[:], gap[:], ACT.Exp).then_inc(e2_ready, 1)

            def turn(run):
                run(qkv_high, -1, 0)
                run(pt_high, 0, 0)
                run(second_exp, 2)
                run(exps, 0, 2)
                run(qkv_high, -1, 1)
                run(pt_high, 0, 1)
                run(exps, 0, 3)
                run(qkv_high, -1, 2)
                run(pt_high, 0, 2)
                run(xm_affine, 1)
                run(xm_high, 1)
                run(pt_high, 0, 3)
                run(xt_affine, -2)
                run(xt_high, -2)
                run(exps, -1, 0)
                run(exps, -1, 1)
                run(ot_high, 0)

            pipeline(act, n_seq, turn)

        @block.vector
        def _(dve):
            def to_lo(dst, src, hi):
                return nc.vector.scalar_tensor_tensor(dst, src, W_SCALE, hi, ALU.mult, ALU.subtract)

            nc.vector.memset(bias_qk[:], 0.0).then_inc(split_step, 1)
            nc.vector.memset(bias_out[:], 0.0).then_inc(split_step, 1)
            for u in range(2):
                nc.vector.memset(v_hi[u][:, :, HD:VW], 1.0).then_inc(split_step, 1)
            dve.wait_ge(weights_ready, 10)
            for w, st in ((w_qk, stage), (w_v, stage_v), (w_p, stage_p), (w_g, stage_g)):
                to_lo(w.a_lo[:], st[:, 0, :], w.a_hi[:]).then_inc(split_step, 1)
                to_lo(w.b_lo[:], st[:, 1, :], w.b_hi[:]).then_inc(split_step, 1)
            dve.wait_ge(split_step, 2)
            nc.vector.tensor_copy(bias_qk[0:1, :], bqk_hi[0:1, :]).then_inc(split_step, 1)
            to_lo(bias_qk[32:33, :], stage_bias[32:33, :], bqk_hi[32:33, :]).then_inc(split_step, 1)
            dve.wait_ge(bias_sum, 1)
            for r in (0, 32):
                nc.vector.tensor_tensor(stage_bout[r:r + 1, :], bank_e[r:r + 1, 0:D], stage_bout[r:r + 1, :], ALU.add
                                        ).then_inc(split_step, 1)
            dve.wait_ge(split_step, 16)
            for r in (0, 32):
                nc.vector.tensor_scalar(bout_hi[r:r + 1, :], stage_bout[r:r + 1, :], W_SCALE * W_SCALE, None, ALU.mult
                                        ).then_inc(split_step, 1)
            dve.wait_ge(split_step, 18)
            nc.vector.tensor_copy(bias_out[0:1, :], bout_hi[0:1, :]).then_inc(split_step, 1)
            nc.vector.scalar_tensor_tensor(bias_out[32:33, :], stage_bout[32:33, :], W_SCALE * W_SCALE, bout_hi[32:33, :],
                                           ALU.mult, ALU.subtract).then_inc(split_step, 1)
            dve.wait_ge(split_step, 20)

            def ln_stats(k, s, u, src, *waits):
                waits_apart(dve, (loaded, LOADS), *waits)
                nc.vector.bn_stats(stats[k][u][:], src).then_inc(ln_step[k], 1)

            def ln_mean(s, u, k):
                used = ((y_ready, s - 1), (z_ready, 2 * s - 2), (z2_ready, 2 * s - 2))[k]
                waits_apart(dve, (loaded, LOADS), (ln_step[k], 3 * s + 1), used)
                nc.vector.bn_aggr(moments[k][u][:], stats[k][u][:]).then_inc(ln_step[k], 1)

            def ln_variance(s, u, k):
                dve.wait_ge(ln_step[k], 3 * s + 2)
                nc.vector.tensor_scalar(var_eps[k][u][:], moments[k][u][:, 1:2], LN_EPS, None, ALU.add).then_inc(ln_step[k], 1)

            def ln_h(s, u):
                ln_stats(0, s, u, h_all[:, seq(s)])

            def make_y(s, u):
                dve.wait_ge(rstd_ready[0], s + 1)
                nc.vector.tensor_scalar(y_all[:, seq(s)], h_all[:, seq(s)], moments[0][u][:, 0:1], rstd[0][u][:, 0:1],
                                        ALU.subtract, ALU.mult).then_inc(y_ready, 1)

            def ln_y(s, u):
                ln_stats(1, s, u, y_all[:, seq(s)], (y_ready, s + 1))

            def make_z(s, u):
                dve.wait_ge(rstd_ready[1], s + 1)
                wait(dve, xt_filled, s - 1)
                for dst, src in ((z[u][:, 0:D], y_all[:, seq(s)]), (z[u][:, D:2 * P], y_all[:, bass.ds(s * D + P, DB)])):
                    nc.vector.tensor_scalar(dst, src, moments[1][u][:, 0:1], rstd[1][u][:, 0:1],
                                            ALU.subtract, ALU.mult).then_inc(z_ready, 1)

            def low_parts(alo, b, hi, full, sems):
                nc.vector.tensor_tensor(alo, full[:, 0:P], hi[:, 0:P], ALU.subtract).then_inc(sems, 1)
                nc.vector.scalar_tensor_tensor(b, hi[:, P:2 * P], sel[:, 0:1], full[:, P:2 * P], ALU.mult, ALU.add
                                               ).then_inc(sems, 1)

            def xt_low(s, u):
                dve.wait_ge(xt_hi_ready, s + 1)
                low_parts(xt_alo[u][:], xt_b[u][:], xt_hi[u], xf[u], xt_ready)

            def qkv_low(s, u, j):
                dve.wait_ge(qkv_hi, 3 * s + j + 1)
                w = bank_w[j % 2]
                if j == 0:
                    wait(dve, scores_filled, 4 * s - 4)
                    nc.vector.scalar_tensor_tensor(q_st[u][:], q_hi[:], sel[:, 1:2], w[:, 0:HALF], ALU.mult, ALU.add
                                                   ).then_inc(qkv_lo, 1)
                elif j == 1:
                    nc.vector.tensor_tensor(k_lo[u][:], w[:, 0:HALF], k_hi[u][:], ALU.subtract).then_inc(qkv_lo, 1)
                else:
                    nc.vector.tensor_tensor(v_lo[u][:], w[:, 0:D].rearrange("p (h d) -> p h d", d=HD), v_hi[u][:, :, 0:HD],
                                            ALU.subtract).then_inc(qkv_lo, 1)

            def maxima(t, u, g):
                dve.wait_ge(scores_filled, 4 * t + g + 1)
                wait(dve, neg_ready, 4 * t + g - 1)
                nc.vector.tensor_reduce(row_max[g % 2][:], bank_st[g][:, 0:HALF].rearrange("p (e k) -> p e k", k=P), AX, ALU.max
                                        ).then_inc(max_ready, 1)

            def neg_maxima(t, u, g):
                dve.wait_ge(max_ready, 4 * t + g + 1)
                wait(dve, prob_ready, 3 * (4 * t + g - 1))
                nc.vector.tensor_scalar(neg_max[g % 2][:], row_max[g % 2][:], -SCALE, None, ALU.mult).then_inc(neg_ready, 1)

            def pt_low(t, u, g):
                dve.wait_ge(pt_hi_ready, 4 * t + g + 1)
                nc.vector.tensor_tensor(pt_lo[g % 2][:], bank_st[g][:, 0:HALF], pt_hi[g % 2][:], ALU.subtract).then_inc(pt_lo_ready, 1)

            o_view = bank_o[:, 0:HEADS * VW].rearrange("p (h d) -> p h d", d=VW)

            def row_sums(t, u):
                dve.wait_ge(heads_done, 4 * t + 4)
                wait(dve, o_ready, 2 * t)
                nc.vector.reciprocal(recip[:], o_view[:, :, HD]).then_inc(recip_ready, 1)

            def normalise(t, u):
                dve.wait_ge(recip_ready, t + 1)
                wait(dve, ot_filled, t)
                for dst, src in ((slice(0, HEADS), slice(0, HEADS)), (slice(HEADS, HEADS + 4), slice(8, HEADS))):
                    n_heads = src.stop - src.start
                    nc.vector.tensor_tensor(o_norm[:, dst, :], o_view[:, src, 0:HD],
                                            recip[:, src].unsqueeze(2).to_broadcast([P, n_heads, HD]), ALU.mult).then_inc(o_ready, 1)

            def ot_low(t, u):
                dve.wait_ge(ot_hi_ready, t + 1)
                low_parts(ot_alo[:], ot_b[:], ot_hi, bank_e, ot_lo_ready)

            def make_x1(t, u):
                dve.wait_ge(out_filled, t + 1)
                nc.vector.scalar_tensor_tensor(y_all[:, seq(t)], bank_e[:, 0:D], 1.0 / (W_SCALE * W_SCALE), y_all[:, seq(t)],
                                               ALU.mult, ALU.add).then_inc(x1_ready, 1)

            def ln_x1(t, u):
                ln_stats(2, t, u, y_all[:, seq(t)], (x1_ready, t + 1))

            def make_z2(t, u):
                dve.wait_ge(rstd_ready[2], t + 1)
                wait(dve, queued[u], 16 * (t - u))
                for dst, src in ((z2[u][:, 0:D], y_all[:, seq(t)]), (z2[u][:, D:2 * P], y_all[:, bass.ds(t * D + P, DB)])):
                    nc.vector.tensor_scalar(dst, src, moments[2][u][:, 0:1], rstd[2][u][:, 0:1],
                                            ALU.subtract, ALU.mult).then_inc(z2_ready, 1)

            def add_x1(t, u):
                dve.wait_ge(x1_ready, t + 1)
                nc.vector.tensor_tensor(h_all[:, seq(t)], h_all[:, seq(t)], y_all[:, seq(t)], ALU.add).then_inc(h_ready, 1)

            def xm_low(t, u):
                dve.wait_ge(xm_hi_ready, t + 1)
                wait(dve, logits_filled, t)
                low_parts(xm_alo[:], xm_b[:], xm_hi, xf2, xm_ready)

            def take_logits(t, u):
                dve.wait_ge(logits_filled, t + 1)
                wait(dve, at_ready, t)
                nc.vector.tensor_scalar(logits[:], bank_e[:, 2 * P:2 * P + N_EXP], 1.0 / W_SCALE, None, ALU.mult).then_inc(logits_out, 1)

            def largest(t, u):
                waits_apart(dve, (loaded, LOADS), (logits_out, t + 1), (gap_ready, t))
                nc.vector.max(top[:], logits[:]).then_inc(top_ready, 1)

            def largest_at(t, u):
                waits_apart(dve, (loaded, LOADS), (top_ready, t + 1), (atf_ready, t))
                nc.vector.max_index(at[:], top[:], logits[:]).then_inc(at_ready, 1)

            def counts(t, u):
                dve.wait_ge(count_filled, t + 1)
                wait(dve, running_ready, t)
                nc.vector.tensor_copy(counted[u][:].rearrange("p a e -> p (a e)"), bank_e[:, COUNTS]).then_inc(count_out, 1)

            def slots(t, u):
                dve.wait_ge(place_ready, t + 1)
                wait(dve, slot_now_ready, t)
                for k in range(2):
                    wait(dve, slot_ready, 2 * t + k)
                    nc.vector.tensor_tensor_reduce(picked_place[:], picked[u][:, k, :], place[u][:], 1.0, 0.0, ALU.mult, ALU.add,
                                                   slot_f[u][:, k:k + 1]).then_inc(slot_ready, 1)

            def turn(run):
                run(maxima, 0, 3)
                run(ot_low, 1)
                run(neg_maxima, 0, 2)
                run(qkv_low, -1, 0)
                run(add_x1, 3)
                run(neg_maxima, 0, 3)
                run(pt_low, 0, 0)
                run(make_x1, 1)
                run(ln_x1, 1)
                run(ln_mean, 1, 2)
                run(ln_variance, 1, 2)
                run(qkv_low, -1, 1)
                run(make_z2, 1)
                run(pt_low, 0, 1)
                run(make_z, -2)
                run(qkv_low, -1, 2)
                run(make_y, -3)
                run(maxima, -1, 0)
                run(pt_low, 0, 2)
                run(neg_maxima, -1, 0)
                run(xm_low, 1)
                run(pt_low, 0, 3)
                run(maxima, -1, 1)
                run(ln_variance, -4, 0)
                run(take_logits, 1)
                run(xt_low, -2)
                run(largest, 1)
                run(row_sums, 0)
                run(counts, 2)
                run(ln_y, -3)
                run(largest_at, 1)
                run(neg_maxima, -1, 1)
                run(normalise, 0)
                run(ln_mean, -3, 1)
                run(ln_variance, -3, 1)
                run(ln_h, -5)
                run(slots, 2)
                run(maxima, -1, 2)
                run(ln_mean, -5, 0)

            pipeline(dve, n_seq, turn)

        @block.tensor
        def _(pe):
            def mm(dst, lhsT, rhs, start, stop):
                return nc.tensor.matmul(dst, lhsT, rhs, start=start, stop=stop)

            pe.wait_ge(loaded, LOADS)
            for r in (0, 32):
                mm(bank_e[r:r + 1, 0:D], bv_col[:, 0:1], stage_p[:, 0, :], True, False)
                last = mm(bank_e[r:r + 1, 0:D], bv_col[0:DB, 1:2], stage_p[0:DB, 1, :], False, True)
            last.then_inc(bias_sum, 1)
            pe.wait_ge(split_step, 20)

            def transpose_x(bank, src):
                nc.tensor.transpose(bank[:, 0:P], src[:, 0:P], ident[:])
                return nc.tensor.transpose(bank[:, P:2 * P], src[:, P:2 * P], ident[:])

            def transpose_z(s, u):
                pe.wait_ge(z_ready, 2 * s + 2)
                wait(pe, qkv_lo, 3 * s)
                transpose_x(bank_w[0], z[u]).then_inc(xt_filled, 1)

            def project(s, u, j):
                w = bank_w[j % 2]
                if j == 0:
                    pe.wait_ge(xt_ready, 2 * s + 2)
                elif j == 1:
                    wait(pe, qkv_lo, 3 * s - 1)
                else:
                    pe.wait_ge(qkv_lo, 3 * s + 1)
                parts = (xt_hi[u][:, 0:P], xt_alo[u][:], xt_b[u][:])
                if j < 2:
                    for c in range(CH):
                        col = slice((CH * j + c) * P, (CH * j + c + 1) * P)
                        dst = w[:, c * P:(c + 1) * P]
                        for k, (x_part, w_part) in enumerate(w_qk.passes(*parts, col)):
                            mm(dst, w_part, x_part, k == 0, False)
                        last = mm(dst, bias_qk[:, col], ones_rows[:], False, True)
                else:
                    for k, (x_part, w_part) in enumerate(w_v.passes(*parts, slice(0, D))):
                        last = mm(w[:, 0:D], x_part, w_part, k == 0, k == 4)
                last.then_inc(qkv_filled, 1)

            def scores(t, u, g):
                if g == 0:
                    pe.wait_ge(qkv_lo, 3 * t + 2)
                wait(pe, pt_lo_ready, 4 * t + g - 3)
                r = slice(32 * g, 32 * g + 32)
                for c in range(GH):
                    col = slice(c * P, (c + 1) * P)
                    mm(bank_st[g][:, col], q_st[u][r, col], k_hi[u][r, col], True, False)
                    last = mm(bank_st[g][:, col], q_st[u][r, col], k_lo[u][r, col], False, True)
                last.then_inc(scores_filled, 1)

            def transpose_prob(t, u, g):
                pe.wait_ge(prob_ready, 3 * (4 * t + g) + 3)
                for e in range(GH):
                    last = nc.tensor.transpose(bank_st[g][:, e * P:(e + 1) * P], prob[g % 2][:, e, :], ident[:])
                last.then_inc(pt_filled, 1)

            def weigh_values(t, u, g):
                pe.wait_ge(pt_lo_ready, 4 * t + g + 1)
                if g == 0:
                    pe.wait_ge(qkv_lo, 3 * t + 3)
                    wait(pe, o_ready, 2 * t)
                for e in range(GH):
                    h = 4 * e + g
                    o = bank_o[:, h * VW:(h + 1) * VW]
                    col = slice(e * P, (e + 1) * P)
                    mm(o, pt_hi[g % 2][:, col], v_hi[u][:, h, :], True, False)
                    mm(o, pt_lo[g % 2][:, col], v_hi[u][:, h, :], False, False)
                    last = mm(o[:, 0:HD], pt_hi[g % 2][:, col], v_lo[u][:, h, :], False, True)
                last.then_inc(heads_done, 1)

            def transpose_o(t, u):
                pe.wait_ge(o_ready, 2 * t + 2)
                wait(pe, logits_out, t)
                wait(pe, count_out, t - 1)
                transpose_x(bank_e, o_norm[:].rearrange("p h d -> p (h d)")).then_inc(ot_filled, 1)

            def project_out(t, u):
                pe.wait_ge(ot_lo_ready, 2 * t + 2)
                for k, (o_part, w_part) in enumerate(w_p.passes(ot_hi[:, 0:P], ot_alo[:], ot_b[:], slice(0, D))):
                    mm(bank_e[:, 0:D], o_part, w_part, k == 0, False)
                mm(bank_e[:, 0:D], ones_rows[:], bias_out[:], False, True).then_inc(out_filled, 1)

            def transpose_z2(t, u):
                pe.wait_ge(z2_ready, 2 * t + 2)
                transpose_x(bank_e, z2[u]).then_inc(xm_filled, 1)

            def gate_logits(t, u):
                pe.wait_ge(xm_ready, 2 * t + 2)
                for k, (x_part, w_part) in enumerate(w_g.passes(xm_hi[:, 0:P], xm_alo[:], xm_b[:], slice(0, N_EXP))):
                    last = mm(bank_e[:, 2 * P:2 * P + N_EXP], x_part, w_part, k == 0, k == 4)
                last.then_inc(logits_filled, 1)

            def count(t, u):
                pe.wait_ge(any_ready, t + 1)
                pe.wait_ge(logits_out, n_seq if isinstance(t, int) and t == n_seq - 1 else t + 2)
                wait(pe, count_out, t)
                at = COUNTS.start
                mm(bank_e[:, at:at + N_EXP], before[:], picked_any[u][:], True, True)
                mm(bank_e[:, at + N_EXP:at + 2 * N_EXP], all_ones[:], picked_any[u][:], True, True).then_inc(count_filled, 1)

            pe.wait_ge(consts_ready, 3)
            def turn(run):
                run(project_out, 1)
                run(transpose_prob, 0, 1)
                run(transpose_prob, 0, 2)
                run(weigh_values, 0, 0)
                run(project, -1, 2)
                run(scores, -1, 0)
                run(transpose_z2, 1)
                run(transpose_prob, 0, 3)
                run(weigh_values, 0, 1)
                run(transpose_z, -2)
                run(scores, -1, 1)
                run(scores, -1, 2)
                run(gate_logits, 1)
                run(weigh_values, 0, 2)
                run(weigh_values, 0, 3)
                run(count, 2)
                run(scores, -1, 3)
                run(project, -2, 0)
                run(transpose_o, 0)
                run(transpose_prob, -1, 0)
                run(project, -2, 1)

            pipeline(pe, n_seq, turn)


class Route:

    def __init__(self, nc, sb, n_seq):
        self.tokens = n_seq * P
        self.stride = self.tokens + TILE
        self.x_queue = nc.dram_tensor("x_queue", [N_EXP * self.stride, 2 * P], F32, kind="Internal").ap()
        self.slots = sb("route_slots", [P, 2 * n_seq], I32)
        self.experts = sb("route_experts", [P, 2 * n_seq], F32)
        self.gates = sb("route_gates", [P, 2 * n_seq], F32)
        self.running = sb("route_running", [P, N_EXP], F32)
        self.tiles = 2 * self.tokens // TILE + N_EXP
        self.y_tiles = nc.dram_tensor("y_tiles", [self.tiles * TILE, D], F32, kind="Internal").ap()


def experts(nc, A, h_all, ident, ones_rows, psum, route, sb, sem, n_seq):
    NT = route.tiles
    A2 = TILE // P
    w1 = Split(sb, "w1", N_EXP * HID)
    w2_hi = sb("w2_hi", [P, N_EXP * HC, D], F16)
    w2_lo = sb("w2_lo", [P, N_EXP * HC, D], F16)
    b1 = sb("b1", [P, N_EXP * HC], F32)
    bias2 = sb("bias2", [P, N_EXP, D], F16)
    stage1 = sb("stage1", [P, 2, HID], F32)
    stage2 = sb("stage2", [P, HC, D], F32)
    stage_b2 = sb("stage_b2", [33, N_EXP, D], F32)
    b2_hi = sb("b2_hi", [33, N_EXP, D], F16)
    norm2 = sb("norm2", [P, 4], F32)
    zeros = sb("zeros", [P, A2, 2 * P], F32)
    consts = sb("consts", [P, 2, N_EXP], F32)
    tile_no = sb("tile_no", [1, NT], F32)
    filled = sb("filled", [P, N_EXP], F32)
    filled_i = sb("filled_i", [P, N_EXP], I32)
    end_i = sb("end_i", [P, N_EXP], I32)
    tiles_i = sb("tiles_i", [P, N_EXP], I32)
    tiles = sb("tiles", [P, N_EXP], F32)
    upto = [sb(f"upto{k}", [P, N_EXP], F32) for k in range(4)]
    first = sb("first", [P, N_EXP], F32)
    last_row = sb("last_row", [P, N_EXP], F32)
    shift = sb("shift", [P, N_EXP], F32)
    moved = [sb(f"moved{k}", [P, 2 * n_seq], F32) for k in range(3)]
    t_a = sb("t_a", [1, NT, N_EXP], F32)
    t_b = sb("t_b", [1, NT, N_EXP], F32)
    t_q = sb("t_q", [1, NT, N_EXP], F32)
    t_e = sb("t_e", [1, NT], F32)
    t_r = sb("t_r", [1, NT], F32)
    tile_expert = sb("tile_expert", [1, NT], I32)
    tile_row = sb("tile_row", [1, NT], I32)
    t_c = sb("t_c", [1, NT, N_EXP], F32)

    def pair(name, shape, dt):
        return [sb(f"{name}{u}", shape, dt) for u in range(2)]

    x_rows = pair("x_rows", [P, A2, 2 * P], F32)
    xf = sb("c_xf", [P, 2, TILE], F32)
    x_hi = pair("c_x_hi", [P, 2, TILE], F16)
    x_alo = pair("c_x_alo", [P, TILE], F16)
    x_b = pair("c_x_b", [P, TILE], F16)
    sel = sb("c_sel", [P, 2], F32)
    hf = pair("hf", [P, TILE], F32)
    h_hi = pair("h_hi", [P, TILE], F16)
    h_lo = pair("h_lo", [P, TILE], F16)
    y_out = pair("y_out", [P, A2, D], F32)
    bank_x, bank_h, bank_y = psum[0:2], psum[2:6], psum[6:8]

    loaded = sem("c_loaded")
    weights_loaded = sem("c_weights_loaded")
    hi_ready = sem("c_hi_ready")
    split_ready = sem("c_split_ready")
    zeroed = sem("c_zeroed")
    table_step = sem("c_table_step")
    padded = sem("c_padded")
    x_loaded = [sem(f"c_x_loaded{u}") for u in range(2)]
    x_filled = sem("c_x_filled")
    xf_ready = sem("c_xf_ready")
    x_hi_ready = sem("c_x_hi_ready")
    x_ready = sem("c_x_ready")
    h_filled = sem("c_h_filled")
    gelu_ready = sem("c_gelu_ready")
    h_hi_ready = sem("c_h_hi_ready")
    h_lo_ready = sem("c_h_lo_ready")
    chunk_used = sem("c_chunk_used")
    y_ready = sem("c_y_ready")
    y_stored = [sem(f"c_y_stored{u}") for u in range(2)]
    TABLE_STEPS = 20

    block = nc.Block()
    with block:
        @block.sync
        def _(sp):
            sp.dma_start(sel[:], A["sel"]).then_inc(loaded, 16)
            sp.dma_start(consts[:, 0, :], A["expert_no"].partition_broadcast(P)).then_inc(loaded, 16)
            sp.dma_start(consts[:, 1, :], A["queue_start"].partition_broadcast(P)).then_inc(loaded, 16)
            sp.dma_start(tile_no[:], A["tile_no"]).then_inc(loaded, 16)
            with nc.allow_non_contiguous_dma(reason="bias columns, once"):
                sp.dma_start(b1[:], A["L0_ffn_b1"].rearrange("e (c p) -> p (e c)", p=P)).then_inc(loaded, 16)
                for k, n in enumerate(("L0_ffn_ln2_g", "L0_ffn_ln2_b")):
                    sp.dma_start(norm2[:, k:k + 1], A[n][0, 0:P].unsqueeze(1)).then_inc(loaded, 16)
                    for r in (0, DB):
                        sp.dma_start(norm2[r:r + DB, 2 + k:3 + k], A[n][0, P:D].unsqueeze(1)).then_inc(loaded, 16)
            for r in (0, 32):
                sp.dma_start(stage_b2[r:r + 1, :, :], A["L0_ffn_b2"].unsqueeze(0)).then_inc(loaded, 16)
            for e in range(N_EXP):
                wait(sp, split_ready, 2 + 3 * e if e else 0)
                load_split(sp, weights_loaded, stage1, A["L0_ffn_w1"][e], HID)
                sp.dma_start(stage2[:], A["L0_ffn_w2"][e].rearrange("(c p) d -> p c d", p=P)).then_inc(weights_loaded, 16)

            with sp.Fori(0, NT // 2) as i:
                for u in range(2):
                    j = 2 * i + u
                    sp.wait_ge(y_ready, j + 1)
                    sp.dma_start(route.y_tiles[bass.ts(j, TILE), :].rearrange("(a p) d -> p a d", p=P), y_out[u][:]
                                 ).then_inc(y_stored[u], 16)
            for u in range(2):
                sp.wait_ge(y_stored[u], 8 * NT)
        LOADS = 16 * 13

        @block.gpsimd
        def _(pool):
            nc.gpsimd.memset(zeros[:], 0.0).then_inc(zeroed, 1)
            pool.wait_ge(zeroed, 1)
            pool.wait_ge(table_step, TABLE_STEPS)
            for e in range(N_EXP):
                end = pool.value_load(end_i[0:1, e:e + 1], min_val=0, max_val=N_EXP * route.stride - TILE)
                pool.dma_start(route.x_queue[bass.ds(end, TILE), :].rearrange("(a p) d -> p a d", p=P), zeros[:]).then_inc(padded, 16)
            pool.wait_ge(padded, 16 * N_EXP)

            def load(j, u):
                wait(pool, x_filled, j - 1)
                row = pool.value_load(tile_row[0:1, bass.ds(j, 1)], min_val=0, max_val=N_EXP * route.stride - TILE)
                pool.dma_start(x_rows[u][:], route.x_queue[bass.ds(row, TILE), :].rearrange("(a p) d -> p a d", p=P)
                               ).then_inc(x_loaded[u], 16)

            load(0, 0)
            load(1, 1)
            with pool.Fori(0, NT // 2 - 1) as i:
                for u in range(2):
                    load(2 * i + 2 + u, u)

        @block.scalar
        def _(act):
            act.wait_ge(loaded, LOADS)
            for r in (0, 32):
                nc.scalar.activation(b2_hi[r:r + 1, :, :], stage_b2[r:r + 1, :, :], ACT.Copy, scale=W_SCALE).then_inc(hi_ready, 1)
            for e in range(N_EXP):
                act.wait_ge(weights_loaded, 64 * e + 64)
                c = slice(e * HID, (e + 1) * HID)
                for dst, src in ((w1.a_hi[:, c], stage1[:, 0, :]), (w1.b_hi[:, c], stage1[:, 1, :]),
                                 (w2_hi[:, e * HC:(e + 1) * HC, :], stage2[:])):
                    nc.scalar.activation(dst, src, ACT.Copy, scale=W_SCALE).then_inc(hi_ready, 1)
            act.wait_ge(table_step, TABLE_STEPS)

            def x_high(j, u):
                act.wait_ge(x_filled, j + 1)
                wait(act, x_ready, 2 * j)
                for k in range(2):
                    nc.scalar.activation(xf[:, k, :], bank_x[u][:, k * TILE:(k + 1) * TILE], ACT.Identity,
                                         bias=norm2[:, 2 * k + 1:2 * k + 2], scale=norm2[:, 2 * k:2 * k + 1]).then_inc(xf_ready, 1)
                act.wait_ge(xf_ready, 2 * j + 2)
                wait(act, h_filled, HC * (j - 1))
                nc.scalar.copy(x_hi[u][:], xf[:]).then_inc(x_hi_ready, 1)

            def tile(j, u, more=True):
                e = act.value_load(tile_expert[0:1, bass.ds(j, 1)], min_val=0, max_val=N_EXP - 1)
                for c in range(HC):
                    k = j * HC + c
                    act.wait_ge(h_filled, k + 1)
                    wait(act, h_lo_ready, k - 1)
                    nc.scalar.activation(hf[c % 2][:], bank_h[c % 4][:, 0:TILE], ACT.Gelu, bias=b1[:, bass.ds(e * HC + c, 1)],
                                         scale=1.0 / W_SCALE).then_inc(gelu_ready, 1)
                    if c == 2 and more:
                        x_high(j + 1, 1 - u)

            x_high(0, 0)
            tile(0, 0)
            with act.Fori(0, NT // 2 - 1) as i:
                for v in range(2):
                    tile(2 * i + 1 + v, 1 - v)
            tile(NT - 1, 1, more=False)

        @block.vector
        def _(dve):
            n = 0
            ops = [
                lambda: nc.vector.tensor_tensor(filled[:], route.running[:], consts[:, 1, :], ALU.subtract),
                lambda: nc.vector.tensor_copy(end_i[:], route.running[:]),
                lambda: nc.vector.tensor_scalar(filled[:], filled[:], float(TILE - 1), None, ALU.add),
                lambda: nc.vector.tensor_copy(filled_i[:], filled[:]),
                lambda: nc.vector.tensor_scalar(tiles_i[:], filled_i[:], TILE.bit_length() - 1, None, ALU.logical_shift_right),
                lambda: nc.vector.tensor_copy(tiles[:], tiles_i[:]),
                lambda: nc.vector.tensor_scalar(upto[0][:], tiles[:], 1.0, None, ALU.max),
                lambda: nc.vector.tensor_copy(tiles[:], upto[0][:]),
            ]
            for k in range(3):
                ops.append(lambda k=k: nc.vector.tensor_copy(upto[k + 1][:], upto[k][:]))
                ops.append(lambda k=k: nc.vector.tensor_tensor(upto[k + 1][:, 1 << k:N_EXP], upto[k][:, 1 << k:N_EXP],
                                                               upto[k][:, 0:N_EXP - (1 << k)], ALU.add))
            whole = [1, NT, N_EXP]
            j_of = tile_no[:].unsqueeze(2).to_broadcast(whole)

            def per_queue(t):
                return t[0:1].unsqueeze(1).to_broadcast(whole)
            ops += [
                lambda: nc.vector.tensor_tensor(first[:], upto[3][:], tiles[:], ALU.subtract),
                lambda: nc.vector.tensor_tensor(t_a[:], j_of, per_queue(upto[3][:]), ALU.is_ge),
                lambda: nc.vector.tensor_reduce(t_e[:], t_a[:], AX, ALU.add),
                lambda: nc.vector.tensor_scalar(t_e[:], t_e[:], float(N_EXP - 1), None, ALU.min),
                lambda: nc.vector.tensor_tensor(t_a[:], j_of, per_queue(first[:]), ALU.subtract),
                lambda: nc.vector.tensor_scalar(last_row[:], tiles[:], -1.0, None, ALU.add),
            ]
            def rows_of(number, dst):
                return [
                    lambda: nc.vector.tensor_scalar(t_c[:], number[:], float(TILE), None, ALU.mult),
                    lambda: nc.vector.tensor_tensor(t_c[:], t_c[:], per_queue(consts[:, 1, :]), ALU.add),
                    lambda: nc.vector.tensor_tensor(t_c[:], t_c[:], t_q[:], ALU.mult),
                    lambda: nc.vector.tensor_reduce(t_r[:], t_c[:], AX, ALU.add),
                    lambda: nc.vector.tensor_copy(dst[:], t_r[:]),
                ]
            ops += [lambda: nc.vector.tensor_tensor(t_q[:], per_queue(consts[:, 0, :]), t_e[:].unsqueeze(2).to_broadcast(whole), ALU.is_equal)]
            ops += [lambda: nc.vector.tensor_tensor(t_b[:], t_a[:], per_queue(last_row[:]), ALU.min)]
            ops += rows_of(t_b, tile_row)
            ops += [lambda: nc.vector.tensor_copy(tile_expert[:], t_e[:])]
            ops += [
                lambda: nc.vector.scalar_tensor_tensor(shift[:], first[:], float(TILE), consts[:, 1, :], ALU.mult, ALU.subtract),
                lambda: nc.vector.tensor_copy(moved[0][:], route.slots[:]),
            ]
            for e in range(N_EXP):
                ops += [
                    lambda e=e: nc.vector.tensor_scalar(moved[2][:], route.experts[:], float(e), shift[:, e:e + 1], ALU.is_equal, ALU.mult),
                    lambda e=e: nc.vector.tensor_tensor(moved[(e + 1) % 2][:], moved[e % 2][:], moved[2][:], ALU.add),
                ]
            ops += [lambda: nc.vector.tensor_copy(route.slots[:], moved[0][:])]
            dve.wait_ge(loaded, LOADS)
            made = sem("c_table_part_made")
            for k, op in enumerate(ops):
                op().then_inc(made, 1)
                dve.wait_ge(made, k + 1)
            nc.vector.memset(bias2[:], 0.0).then_inc(table_step, TABLE_STEPS)
            dve.wait_ge(table_step, TABLE_STEPS)

            dve.wait_ge(hi_ready, 2)
            nc.vector.tensor_copy(bias2[0:1, :, :], b2_hi[0:1, :, :]).then_inc(split_ready, 1)
            nc.vector.scalar_tensor_tensor(bias2[32:33, :, :], stage_b2[32:33, :, :], W_SCALE, b2_hi[32:33, :, :], ALU.mult,
                                           ALU.subtract).then_inc(split_ready, 1)
            for e in range(N_EXP):
                dve.wait_ge(hi_ready, 2 + 3 * e + 3)
                c, cc = slice(e * HID, (e + 1) * HID), slice(e * HC, (e + 1) * HC)
                for dst, src, hi in ((w1.a_lo[:, c], stage1[:, 0, :], w1.a_hi[:, c]), (w1.b_lo[:, c], stage1[:, 1, :], w1.b_hi[:, c]),
                                     (w2_lo[:, cc, :], stage2[:], w2_hi[:, cc, :])):
                    nc.vector.scalar_tensor_tensor(dst, src, W_SCALE, hi, ALU.mult, ALU.subtract).then_inc(split_ready, 1)

            def x_low(j, u):
                dve.wait_ge(x_hi_ready, j + 1)
                nc.vector.tensor_tensor(x_alo[u][:], xf[:, 0, :], x_hi[u][:, 0, :], ALU.subtract).then_inc(x_ready, 1)
                nc.vector.scalar_tensor_tensor(x_b[u][:], x_hi[u][:, 1, :], sel[:, 0:1], xf[:, 1, :], ALU.mult, ALU.add
                                               ).then_inc(x_ready, 1)

            def y_part(j, u):
                dve.wait_ge(chunk_used, HC * j + HC)
                wait(dve, y_stored[u], 8 * (j - u))
                nc.vector.tensor_scalar(y_out[u][:].rearrange("p a d -> p (a d)"), bank_y[u][:, 0:A2 * D], 1.0 / W_SCALE, None,
                                        ALU.mult).then_inc(y_ready, 1)

            def tile(j, u, more=True, before=True):
                for c in range(HC):
                    k = j * HC + c
                    dve.wait_ge(gelu_ready, k + 1)
                    wait(dve, chunk_used, k - 1)
                    nc.vector.tensor_copy(h_hi[c % 2][:], hf[c % 2][:]).then_inc(h_hi_ready, 1)
                    dve.wait_ge(h_hi_ready, k + 1)
                    nc.vector.tensor_tensor(h_lo[c % 2][:], hf[c % 2][:], h_hi[c % 2][:], ALU.subtract).then_inc(h_lo_ready, 1)
                    if c == 1 and before:
                        y_part(j - 1, 1 - u)
                    if c == 3 and more:
                        x_low(j + 1, 1 - u)

            x_low(0, 0)
            tile(0, 0, before=False)
            with dve.Fori(0, NT // 2 - 1) as i:
                for v in range(2):
                    tile(2 * i + 1 + v, 1 - v)
            tile(NT - 1, 1, more=False)
            y_part(NT - 1, 1)

        @block.tensor
        def _(pe):
            def mm(dst, lhsT, rhs, start, stop, **k):
                return nc.tensor.matmul(dst, lhsT, rhs, start=start, stop=stop, **k)

            pe.wait_ge(split_ready, 2 + 3 * N_EXP)
            pe.wait_ge(table_step, TABLE_STEPS)

            def transpose_x(j, u):
                pe.wait_ge(x_loaded[u], 8 * (j - u) + 16)
                wait(pe, xf_ready, 2 * (j - 1))
                for a in range(A2):
                    c = slice(a * P, (a + 1) * P)
                    d = slice(TILE + a * P, TILE + (a + 1) * P)
                    nc.tensor.transpose(bank_x[u][:, c], x_rows[u][:, a, 0:P], ident[:])
                    last = nc.tensor.transpose(bank_x[u][:, d], x_rows[u][:, a, P:2 * P], ident[:])
                last.then_inc(x_filled, 1)

            def up(j, u, e, c):
                k = j * HC + c
                wait(pe, gelu_ready, k - 3)
                if c == 0:
                    pe.wait_ge(x_ready, 2 * j + 2)
                dst = bank_h[c % 4][:, 0:TILE]
                for i, (x_part, w_part) in enumerate(w1.passes(x_hi[u][:, 0, :], x_alo[u][:], x_b[u][:], bass.ds(e * HID + c * P, P))):
                    last = mm(dst, w_part, x_part, i == 0, i == 4)
                last.then_inc(h_filled, 1)

            def down(j, u, e, c):
                k = j * HC + c
                if c == 0:
                    wait(pe, y_ready, j - 1)
                pe.wait_ge(h_lo_ready, k + 1)
                row = bass.ds(e * HC + c, 1)
                wh, wl = (w[:, row, :].rearrange("p o d -> p (o d)") for w in (w2_hi, w2_lo))
                for a in range(A2):
                    dst = bank_y[u][:, a * D:(a + 1) * D]
                    tok = slice(a * P, (a + 1) * P)
                    if c == 0:
                        mm(dst, ones_rows[:], bias2[:, bass.ds(e, 1), :].rearrange("p o d -> p (o d)"), a == 0, False,
                           skip_group_check=True)
                    mm(dst, h_hi[c % 2][:, tok], wh, False, False, skip_group_check=True)
                    mm(dst, h_hi[c % 2][:, tok], wl, False, False, skip_group_check=True)
                    last = mm(dst, h_lo[c % 2][:, tok], wh, False, c == HC - 1, skip_group_check=True)
                last.then_inc(chunk_used, 1)

            def expert_of(j):
                return pe.value_load(tile_expert[0:1, bass.ds(j, 1)], min_val=0, max_val=N_EXP - 1)

            def tile(j, u, more=True):
                e = expert_of(j)
                for c in range(HC):
                    up(j, u, e, c)
                    if c >= 2:
                        down(j, u, e, c - 2)
                    if c == 0 and more:
                        transpose_x(j + 1, 1 - u)
                down(j, u, e, HC - 2)
                down(j, u, e, HC - 1)

            transpose_x(0, 0)
            tile(0, 0)
            with pe.Fori(0, NT // 2 - 1) as i:
                for v in range(2):
                    tile(2 * i + 1 + v, 1 - v)
            tile(NT - 1, 1, more=False)


def combine(nc, A, h_all, route, out, sb, sem, n_seq):
    DEPTH = 4
    y_rows = [[sb(f"y_rows{k}_{u}", [P, D], F32) for k in range(2)] for u in range(DEPTH)]
    slot_now = [sb(f"d_slot_now{u}", [P, 2], I32) for u in range(DEPTH)]
    slot_at_hand = sem("d_slot_at_hand")
    fetched = [sem(f"d_fetched{u}") for u in range(DEPTH)]
    added = sem("d_added")
    stored = sem("d_stored")

    def seq(s):
        return bass.ts(s, D)

    block = nc.Block()
    with block:
        @block.gpsimd
        def _(pool):
            def fetch(s, u):
                nc.gpsimd.tensor_copy(slot_now[u][:], route.slots[:, bass.ds(2 * s, 2)]).then_inc(slot_at_hand, 1)
                waits_apart(pool, (slot_at_hand, 1), (slot_at_hand, s + 1))
                for k in range(2):
                    nc.gpsimd.indirect_dma_start(
                        out=y_rows[u][k][:, :], out_offset=None, in_=route.y_tiles,
                        in_offset=bass.IndirectOffsetOnAxis(ap=slot_now[u][:, k:k + 1].bitcast(U32), axis=0),
                    ).then_inc(fetched[u], 16)

            for u in range(DEPTH):
                fetch(u, u)
            with pool.Fori(1, n_seq // DEPTH) as i:
                for u in range(DEPTH):
                    s = DEPTH * i + u
                    waits_apart(pool, (slot_at_hand, 1), (added, 2 * s - 2 * DEPTH + 2))
                    fetch(s, u)

        @block.vector
        def _(dve):
            with dve.Fori(0, n_seq // DEPTH) as i:
                for u in range(DEPTH):
                    s = DEPTH * i + u
                    dve.wait_ge(fetched[u], 32 * i + 32)
                    for k in range(2):
                        dve.wait_ge(added, 2 * s + k)
                        nc.vector.scalar_tensor_tensor(h_all[:, seq(s)], y_rows[u][k][:], route.gates[:, bass.ds(2 * s + k, 1)],
                                                       h_all[:, seq(s)], ALU.mult, ALU.add).then_inc(added, 1)

        @block.sync
        def _(sp):
            with sp.Fori(0, n_seq) as s:
                sp.wait_ge(added, 2 * s + 2)
                sp.dma_start(out[bass.ds(s, 1), :, :].rearrange("b s d -> s (b d)"), h_all[:, seq(s)]).then_inc(stored, 16)
            sp.wait_ge(stored, 16 * n_seq)


def kernel(**inputs):
    import numpy as np
    import concourse.bacc as bacc
    from concourse.bass_utils import run_bass_kernel_spmd

    a = {k: np.asarray(v) for k, v in inputs.items()}
    n_seq, n_tok = a["x"].shape
    for k in ("x", "itok_BS_0_1003", "itok_BS_0_5", "mask_BS_i1_0"):
        a[k] = a[k].T
    a["L0_attn_qkv_wT"] = a.pop("L0_attn_qkv_w").T
    a["L0_attn_proj_wT"] = a.pop("L0_attn_proj_w").T

    w, b = a["L0_ffn_qkv_w"], a["L0_ffn_qkv_b"]
    twice = np.concatenate([np.arange(16 * h, 16 * h + 16) for h in range(2 * HEADS) for _ in range(2)])
    a["qk_dup_wT"], a["qk_dup_b"] = w[:, twice], b[twice]

    p = np.arange(P)
    a["sel"] = np.stack([-(p >= DB).astype(np.float32), -(p % 32 >= 16).astype(np.float32)], axis=1)
    a["expert_no"] = np.arange(N_EXP, dtype=np.float32)
    a["queue_start"] = (np.arange(N_EXP) * (n_seq * n_tok + TILE)).astype(np.float32)
    a["tile_no"] = np.arange(2 * n_seq * n_tok // TILE + N_EXP, dtype=np.float32)

    nc = bacc.Bacc("TRN2", target_bir_lowering=False, num_devices=1)
    arrays, aps = {}, {}
    for name, v in a.items():
        v = np.ascontiguousarray(v if v.ndim > 1 else v[None])
        arrays[f"in_{name}"] = v
        aps[name] = nc.dram_tensor(f"in_{name}", v.shape, mybir.dt.from_np(v.dtype), kind="ExternalInput").ap()
    out = nc.dram_tensor("out", [n_seq, n_tok, D], F32, kind="ExternalOutput").ap()
    build(nc, aps, out)
    return run_bass_kernel_spmd(nc, [arrays], core_ids=[0]).results[0]["out"]
```

```python
from contextlib import ExitStack

import numpy as np

import concourse.bass as bass
from concourse import mybir

F32 = mybir.dt.float32
F16 = mybir.dt.float16
I32 = mybir.dt.int32
U32 = mybir.dt.uint32
ALU = mybir.AluOpType
ACT = mybir.ActivationFunctionType
AX = mybir.AxisListType.X

P = 128
D = 192
DB = D - P
HEADS = 12
HALF = 384
W_SCALE = 64.0
LN_EPS = 1e-5
N_EXP = 8
ROW = 2 * P + 2
HID = 768
HC = HID // P
TILE = 256
GROUP = 4


def wait(eng, sem, value):
    if not (isinstance(value, int) and value <= 0):
        eng.wait_ge(sem, value)


def waits_apart(eng, over, *waits):
    waits = [(sem, value if isinstance(value, int) else eng.to_reg(value)) for sem, value in waits]
    eng.wait_ge(*over)
    for sem, value in waits:
        wait(eng, sem, value)


def pipeline(eng, n_seq, turn, alone=1):
    def one_turn(t, parity):
        def run(step, behind, *args):
            s = t - behind
            if not isinstance(t, int) or 0 <= s < n_seq:
                step(s, (parity - behind) % 2, *args)
        turn(run)

    distances = []
    turn(lambda step, behind, *args: distances.append(behind))
    nearest, farthest = min(distances), max(distances)
    first = farthest + alone
    pairs = (n_seq + nearest - first) // 2
    for t in range(nearest, first):
        one_turn(t, t % 2)
    with eng.Fori(0, pairs) as i:
        for v in range(2):
            one_turn(2 * i + first + v, (first + v) % 2)
    for t in range(first + 2 * pairs, n_seq + farthest):
        one_turn(t, t % 2)


class Split:

    def __init__(self, sb, name, cols):
        self.cols = cols
        self.a_hi, self.a_lo, self.b_hi, self.b_lo = (
            sb(f"{name}_{part}", [P, cols], F16) for part in ("a_hi", "a_lo", "b_hi", "b_lo"))

    def passes(self, act_a_hi, act_a_lo, act_b, cols):
        return [(act_a_hi, self.a_hi[:, cols]), (act_a_lo, self.a_hi[:, cols]),
                (act_a_hi, self.a_lo[:, cols]), (act_b, self.b_hi[:, cols]), (act_b, self.b_lo[:, cols])]


def build(nc, A, out):
    n_seq = A["x"].shape[1]
    S_ALL = n_seq * D
    with ExitStack() as whole:
        def sb(name, shape, dt, ctx=whole):
            return ctx.enter_context(nc.sbuf_tensor(name, shape, dt))

        def sem(name):
            return whole.enter_context(nc.semaphore(name))

        h_all = sb("h_all", [P, S_ALL], F32)
        ident = sb("ident", [P, P], F32)
        ones_rows = sb("ones_rows", [P, P], F16)
        neg_low = sb("neg_low", [P, 1], F32)
        half_pow = sb("half_pow", [P, 1], F32)
        psum = [whole.enter_context(nc.psum_tensor(f"bank{i}", [P, 512], F32)) for i in range(8)]

        phases(nc, A, out, h_all, ident, ones_rows, neg_low, half_pow, psum, sb, sem, n_seq)


def load_split(eng, sems, stage, src, cols):
    eng.dma_start(stage[:, 0, 0:cols], src[0:P, :]).then_inc(sems, 16)
    eng.dma_start(stage[0:DB, 1, 0:cols], src[P:D, :]).then_inc(sems, 16)
    eng.dma_start(stage[DB:P, 1, 0:cols], src[P:D, :]).then_inc(sems, 16)


def phases(nc, A, out, h_all, ident, ones_rows, neg_low, half_pow, psum, sb, sem, n_seq):
    with ExitStack() as ctx:
        first_attention(nc, A, h_all, ident, ones_rows, neg_low, half_pow, psum,
                        lambda n, s, d: sb(n, s, d, ctx), sem, n_seq)
    with ExitStack() as routed:
        route = Route(nc, lambda n, s, d: sb(n, s, d, routed), n_seq)
        staged = Staged(lambda n, s, d: sb(n, s, d, routed), sem)
        with ExitStack() as ctx:
            second_attention(nc, A, h_all, ident, ones_rows, half_pow, psum, route, staged,
                             lambda n, s, d: sb(n, s, d, ctx), sem, n_seq)
        with ExitStack() as ctx:
            experts(nc, A, h_all, ident, ones_rows, psum, route, staged, lambda n, s, d: sb(n, s, d, ctx), sem, n_seq)
        with ExitStack() as ctx:
            combine(nc, A, h_all, route, out, lambda n, s, d: sb(n, s, d, ctx), sem, n_seq)


def first_attention(nc, A, h_all, ident, ones_rows, neg_low, half_pow, psum, sb, sem, n_seq):
    HD = 64
    CH = 6
    QK = 2 * CH * P
    SCALE = float(HD) ** -0.5 / (W_SCALE * W_SCALE)
    VW = HD + 1

    w_qk = Split(sb, "w_qk", QK)
    w_v = Split(sb, "w_v", CH * P)
    wp_hi = sb("wp_hi", [P, CH, D], F16)
    wp_lo = sb("wp_lo", [P, CH, D], F16)
    bias_qk = sb("bias_qk", [P, QK], F16)
    bias_out = sb("bias_out", [P, D], F16)
    pe_base = sb("pe_base", [P, D], F32)
    names = ("problem", "skill", "correct", "segment")
    tables = [A[f"L0_tok_{n}_table"] for n in names]
    sizes = [t.shape[0] for t in tables]
    ids_all = sb("ids_all", [P, 4, n_seq], I32)
    ids_i = [ids_all[:, n, :] for n in range(4)]
    ids_now = [sb(f"ids_now{u}", [P, 4], I32) for u in range(2)]
    coef = [sb(f"{n}_coef", [P, n_seq], F32) for n in names]
    rows = [[sb(f"{n}_rows{u}", [P, D], F32) for u in range(2)] for n in names]

    stats = [sb(f"stats{u}", [P, 6], F32) for u in range(2)]
    moments = [sb(f"moments{u}", [P, 2], F32) for u in range(2)]
    var_eps = [sb(f"var_eps{u}", [P, 1], F32) for u in range(2)]
    rstd = [sb(f"rstd{u}", [P, 1], F32) for u in range(2)]
    y = [sb(f"y{u}", [P, 2 * P], F32) for u in range(2)]
    xt_hi = [sb(f"xt_hi{u}", [P, 2 * P], F16) for u in range(2)]
    xt_alo = [sb(f"xt_alo{u}", [P, P], F16) for u in range(2)]
    xt_b = [sb(f"xt_b{u}", [P, P], F16) for u in range(2)]
    q_hi = [sb(f"q_hi{u}", [P, CH * P], F16) for u in range(2)]
    q_lo = [sb(f"q_lo{u}", [P, CH * P], F16) for u in range(2)]
    kp_hi = [sb(f"kp_hi{u}", [P, CH, 2, P], F16) for u in range(2)]
    kp_lo = [sb(f"kp_lo{u}", [P, CH, 2, P], F16) for u in range(2)]
    v_hi = [sb(f"v_hi{u}", [P, HEADS, VW], F16) for u in range(2)]
    v_lo = [sb(f"v_lo{u}", [P, HEADS, HD], F16) for u in range(2)]
    row_max = [sb(f"row_max{u}", [P, GROUP], F32) for u in range(2)]
    neg_max = [sb(f"neg_max{u}", [P, GROUP], F32) for u in range(2)]
    prob = [sb(f"prob{u}", [P, GROUP, P], F32) for u in range(2)]
    pt_hi = [sb(f"pt_hi{u}", [P, GROUP, P], F16) for u in range(2)]
    pt_lo = [sb(f"pt_lo{u}", [P, GROUP, P], F16) for u in range(2)]
    recip = sb("recip", [P, HEADS], F32)
    o_norm = sb("o_norm", [P, HEADS, HD], F32)
    ot_hi = sb("ot_hi", [P, CH, P], F16)
    ot_lo = sb("ot_lo", [P, CH, P], F16)
    stage = sb("stage", [P, 2, QK], F32)
    stage_v = sb("stage_v", [P, 2, CH * P], F32)
    stage_p = sb("stage_p", [P, CH, D], F32)
    stage_bias = sb("stage_bias", [33, QK], F32)
    stage_bout = sb("stage_bout", [33, D], F32)
    bout_hi = sb("bout_hi", [33, D], F16)
    bqk_hi = sb("bqk_hi", [33, QK], F16)
    bv_col = sb("bv_col", [P, CH], F32)
    wvec = sb("wvec", [P, 6], F32)
    idf = sb("idf", [P, n_seq], F32)
    idn = sb("idn", [P, n_seq], F32)

    bank_s, bank_t, bank_o, bank_w = psum[0:2], psum[2:4], psum[4:6], psum[6:8]

    loaded = sem("a_loaded")
    const_done = sem("a_const_done")
    wide_loaded = sem("a_wide_loaded")
    v_loaded = sem("a_v_loaded")
    split_step = sem("a_split_step")
    bias_sum = sem("a_bias_sum")
    masks_ready = sem("a_masks_ready")
    ids_ready = sem("a_ids_ready")
    ids_at_hand = sem("a_ids_at_hand")
    id_step = sem("a_id_step")
    weights_ready = sem("a_weights_ready")
    rows_loaded = [sem(f"a_rows_loaded{u}") for u in range(2)]
    embedded = sem("a_embedded")
    ln_step = sem("a_ln_step")
    rstd_ready = sem("a_rstd_ready")
    y_ready = sem("a_y_ready")
    xt_filled = sem("a_xt_filled")
    xt_hi_ready = sem("a_xt_hi_ready")
    xt_ready = sem("a_xt_ready")
    qkv_filled = sem("a_qkv_filled")
    qkv_hi = sem("a_qkv_hi")
    qkv_lo = sem("a_qkv_lo")
    scores_filled = sem("a_scores_filled")
    max_ready = sem("a_max_ready")
    neg_ready = sem("a_neg_ready")
    prob_ready = sem("a_prob_ready")
    pt_filled = sem("a_pt_filled")
    pt_hi_ready = sem("a_pt_hi_ready")
    pt_lo_ready = sem("a_pt_lo_ready")
    heads_done = sem("a_heads_done")
    recip_ready = sem("a_recip_ready")
    o_ready = sem("a_o_ready")
    ot_filled = sem("a_ot_filled")
    ot_hi_ready = sem("a_ot_hi_ready")
    ot_lo_ready = sem("a_ot_lo_ready")
    out_filled = sem("a_out_filled")
    h_ready = sem("a_h_ready")
    HI_AT = [1, 2, 4, 6, 7, 8]

    def seq(s):
        return bass.ts(s, D)

    wq_src, wv_src = A["L0_attn_qkv_wT"][:, 0:QK], A["L0_attn_qkv_wT"][:, QK:QK + CH * P]
    block = nc.Block()
    with block:
        @block.sync
        def _(sp):
            for n, ids in zip(("x", "itok_BS_0_1003", "itok_BS_0_5", "mask_BS_i1_0"), ids_i):
                sp.dma_start(ids, A[n]).then_inc(loaded, 16)
            sp.dma_start(wvec[:, 0:5], A["L0_tok_combine_w"].partition_broadcast(P)).then_inc(loaded, 16)
            sp.dma_start(wvec[:, 5:6], A["L0_tok_combine_b"].partition_broadcast(P)).then_inc(loaded, 16)
            sp.dma_start(pe_base[:], A["L0_tok_pe"]).then_inc(loaded, 16)
            load_split(sp, wide_loaded, stage, wq_src, QK)
            for r in (0, 32):
                sp.dma_start(stage_bias[r:r + 1, :], A["L0_attn_qkv_b"][:, 0:QK]).then_inc(wide_loaded, 16)
                sp.dma_start(stage_bout[r:r + 1, :], A["L0_attn_proj_b"]).then_inc(wide_loaded, 16)
            sp.dma_start(bv_col[:], A["L0_attn_qkv_b"][0, QK:QK + CH * P].rearrange("(c p) -> p c", p=P),
                         allow_slow_non_contiguous=True).then_inc(wide_loaded, 16)
            sp.dma_start(stage_p[:], A["L0_attn_proj_wT"].rearrange("(c p) d -> p c d", p=P)).then_inc(wide_loaded, 16)
            load_split(sp, v_loaded, stage_v, wv_src, CH * P)

        @block.gpsimd
        def _(pool):
            nc.gpsimd.memset(ident[:], 1.0).then_inc(masks_ready, 1)
            nc.gpsimd.memset(half_pow[:], -0.5).then_inc(masks_ready, 1)
            pool.wait_ge(masks_ready, 1)
            nc.gpsimd.affine_select(out=ident[:], in_=ident[:], compare_op=ALU.is_equal, fill=0.0, base=0,
                                    pattern=[[-1, P]], channel_multiplier=1).then_inc(masks_ready, 1)
            pool.wait_ge(masks_ready, 3)
            pool.wait_ge(ids_ready, 4)

            def gather(s, u):
                waits_apart(pool, (masks_ready, 3), (embedded, 4 * s - 4))
                nc.gpsimd.tensor_copy(ids_now[u][:], ids_all[:, :, bass.ds(s, 1)].rearrange("p n o -> p (n o)")).then_inc(ids_at_hand, 1)
                waits_apart(pool, (masks_ready, 3), (ids_at_hand, s + 1))
                for n in range(4):
                    nc.gpsimd.indirect_dma_start(
                        out=rows[n][u][:, :], out_offset=None, in_=tables[n],
                        in_offset=bass.IndirectOffsetOnAxis(ap=ids_now[u][:, n:n + 1].bitcast(U32), axis=0),
                    ).then_inc(rows_loaded[u], 16)

            def rsqrt(s, u):
                pool.wait_ge(ln_step, 3 * s + 3)
                nc.gpsimd.tensor_tensor(rstd[u][:], var_eps[u][:], half_pow[:], ALU.pow).then_inc(rstd_ready, 1)

            def turn(run):
                run(gather, 0)
                run(rsqrt, 1)

            pipeline(pool, n_seq, turn)

        @block.scalar
        def _(act):
            def to_hi(dst, src):
                return nc.scalar.activation(dst, src, ACT.Copy, scale=W_SCALE)

            act.wait_ge(wide_loaded, 16 * 9)
            to_hi(w_qk.a_hi[:], stage[:, 0, :]).then_inc(weights_ready, 1)
            to_hi(w_qk.b_hi[:], stage[:, 1, :]).then_inc(weights_ready, 1)
            to_hi(wp_hi[:], stage_p[:]).then_inc(weights_ready, 1)
            to_hi(bqk_hi[0:1, :], stage_bias[0:1, :]).then_inc(weights_ready, 1)
            to_hi(bqk_hi[32:33, :], stage_bias[32:33, :]).then_inc(weights_ready, 1)
            act.wait_ge(v_loaded, 48)
            to_hi(w_v.a_hi[:], stage_v[:, 0, :]).then_inc(weights_ready, 1)
            to_hi(w_v.b_hi[:], stage_v[:, 1, :]).then_inc(weights_ready, 1)

            def xt_high(s, u):
                act.wait_ge(xt_filled, s + 1)
                wait(act, qkv_filled, 6 * s - 6)
                nc.scalar.copy(xt_hi[u][:], bank_w[0][:, 0:2 * P]).then_inc(xt_hi_ready, 1)

            def qkv_high(s, u, j):
                w = bank_w[j % 2]
                act.wait_ge(qkv_filled, 6 * s + j + 1)
                if j < 2:
                    wait(act, scores_filled, 3 * s - 3)
                    nc.scalar.copy(q_hi[u][:, j * HALF:(j + 1) * HALF], w[:, 0:HALF]).then_inc(qkv_hi, 1)
                elif j < 4:
                    for g in range(2):
                        r = slice(64 * g, 64 * g + 64)
                        nc.scalar.copy(kp_hi[u][r, 3 * (j - 2):3 * (j - 1), g, :],
                                       w[r, 0:HALF].rearrange("p (c k) -> p c k", k=P)).then_inc(qkv_hi, 1)
                else:
                    wait(act, heads_done, 3 * s - 3)
                    nc.scalar.copy(v_hi[u][:, 6 * (j - 4):6 * (j - 3), 0:HD],
                                   w[:, 0:HALF].rearrange("p (h d) -> p h d", d=HD)).then_inc(qkv_hi, 1)

            def exps(t, u, g):
                b = (u + g) % 2
                act.wait_ge(neg_ready, 3 * t + g + 1)
                wait(act, pt_filled, 3 * t + g - 1)
                for e in range(GROUP):
                    nc.scalar.activation(prob[b][:, e, :], bank_s[b][:, e * P:(e + 1) * P], ACT.Exp,
                                         bias=neg_max[b][:, e:e + 1], scale=SCALE).then_inc(prob_ready, 1)

            def pt_high(t, u, g):
                b = (u + g) % 2
                act.wait_ge(pt_filled, 3 * t + g + 1)
                wait(act, heads_done, 3 * t + g - 1)
                nc.scalar.copy(pt_hi[b][:].rearrange("p e k -> p (e k)"), bank_t[b][:]).then_inc(pt_hi_ready, 1)

            def ot_high(t, u, half):
                act.wait_ge(ot_filled, 2 * t + half + 1)
                wait(act, out_filled, t)
                nc.scalar.copy(ot_hi[:, 3 * half:3 * half + 3, :].rearrange("p c k -> p (c k)"),
                               bank_o[half][:, 0:HALF]).then_inc(ot_hi_ready, 1)

            act.wait_ge(const_done, 1)
            def turn(run):
                run(ot_high, 3, 1)
                run(pt_high, 2, 0)
                run(qkv_high, 1, 2)
                run(qkv_high, 1, 3)
                run(pt_high, 2, 1)
                run(exps, 2, 2)
                run(qkv_high, 1, 4)
                run(pt_high, 2, 2)
                run(xt_high, 0)
                run(exps, 1, 0)
                run(qkv_high, 1, 5)
                run(qkv_high, 0, 0)
                run(exps, 1, 1)
                run(qkv_high, 0, 1)
                run(ot_high, 2, 0)

            pipeline(act, n_seq, turn)

        @block.vector
        def _(dve):
            nc.vector.memset(ones_rows[:], 0.0).then_inc(id_step, 1)
            nc.vector.memset(bias_qk[:], 0.0).then_inc(id_step, 1)
            nc.vector.memset(bias_out[:], 0.0).then_inc(id_step, 1)
            nc.vector.memset(neg_low[0:64, :], 0.0).then_inc(id_step, 1)
            nc.vector.memset(neg_low[64:P, :], -1.0).then_inc(id_step, 1)
            for u in range(2):
                for kp in (kp_hi[u], kp_lo[u]):
                    nc.vector.memset(kp[:], 0.0).then_inc(id_step, 1)
                nc.vector.memset(v_hi[u][:, :, HD:VW], 1.0).then_inc(id_step, 1)
            dve.wait_ge(id_step, 11)
            nc.vector.memset(ones_rows[0:1, :], 1.0).then_inc(id_step, 1)
            nc.vector.memset(ones_rows[32:33, :], 1.0).then_inc(id_step, 1)
            dve.wait_ge(loaded, 16 * 7)
            nc.vector.tensor_scalar(pe_base[:], pe_base[:], wvec[:, 0:1], wvec[:, 5:6], ALU.mult, ALU.add).then_inc(id_step, 1)
            done = 14
            for n, w_at in zip(range(4), (2, 3, 4, 1)):
                v_n = float(sizes[n])
                steps = [
                    lambda: nc.vector.tensor_copy(idf[:], ids_i[n]),
                    lambda: nc.vector.tensor_scalar(idn[:], idf[:], 0.0, v_n, ALU.is_lt, ALU.mult),
                    lambda: nc.vector.tensor_tensor(idf[:], idf[:], idn[:], ALU.add),
                    lambda: nc.vector.tensor_scalar(idf[:], idf[:], 0.0, v_n - 1.0, ALU.max, ALU.min),
                    lambda: nc.vector.tensor_scalar(coef[n][:], idf[:], 0.0, wvec[:, w_at:w_at + 1], ALU.not_equal, ALU.mult),
                ]
                for step in steps:
                    dve.wait_ge(id_step, done)
                    step().then_inc(id_step, 1)
                    done += 1
                nc.vector.tensor_copy(ids_i[n], idf[:]).then_inc(ids_ready, 1)
                dve.wait_ge(ids_ready, n + 1)
                dve.wait_ge(id_step, done)

            def embed(s, u, n):
                dve.wait_ge(rows_loaded[u], 32 * (s - u) + 64)
                wait(dve, embedded, 4 * s + n)
                base = pe_base[:] if n == 0 else h_all[:, seq(s)]
                nc.vector.scalar_tensor_tensor(h_all[:, seq(s)], rows[n][u][:], coef[n][:, bass.ds(s, 1)], base,
                                               ALU.mult, ALU.add).then_inc(embedded, 1)

            def ln_stats(s, u):
                waits_apart(dve, (const_done, 1), (embedded, 4 * s + 4))
                nc.vector.bn_stats(stats[u][:], h_all[:, seq(s)]).then_inc(ln_step, 1)

            def ln_aggr(s, u):
                waits_apart(dve, (const_done, 1), (ln_step, 3 * s + 1), (y_ready, 2 * s - 2))
                nc.vector.bn_aggr(moments[u][:], stats[u][:]).then_inc(ln_step, 1)

            def ln_eps(s, u):
                dve.wait_ge(ln_step, 3 * s + 2)
                nc.vector.tensor_scalar(var_eps[u][:], moments[u][:, 1:2], LN_EPS, None, ALU.add).then_inc(ln_step, 1)

            def ln_apply(s, u):
                dve.wait_ge(rstd_ready, s + 1)
                wait(dve, xt_filled, s - 1)
                for dst, src in ((y[u][:, 0:D], h_all[:, seq(s)]), (y[u][:, D:2 * P], h_all[:, bass.ds(s * D + P, DB)])):
                    nc.vector.tensor_scalar(dst, src, moments[u][:, 0:1], rstd[u][:, 0:1],
                                            ALU.subtract, ALU.mult).then_inc(y_ready, 1)

            def xt_low(s, u):
                dve.wait_ge(xt_hi_ready, s + 1)
                nc.vector.tensor_tensor(xt_alo[u][:], bank_w[0][:, 0:P], xt_hi[u][:, 0:P], ALU.subtract).then_inc(xt_ready, 1)
                nc.vector.scalar_tensor_tensor(xt_b[u][:], xt_hi[u][:, P:2 * P], neg_low[:, 0:1], bank_w[0][:, P:2 * P],
                                               ALU.mult, ALU.add).then_inc(xt_ready, 1)

            def qkv_low(s, u, j):
                w = bank_w[j % 2]
                dve.wait_ge(qkv_hi, 8 * s + HI_AT[j])
                if j < 2:
                    c = slice(j * HALF, (j + 1) * HALF)
                    nc.vector.tensor_tensor(q_lo[u][:, c], w[:, 0:HALF], q_hi[u][:, c], ALU.subtract).then_inc(qkv_lo, 1)
                elif j < 4:
                    for g in range(2):
                        r = slice(64 * g, 64 * g + 64)
                        c = slice(3 * (j - 2), 3 * (j - 1))
                        nc.vector.tensor_tensor(kp_lo[u][r, c, g, :], w[r, 0:HALF].rearrange("p (c k) -> p c k", k=P),
                                                kp_hi[u][r, c, g, :], ALU.subtract).then_inc(qkv_lo, 1)
                else:
                    c = slice(6 * (j - 4), 6 * (j - 3))
                    nc.vector.tensor_tensor(v_lo[u][:, c, :], w[:, 0:HALF].rearrange("p (h d) -> p h d", d=HD),
                                            v_hi[u][:, c, 0:HD], ALU.subtract).then_inc(qkv_lo, 1)

            def maxima(t, u, g):
                b = (u + g) % 2
                dve.wait_ge(scores_filled, 3 * t + g + 1)
                wait(dve, neg_ready, 3 * t + g - 1)
                nc.vector.tensor_reduce(row_max[b][:], bank_s[b][:].rearrange("p (e k) -> p e k", k=P), AX, ALU.max
                                        ).then_inc(max_ready, 1)

            def neg_maxima(t, u, g):
                b = (u + g) % 2
                dve.wait_ge(max_ready, 3 * t + g + 1)
                wait(dve, prob_ready, 4 * (3 * t + g - 1))
                nc.vector.tensor_scalar(neg_max[b][:], row_max[b][:], -SCALE, None, ALU.mult).then_inc(neg_ready, 1)

            def pt_low(t, u, g):
                b = (u + g) % 2
                dve.wait_ge(pt_hi_ready, 3 * t + g + 1)
                nc.vector.tensor_tensor(pt_lo[b][:].rearrange("p e k -> p (e k)"), bank_t[b][:],
                                        pt_hi[b][:].rearrange("p e k -> p (e k)"), ALU.subtract).then_inc(pt_lo_ready, 1)

            def o_view(half):
                return bank_o[half][:, 0:6 * VW].rearrange("p (h d) -> p h d", d=VW)

            def row_sums(t, u, half):
                dve.wait_ge(heads_done, 3 * t + 2 + half)
                wait(dve, o_ready, 2 * t)
                nc.vector.reciprocal(recip[:, 6 * half:6 * half + 6], o_view(half)[:, :, HD]).then_inc(recip_ready, 1)

            def normalise(t, u, half):
                dve.wait_ge(recip_ready, 2 * t + half + 1)
                wait(dve, ot_filled, 2 * t)
                nc.vector.tensor_tensor(o_norm[:, 6 * half:6 * half + 6, :], o_view(half)[:, :, 0:HD],
                                        recip[:, 6 * half:6 * half + 6].unsqueeze(2).to_broadcast([P, 6, HD]),
                                        ALU.mult).then_inc(o_ready, 1)

            def ot_low(t, u, half):
                dve.wait_ge(ot_hi_ready, 2 * t + half + 1)
                nc.vector.tensor_tensor(ot_lo[:, 3 * half:3 * half + 3, :].rearrange("p c k -> p (c k)"), bank_o[half][:, 0:HALF],
                                        ot_hi[:, 3 * half:3 * half + 3, :].rearrange("p c k -> p (c k)"),
                                        ALU.subtract).then_inc(ot_lo_ready, 1)

            def add_output(t, u):
                dve.wait_ge(out_filled, t + 1)
                nc.vector.scalar_tensor_tensor(h_all[:, seq(t)], bank_o[0][:, 0:D], 1.0 / (W_SCALE * W_SCALE), h_all[:, seq(t)],
                                               ALU.mult, ALU.add).then_inc(h_ready, 1)

            def to_lo(dst, src, hi):
                return nc.vector.scalar_tensor_tensor(dst, src, W_SCALE, hi, ALU.mult, ALU.subtract)

            dve.wait_ge(weights_ready, 1)
            to_lo(w_qk.a_lo[:], stage[:, 0, :], w_qk.a_hi[:]).then_inc(split_step, 1)
            dve.wait_ge(weights_ready, 2)
            to_lo(w_qk.b_lo[:], stage[:, 1, :], w_qk.b_hi[:]).then_inc(split_step, 1)
            dve.wait_ge(weights_ready, 5)
            to_lo(wp_lo[:], stage_p[:], wp_hi[:]).then_inc(split_step, 1)
            nc.vector.tensor_copy(bias_qk[0:1, :], bqk_hi[0:1, :]).then_inc(split_step, 1)
            to_lo(bias_qk[32:33, :], stage_bias[32:33, :], bqk_hi[32:33, :]).then_inc(split_step, 1)
            dve.wait_ge(bias_sum, 1)
            for r in (0, 32):
                nc.vector.tensor_tensor(stage_bout[r:r + 1, :], bank_t[0][r:r + 1, 0:D], stage_bout[r:r + 1, :], ALU.add
                                        ).then_inc(split_step, 1)
            dve.wait_ge(split_step, 7)
            for r in (0, 32):
                nc.vector.tensor_scalar(bout_hi[r:r + 1, :], stage_bout[r:r + 1, :], W_SCALE * W_SCALE, None, ALU.mult
                                        ).then_inc(split_step, 1)
            dve.wait_ge(split_step, 9)
            nc.vector.tensor_copy(bias_out[0:1, :], bout_hi[0:1, :]).then_inc(split_step, 1)
            nc.vector.scalar_tensor_tensor(bias_out[32:33, :], stage_bout[32:33, :], W_SCALE * W_SCALE, bout_hi[32:33, :],
                                           ALU.mult, ALU.subtract).then_inc(split_step, 1)
            dve.wait_ge(weights_ready, 7)
            to_lo(w_v.a_lo[:], stage_v[:, 0, :], w_v.a_hi[:]).then_inc(split_step, 1)
            to_lo(w_v.b_lo[:], stage_v[:, 1, :], w_v.b_hi[:]).then_inc(split_step, 1)
            dve.wait_ge(split_step, 13)
            nc.vector.memset(stats[0][:], 0.0).then_inc(const_done, 1)
            dve.wait_ge(const_done, 1)

            def turn(run):
                run(maxima, 4, 2)
                run(embed, 1, 1)
                run(qkv_low, 3, 1)
                run(embed, 1, 2)
                run(ot_low, 5, 0)
                run(embed, 1, 3)
                run(ot_low, 5, 1)
                run(ln_stats, 1)
                run(neg_maxima, 4, 2)
                run(qkv_low, 3, 2)
                run(qkv_low, 3, 3)
                run(pt_low, 4, 0)
                run(add_output, 5)
                run(pt_low, 4, 1)
                run(qkv_low, 3, 4)
                run(ln_aggr, 1)
                run(maxima, 3, 0)
                run(row_sums, 4, 0)
                run(ln_eps, 1)
                run(neg_maxima, 3, 0)
                run(pt_low, 4, 2)
                run(xt_low, 2)
                run(maxima, 3, 1)
                run(normalise, 4, 0)
                run(ln_apply, 1)
                run(neg_maxima, 3, 1)
                run(row_sums, 4, 1)
                run(qkv_low, 3, 5)
                run(normalise, 4, 1)
                run(qkv_low, 2, 0)
                run(embed, 0, 0)

            pipeline(dve, n_seq, turn)

        @block.tensor
        def _(pe):
            def mm(dst, lhsT, rhs, start, stop):
                return nc.tensor.matmul(dst, lhsT, rhs, start=start, stop=stop)

            pe.wait_ge(wide_loaded, 16 * 9)
            for r in (0, 32):
                for c in range(CH):
                    last = mm(bank_t[0][r:r + 1, 0:D], bv_col[:, c:c + 1], stage_p[:, c, :], c == 0, c == CH - 1)
            last.then_inc(bias_sum, 1)
            pe.wait_ge(masks_ready, 3)
            pe.wait_ge(const_done, 1)

            def transpose_y(s, u):
                pe.wait_ge(y_ready, 2 * s + 2)
                wait(pe, qkv_lo, 8 * s + HI_AT[4] - 8)
                nc.tensor.transpose(bank_w[0][:, 0:P], y[u][:, 0:P], ident[:])
                nc.tensor.transpose(bank_w[0][:, P:2 * P], y[u][:, P:2 * P], ident[:]).then_inc(xt_filled, 1)

            def project(s, u, j):
                w = bank_w[j % 2]
                if j == 0:
                    pe.wait_ge(xt_ready, 2 * s + 2)
                elif j == 1:
                    wait(pe, qkv_lo, 8 * s)
                else:
                    pe.wait_ge(qkv_lo, 8 * s + HI_AT[j - 2])
                parts = (xt_hi[u][:, 0:P], xt_alo[u][:], xt_b[u][:])
                if j < 4:
                    for c in range(3):
                        col = slice((3 * j + c) * P, (3 * j + c + 1) * P)
                        dst = w[:, c * P:(c + 1) * P]
                        for k, (x_part, w_part) in enumerate(w_qk.passes(*parts, col)):
                            mm(dst, w_part, x_part, k == 0, False)
                        last = mm(dst, bias_qk[:, col], ones_rows[:], False, True)
                else:
                    col = slice((j - 4) * HALF, (j - 3) * HALF)
                    for k, (x_part, w_part) in enumerate(w_v.passes(*parts, col)):
                        last = mm(w[:, 0:HALF], x_part, w_part, k == 0, k == 4)
                last.then_inc(qkv_filled, 1)

            def scores(t, u, g):
                b = (u + g) % 2
                if g == 0:
                    pe.wait_ge(qkv_lo, 8 * t + HI_AT[3])
                wait(pe, prob_ready, 4 * (3 * t + g - 1))
                for c in range(2 * g, 2 * g + 2):
                    dst = bank_s[b][:, (c - 2 * g) * 256:(c - 2 * g + 1) * 256]
                    col = slice(c * P, (c + 1) * P)
                    kh, kl = (kp[u][:, c, :, :].rearrange("p g k -> p (g k)") for kp in (kp_hi, kp_lo))
                    mm(dst, q_hi[u][:, col], kh, True, False)
                    mm(dst, q_hi[u][:, col], kl, False, False)
                    last = mm(dst, q_lo[u][:, col], kh, False, True)
                last.then_inc(scores_filled, 1)

            def transpose_prob(t, u, g):
                b = (u + g) % 2
                pe.wait_ge(prob_ready, 4 * (3 * t + g) + 4)
                wait(pe, pt_lo_ready, 3 * t + g - 1)
                for e in range(GROUP):
                    last = nc.tensor.transpose(bank_t[b][:, e * P:(e + 1) * P], prob[b][:, e, :], ident[:])
                last.then_inc(pt_filled, 1)

            def weigh_values(t, u, g):
                b = (u + g) % 2
                pe.wait_ge(pt_lo_ready, 3 * t + g + 1)
                if g == 0:
                    pe.wait_ge(qkv_lo, 8 * t + 8)
                    wait(pe, h_ready, t)
                for e in range(GROUP):
                    h = GROUP * g + e
                    o = bank_o[h // 6][:, (h % 6) * VW:(h % 6 + 1) * VW]
                    mm(o, pt_hi[b][:, e, :], v_hi[u][:, h, :], True, False)
                    mm(o, pt_lo[b][:, e, :], v_hi[u][:, h, :], False, False)
                    last = mm(o[:, 0:HD], pt_hi[b][:, e, :], v_lo[u][:, h, :], False, True)
                last.then_inc(heads_done, 1)

            def transpose_o(t, u, half):
                pe.wait_ge(o_ready, 2 * t + half + 1)
                for c in range(3):
                    last = nc.tensor.transpose(bank_o[half][:, c * P:(c + 1) * P],
                                               o_norm[:, 6 * half + 2 * c:6 * half + 2 * c + 2, :].rearrange("p h d -> p (h d)"),
                                               ident[:])
                last.then_inc(ot_filled, 1)

            def project_out(t, u):
                pe.wait_ge(ot_lo_ready, 2 * t + 2)
                dst = bank_o[0][:, 0:D]
                for c in range(CH):
                    mm(dst, ot_hi[:, c, :], wp_hi[:, c, :], c == 0, False)
                    mm(dst, ot_hi[:, c, :], wp_lo[:, c, :], False, False)
                    mm(dst, ot_lo[:, c, :], wp_hi[:, c, :], False, False)
                mm(dst, ones_rows[:], bias_out[:], False, True).then_inc(out_filled, 1)

            def turn(run):
                run(project, 2, 5)
                run(weigh_values, 3, 2)
                run(project, 1, 0)
                run(scores, 2, 2)
                run(transpose_o, 3, 0)
                run(project, 1, 1)
                run(transpose_prob, 2, 0)
                run(transpose_o, 3, 1)
                run(project, 1, 2)
                run(project, 1, 3)
                run(transpose_prob, 2, 1)
                run(project_out, 3)
                run(project, 1, 4)
                run(scores, 1, 0)
                run(transpose_prob, 2, 2)
                run(weigh_values, 2, 0)
                run(weigh_values, 2, 1)
                run(transpose_y, 0)
                run(scores, 1, 1)

            pipeline(pe, n_seq, turn)




def second_attention(nc, A, h_all, ident, ones_rows, half_pow, psum, route, staged, sb, sem, n_seq):
    HD = 16
    CH = 3
    QK = 2 * CH * P
    NG, GH = 4, 3
    VW = HD + 1
    SCALE = float(HD) ** -0.5 / (W_SCALE * W_SCALE)

    w_qk = Split(sb, "u_qk", QK)
    w_v = Split(sb, "u_v", D)
    w_p = Split(sb, "u_p", D)
    w_g = Split(sb, "u_g", N_EXP)
    bias_qk = sb("u_bias_qk", [P, QK], F16)
    bias_out = sb("u_bias_out", [P, D], F16)
    sel = sb("u_sel", [P, 2], F32)
    norm1 = sb("u_norm1", [P, 4], F32)
    norm2 = sb("u_norm2", [P, 4], F32)
    y_all = sb("u_y_all", [P, n_seq * D], F32)

    def pair(name, shape, dt):
        return [sb(f"{name}{u}", shape, dt) for u in range(2)]

    stats = [pair(f"u_stats_{k}", [P, 6], F32) for k in range(3)]
    moments = [pair(f"u_moments_{k}", [P, 2], F32) for k in range(3)]
    var_eps = [pair(f"u_var_eps_{k}", [P, 1], F32) for k in range(3)]
    rstd = [pair(f"u_rstd_{k}", [P, 1], F32) for k in range(3)]
    z = pair("u_z", [P, 2 * P], F32)
    xf = pair("u_xf", [P, 2 * P], F32)
    xt_hi = pair("u_xt_hi", [P, 2 * P], F16)
    xt_alo = pair("u_xt_alo", [P, P], F16)
    xt_b = pair("u_xt_b", [P, P], F16)
    q_hi = sb("u_q_hi", [P, CH * P], F16)
    q_st = pair("u_q_st", [P, CH * P], F16)
    k_hi = pair("u_k_hi", [P, CH * P], F16)
    k_lo = pair("u_k_lo", [P, CH * P], F16)
    v_hi = pair("u_v_hi", [P, HEADS, VW], F16)
    v_lo = pair("u_v_lo", [P, HEADS, HD], F16)
    row_max = pair("u_row_max", [P, GH], F32)
    neg_max = pair("u_neg_max", [P, GH], F32)
    prob = pair("u_prob", [P, GH, P], F32)
    pt_hi = pair("u_pt_hi", [P, GH * P], F16)
    pt_lo = pair("u_pt_lo", [P, GH * P], F16)
    recip = sb("u_recip", [P, HEADS], F32)
    o_norm = sb("u_o_norm", [P, HEADS + 4, HD], F32)
    ot_hi = sb("u_ot_hi", [P, 2 * P], F16)
    ot_alo = sb("u_ot_alo", [P, P], F16)
    ot_b = sb("u_ot_b", [P, P], F16)
    z2 = pair("u_z2", [P, ROW], F32)
    xf2 = sb("u_xf2", [P, 2 * P], F32)
    xm_hi = sb("u_xm_hi", [P, 2 * P], F16)
    xm_alo = sb("u_xm_alo", [P, P], F16)
    xm_b = sb("u_xm_b", [P, P], F16)
    logits = sb("u_logits", [P, N_EXP], F32)
    top = sb("u_top", [P, 8], F32)
    at = sb("u_at", [P, 8], U32)
    atf = sb("u_atf", [P, 2], F32)
    gap = sb("u_gap", [P, 1], F32)
    e2 = sb("u_e2", [P, 1], F32)
    den = sb("u_den", [P, 1], F32)
    minus_one = sb("u_minus_one", [P, 1], F32)
    picked = pair("u_picked", [P, 2, N_EXP], F32)
    picked_any = pair("u_picked_any", [P, N_EXP], F16)
    before = sb("u_before", [P, P], F16)
    all_ones = sb("u_all_ones", [P, P], F16)
    counted = pair("u_counted", [P, 2, N_EXP], F32)
    place = pair("u_place", [P, N_EXP], F32)
    picked_place = sb("u_picked_place", [P, N_EXP], F32)
    slot_f = pair("u_slot_f", [P, 2], F32)
    slot_now = pair("u_slot_now", [P, 2], I32)
    expert_no = sb("u_expert_no", [P, N_EXP], F32)
    token_rows = sb("u_token_rows", [P, n_seq], F32)
    stage = sb("u_stage", [P, 2, QK], F32)
    stage_v = sb("u_stage_v", [P, 2, D], F32)
    stage_p = sb("u_stage_p", [P, 2, D], F32)
    stage_g = sb("u_stage_g", [P, 2, N_EXP], F32)
    stage_bias = sb("u_stage_bias", [33, QK], F32)
    bqk_hi = sb("u_bqk_hi", [33, QK], F16)
    stage_bout = sb("u_stage_bout", [33, D], F32)
    bout_hi = sb("u_bout_hi", [33, D], F16)
    bv_col = sb("u_bv_col", [P, 2], F32)

    bank_st, bank_o, bank_w, bank_e = psum[0:4], psum[4], psum[5:7], psum[7]

    loaded = sem("b_loaded")
    weights_ready = sem("b_weights_ready")
    split_step = sem("b_split_step")
    bias_sum = sem("b_bias_sum")
    ln_step = [sem(f"b_ln{k}_step") for k in range(3)]
    rstd_ready = [sem(f"b_rstd{k}_ready") for k in range(3)]
    y_ready = sem("b_y_ready")
    z_ready = sem("b_z_ready")
    xt_filled = sem("b_xt_filled")
    xf_ready = sem("b_xf_ready")
    xt_hi_ready = sem("b_xt_hi_ready")
    xt_ready = sem("b_xt_ready")
    qkv_filled = sem("b_qkv_filled")
    qkv_hi = sem("b_qkv_hi")
    qkv_lo = sem("b_qkv_lo")
    scores_filled = sem("b_scores_filled")
    max_ready = sem("b_max_ready")
    neg_ready = sem("b_neg_ready")
    prob_ready = sem("b_prob_ready")
    pt_filled = sem("b_pt_filled")
    pt_hi_ready = sem("b_pt_hi_ready")
    pt_lo_ready = sem("b_pt_lo_ready")
    heads_done = sem("b_heads_done")
    recip_ready = sem("b_recip_ready")
    o_ready = sem("b_o_ready")
    ot_filled = sem("b_ot_filled")
    ot_hi_ready = sem("b_ot_hi_ready")
    ot_lo_ready = sem("b_ot_lo_ready")
    out_filled = sem("b_out_filled")
    x1_ready = sem("b_x1_ready")
    h_ready = sem("b_h_ready")
    z2_ready = sem("b_z2_ready")
    xm_filled = sem("b_xm_filled")
    xf2_ready = sem("b_xf2_ready")
    xm_hi_ready = sem("b_xm_hi_ready")
    xm_ready = sem("b_xm_ready")
    logits_filled = sem("b_logits_filled")
    logits_out = sem("b_logits_out")
    top_ready = sem("b_top_ready")
    at_ready = sem("b_at_ready")
    gap_ready = sem("b_gap_ready")
    e2_ready = sem("b_e2_ready")
    den_ready = sem("b_den_ready")
    gate_ready = sem("b_gate_ready")
    marked = sem("b_marked")
    atf_ready = sem("b_atf_ready")
    picked_ready = sem("b_picked_ready")
    any_ready = sem("b_any_ready")
    count_filled = sem("b_count_filled")
    count_out = sem("b_count_out")
    place_ready = sem("b_place_ready")
    running_ready = sem("b_running_ready")
    slot_ready = sem("b_slot_ready")
    slot_now_ready = sem("b_slot_now_ready")
    queued = [sem(f"b_queued{u}") for u in range(2)]
    consts_ready = sem("b_consts_ready")

    def seq(s):
        return bass.ts(s, D)

    AHEAD = 2
    COUNTS = slice(2 * P + 2 * N_EXP, 2 * P + 4 * N_EXP)
    block = nc.Block()
    with block:
        @block.sync
        def _(sp):
            load_split(sp, loaded, stage, A["qk_dup_wT"], QK)
            load_split(sp, loaded, stage_v, A["L0_ffn_qkv_w"][:, 2 * D:3 * D], D)
            load_split(sp, loaded, stage_p, A["L0_ffn_proj_w"], D)
            load_split(sp, loaded, stage_g, A["L0_ffn_gate_w"], N_EXP)
            for r in (0, 32):
                sp.dma_start(stage_bias[r:r + 1, :], A["qk_dup_b"]).then_inc(loaded, 16)
                sp.dma_start(stage_bout[r:r + 1, :], A["L0_ffn_proj_b"]).then_inc(loaded, 16)
            with nc.allow_non_contiguous_dma(reason="columns of 192 numbers, once"):
                v_b = A["L0_ffn_qkv_b"][0, 2 * D:3 * D]
                sp.dma_start(bv_col[:, 0:1], v_b[0:P].unsqueeze(1)).then_inc(loaded, 16)
                sp.dma_start(bv_col[0:DB, 1:2], v_b[P:D].unsqueeze(1)).then_inc(loaded, 16)
                for tile, names in ((norm1, ("L0_ffn_ln1_g", "L0_ffn_ln1_b")), (norm2, ("L0_ffn_ln2_g", "L0_ffn_ln2_b"))):
                    for k, n in enumerate(names):
                        sp.dma_start(tile[:, k:k + 1], A[n][0, 0:P].unsqueeze(1)).then_inc(loaded, 16)
                        for r in (0, DB):
                            sp.dma_start(tile[r:r + DB, 2 + k:3 + k], A[n][0, P:D].unsqueeze(1)).then_inc(loaded, 16)
            sp.dma_start(sel[:], A["sel"]).then_inc(loaded, 16)
            sp.dma_start(expert_no[:], A["expert_no"].partition_broadcast(P)).then_inc(loaded, 16)
            sp.dma_start(token_rows[:], A["token_rows"]).then_inc(loaded, 16)
            sp.dma_start(route.running[:], A["queue_start"].partition_broadcast(P)).then_inc(loaded, 16)
            for e in range(2):
                staged.load(sp, A, e)
        LOADS = 16 * (12 + 4 + 2 + 12 + 4)

        @block.gpsimd
        def _(pool):
            def rsqrt(s, u, k):
                pool.wait_ge(ln_step[k], 3 * s + 3)
                nc.gpsimd.tensor_tensor(rstd[k][u][:], var_eps[k][u][:], half_pow[:], ALU.pow).then_inc(rstd_ready[k], 1)

            def add_x1(s, u):
                pool.wait_ge(x1_ready, s + 1)
                nc.gpsimd.tensor_tensor(h_all[:, seq(s)], h_all[:, seq(s)], y_all[:, seq(s)], ALU.add).then_inc(h_ready, 1)

            def gap_of(s, u):
                pool.wait_ge(top_ready, s + 1)
                wait(pool, e2_ready, s)
                nc.gpsimd.tensor_tensor(gap[:], top[:, 1:2], top[:, 0:1], ALU.subtract).then_inc(gap_ready, 1)

            def expert_numbers(s, u):
                waits_apart(pool, (loaded, LOADS), (at_ready, s + 1), (picked_ready, 2 * s))
                nc.gpsimd.tensor_copy(atf[:], at[:, 0:2]).then_inc(atf_ready, 1)

            def one_hot(s, u):
                waits_apart(pool, (loaded, LOADS), (atf_ready, s + 1), (slot_ready, 2 * s - 2), (queued[u], 16 * (s - u)))
                nc.gpsimd.tensor_copy(z2[u][:, 2 * P:2 * P + 1], token_rows[:, bass.ds(s, 1)]).then_inc(marked, 1)
                nc.gpsimd.tensor_copy(z2[u][:, 2 * P + 1:ROW], atf[:, 0:1]).then_inc(marked, 1)
                for k in range(2):
                    nc.gpsimd.tensor_scalar(picked[u][:, k, :], expert_no[:], atf[:, k:k + 1], None, ALU.is_equal
                                            ).then_inc(picked_ready, 1)

            def either(s, u):
                pool.wait_ge(picked_ready, 2 * s + 2)
                wait(pool, count_filled, s - 1)
                nc.gpsimd.tensor_tensor(picked_any[u][:], picked[u][:, 0, :], picked[u][:, 1, :], ALU.add).then_inc(any_ready, 1)

            def denominator(s, u):
                waits_apart(pool, (loaded, LOADS), (e2_ready, s + 1), (gate_ready, 2 * s))
                nc.gpsimd.tensor_scalar(den[:], e2[:], 1.0, None, ALU.add).then_inc(den_ready, 1)

            def first_gate(s, u):
                pool.wait_ge(den_ready, s + 1)
                nc.gpsimd.tensor_tensor(route.gates[:, bass.ds(2 * s, 1)], den[:], minus_one[:], ALU.pow).then_inc(gate_ready, 1)

            def second_gate(s, u):
                pool.wait_ge(gate_ready, 2 * s + 1)
                nc.gpsimd.tensor_tensor(route.gates[:, bass.ds(2 * s + 1, 1)], route.gates[:, bass.ds(2 * s, 1)], e2[:], ALU.mult
                                        ).then_inc(gate_ready, 1)

            def places(s, u):
                pool.wait_ge(count_out, s + 1)
                wait(pool, running_ready, s)
                wait(pool, slot_ready, 2 * s)
                nc.gpsimd.tensor_tensor(place[u][:], counted[u][:, 0, :], route.running[:], ALU.add).then_inc(place_ready, 1)
                pool.wait_ge(place_ready, s + 1)
                nc.gpsimd.tensor_tensor(route.running[:], route.running[:], counted[u][:, 1, :], ALU.add).then_inc(running_ready, 1)

            def enqueue(s, u):
                waits_apart(pool, (loaded, LOADS), (slot_ready, 2 * s + 2), (queued[u], 16 * (s - u)))
                nc.gpsimd.tensor_copy(slot_now[u][:], slot_f[u][:]).then_inc(slot_now_ready, 1)
                waits_apart(pool, (loaded, LOADS), (slot_now_ready, s + 1), (marked, 2 * s + 2))
                for k in range(2):
                    nc.gpsimd.indirect_dma_start(
                        out=route.x_queue, out_offset=bass.IndirectOffsetOnAxis(ap=slot_now[u][:, k:k + 1].bitcast(U32), axis=0),
                        in_=z2[u][:, :], in_offset=None).then_inc(queued[u], 16)

            nc.gpsimd.memset(minus_one[:], -1.0).then_inc(consts_ready, 1)
            nc.gpsimd.memset(all_ones[:], 1.0).then_inc(consts_ready, 1)
            pool.wait_ge(consts_ready, 2)
            nc.gpsimd.affine_select(out=before[:], in_=all_ones[:], compare_op=ALU.is_gt, fill=0.0, base=0,
                                    pattern=[[1, P]], channel_multiplier=-1).then_inc(consts_ready, 1)
            pool.wait_ge(loaded, LOADS)
            def turn(run):
                run(expert_numbers, 7)
                run(rsqrt, 6, 2)
                run(gap_of, 7)
                run(first_gate, 8)
                run(rsqrt, 0, 0)
                run(one_hot, 7)
                run(second_gate, 8)
                run(either, 7)
                run(add_x1, 7)
                run(rsqrt, 2, 1)
                run(places, 7)
                run(enqueue, 7)
                run(denominator, 7)

            pipeline(pool, n_seq, turn, AHEAD + 1)
            for u in range(2):
                pool.wait_ge(queued[u], 16 * n_seq)

        @block.scalar
        def _(act):
            def to_hi(dst, src):
                return nc.scalar.activation(dst, src, ACT.Copy, scale=W_SCALE)

            act.wait_ge(loaded, LOADS)
            for w, st in ((w_qk, stage), (w_v, stage_v), (w_p, stage_p), (w_g, stage_g)):
                to_hi(w.a_hi[:], st[:, 0, :]).then_inc(weights_ready, 1)
                to_hi(w.b_hi[:], st[:, 1, :]).then_inc(weights_ready, 1)
            to_hi(bqk_hi[0:1, :], stage_bias[0:1, :]).then_inc(weights_ready, 1)
            to_hi(bqk_hi[32:33, :], stage_bias[32:33, :]).then_inc(weights_ready, 1)

            def affine(dst, bank, norm, sems, first_wait):
                first_wait()
                for k in range(2):
                    nc.scalar.activation(dst[:, k * P:(k + 1) * P], bank[:, k * P:(k + 1) * P], ACT.Identity,
                                         bias=norm[:, 2 * k + 1:2 * k + 2], scale=norm[:, 2 * k:2 * k + 1]).then_inc(sems, 1)

            def xt_affine(s, u):
                act.wait_ge(xt_filled, s + 1)
                affine(xf[u], bank_w[0], norm1, xf_ready, lambda: wait(act, xt_ready, 2 * s - 2))

            def xt_high(s, u):
                act.wait_ge(xf_ready, 2 * s + 2)
                wait(act, qkv_filled, 3 * s - 3)
                nc.scalar.copy(xt_hi[u][:], xf[u][:]).then_inc(xt_hi_ready, 1)

            def qkv_high(s, u, j):
                act.wait_ge(qkv_filled, 3 * s + j + 1)
                w = bank_w[j % 2]
                if j == 0:
                    wait(act, qkv_lo, 3 * s - 2)
                    nc.scalar.copy(q_hi[:], w[:, 0:HALF]).then_inc(qkv_hi, 1)
                elif j == 1:
                    wait(act, scores_filled, 4 * s - 4)
                    nc.scalar.copy(k_hi[u][:], w[:, 0:HALF]).then_inc(qkv_hi, 1)
                else:
                    wait(act, heads_done, 4 * s - 4)
                    nc.scalar.copy(v_hi[u][:, :, 0:HD], w[:, 0:D].rearrange("p (h d) -> p h d", d=HD)).then_inc(qkv_hi, 1)

            def exps(t, u, g):
                act.wait_ge(neg_ready, 4 * t + g + 1)
                wait(act, pt_filled, 4 * t + g - 1)
                for e in range(GH):
                    nc.scalar.activation(prob[g % 2][:, e, :], bank_st[g][:, e * P:(e + 1) * P], ACT.Exp,
                                         bias=neg_max[g % 2][:, e:e + 1], scale=SCALE).then_inc(prob_ready, 1)

            def pt_high(t, u, g):
                act.wait_ge(pt_filled, 4 * t + g + 1)
                wait(act, heads_done, 4 * t + g - 1)
                nc.scalar.copy(pt_hi[g % 2][:], bank_st[g][:, 0:HALF]).then_inc(pt_hi_ready, 1)

            def ot_high(t, u):
                act.wait_ge(ot_filled, t + 1)
                wait(act, out_filled, t)
                nc.scalar.copy(ot_hi[:], bank_e[:, 0:2 * P]).then_inc(ot_hi_ready, 1)

            def xm_affine(t, u):
                act.wait_ge(xm_filled, t + 1)
                affine(xf2, bank_w[1], norm2, xf2_ready, lambda: wait(act, xm_ready, 2 * t))

            def xm_high(t, u):
                act.wait_ge(xf2_ready, 2 * t + 2)
                wait(act, logits_filled, t)
                nc.scalar.copy(xm_hi[:], xf2[:]).then_inc(xm_hi_ready, 1)

            def second_exp(t, u):
                act.wait_ge(gap_ready, t + 1)
                wait(act, gate_ready, 2 * t)
                nc.scalar.activation(e2[:], gap[:], ACT.Exp).then_inc(e2_ready, 1)

            def turn(run):
                run(pt_high, 3, 3)
                run(xm_affine, 4)
                run(xm_high, 4)
                run(exps, 2, 0)
                run(exps, 2, 1)
                run(second_exp, 5)
                run(pt_high, 2, 0)
                run(ot_high, 3)
                run(qkv_high, 1, 0)
                run(exps, 2, 2)
                run(qkv_high, 1, 1)
                run(pt_high, 2, 1)
                run(qkv_high, 1, 2)
                run(exps, 2, 3)
                run(pt_high, 2, 2)
                run(xt_affine, 0)
                run(xt_high, 0)

            pipeline(act, n_seq, turn, AHEAD + 1)

        @block.vector
        def _(dve):
            def to_lo(dst, src, hi):
                return nc.vector.scalar_tensor_tensor(dst, src, W_SCALE, hi, ALU.mult, ALU.subtract)

            nc.vector.memset(bias_qk[:], 0.0).then_inc(split_step, 1)
            nc.vector.memset(bias_out[:], 0.0).then_inc(split_step, 1)
            for u in range(2):
                nc.vector.memset(v_hi[u][:, :, HD:VW], 1.0).then_inc(split_step, 1)
            dve.wait_ge(weights_ready, 10)
            for w, st in ((w_qk, stage), (w_v, stage_v), (w_p, stage_p), (w_g, stage_g)):
                to_lo(w.a_lo[:], st[:, 0, :], w.a_hi[:]).then_inc(split_step, 1)
                to_lo(w.b_lo[:], st[:, 1, :], w.b_hi[:]).then_inc(split_step, 1)
            dve.wait_ge(split_step, 2)
            nc.vector.tensor_copy(bias_qk[0:1, :], bqk_hi[0:1, :]).then_inc(split_step, 1)
            to_lo(bias_qk[32:33, :], stage_bias[32:33, :], bqk_hi[32:33, :]).then_inc(split_step, 1)
            dve.wait_ge(bias_sum, 1)
            for r in (0, 32):
                nc.vector.tensor_tensor(stage_bout[r:r + 1, :], bank_e[r:r + 1, 0:D], stage_bout[r:r + 1, :], ALU.add
                                        ).then_inc(split_step, 1)
            dve.wait_ge(split_step, 16)
            for r in (0, 32):
                nc.vector.tensor_scalar(bout_hi[r:r + 1, :], stage_bout[r:r + 1, :], W_SCALE * W_SCALE, None, ALU.mult
                                        ).then_inc(split_step, 1)
            dve.wait_ge(split_step, 18)
            nc.vector.tensor_copy(bias_out[0:1, :], bout_hi[0:1, :]).then_inc(split_step, 1)
            nc.vector.scalar_tensor_tensor(bias_out[32:33, :], stage_bout[32:33, :], W_SCALE * W_SCALE, bout_hi[32:33, :],
                                           ALU.mult, ALU.subtract).then_inc(split_step, 1)
            dve.wait_ge(split_step, 20)

            def ln_stats(k, s, u, src, *waits):
                waits_apart(dve, (loaded, LOADS), *waits)
                nc.vector.bn_stats(stats[k][u][:], src).then_inc(ln_step[k], 1)

            def ln_mean(s, u, k):
                used = ((y_ready, s - 1), (z_ready, 2 * s - 2), (z2_ready, 2 * s - 2))[k]
                waits_apart(dve, (loaded, LOADS), (ln_step[k], 3 * s + 1), used)
                nc.vector.bn_aggr(moments[k][u][:], stats[k][u][:]).then_inc(ln_step[k], 1)

            def ln_variance(s, u, k):
                dve.wait_ge(ln_step[k], 3 * s + 2)
                nc.vector.tensor_scalar(var_eps[k][u][:], moments[k][u][:, 1:2], LN_EPS, None, ALU.add).then_inc(ln_step[k], 1)

            def ln_h(s, u):
                ln_stats(0, s, u, h_all[:, seq(s)])

            def make_y(s, u):
                dve.wait_ge(rstd_ready[0], s + 1)
                nc.vector.tensor_scalar(y_all[:, seq(s)], h_all[:, seq(s)], moments[0][u][:, 0:1], rstd[0][u][:, 0:1],
                                        ALU.subtract, ALU.mult).then_inc(y_ready, 1)

            def ln_y(s, u):
                ln_stats(1, s, u, y_all[:, seq(s)], (y_ready, s + 1))

            def make_z(s, u):
                dve.wait_ge(rstd_ready[1], s + 1)
                wait(dve, xt_filled, s - 1)
                for dst, src in ((z[u][:, 0:D], y_all[:, seq(s)]), (z[u][:, D:2 * P], y_all[:, bass.ds(s * D + P, DB)])):
                    nc.vector.tensor_scalar(dst, src, moments[1][u][:, 0:1], rstd[1][u][:, 0:1],
                                            ALU.subtract, ALU.mult).then_inc(z_ready, 1)

            def low_parts(alo, b, hi, full, sems):
                nc.vector.tensor_tensor(alo, full[:, 0:P], hi[:, 0:P], ALU.subtract).then_inc(sems, 1)
                nc.vector.scalar_tensor_tensor(b, hi[:, P:2 * P], sel[:, 0:1], full[:, P:2 * P], ALU.mult, ALU.add
                                               ).then_inc(sems, 1)

            def xt_low(s, u):
                dve.wait_ge(xt_hi_ready, s + 1)
                low_parts(xt_alo[u][:], xt_b[u][:], xt_hi[u], xf[u], xt_ready)

            def qkv_low(s, u, j):
                dve.wait_ge(qkv_hi, 3 * s + j + 1)
                w = bank_w[j % 2]
                if j == 0:
                    wait(dve, scores_filled, 4 * s - 4)
                    nc.vector.scalar_tensor_tensor(q_st[u][:], q_hi[:], sel[:, 1:2], w[:, 0:HALF], ALU.mult, ALU.add
                                                   ).then_inc(qkv_lo, 1)
                elif j == 1:
                    nc.vector.tensor_tensor(k_lo[u][:], w[:, 0:HALF], k_hi[u][:], ALU.subtract).then_inc(qkv_lo, 1)
                else:
                    nc.vector.tensor_tensor(v_lo[u][:], w[:, 0:D].rearrange("p (h d) -> p h d", d=HD), v_hi[u][:, :, 0:HD],
                                            ALU.subtract).then_inc(qkv_lo, 1)

            def maxima(t, u, g):
                dve.wait_ge(scores_filled, 4 * t + g + 1)
                wait(dve, neg_ready, 4 * t + g - 1)
                nc.vector.tensor_reduce(row_max[g % 2][:], bank_st[g][:, 0:HALF].rearrange("p (e k) -> p e k", k=P), AX, ALU.max
                                        ).then_inc(max_ready, 1)

            def neg_maxima(t, u, g):
                dve.wait_ge(max_ready, 4 * t + g + 1)
                wait(dve, prob_ready, 3 * (4 * t + g - 1))
                nc.vector.tensor_scalar(neg_max[g % 2][:], row_max[g % 2][:], -SCALE, None, ALU.mult).then_inc(neg_ready, 1)

            def pt_low(t, u, g):
                dve.wait_ge(pt_hi_ready, 4 * t + g + 1)
                nc.vector.tensor_tensor(pt_lo[g % 2][:], bank_st[g][:, 0:HALF], pt_hi[g % 2][:], ALU.subtract).then_inc(pt_lo_ready, 1)

            o_view = bank_o[:, 0:HEADS * VW].rearrange("p (h d) -> p h d", d=VW)

            def row_sums(t, u):
                dve.wait_ge(heads_done, 4 * t + 4)
                wait(dve, o_ready, 2 * t)
                nc.vector.reciprocal(recip[:], o_view[:, :, HD]).then_inc(recip_ready, 1)

            def normalise(t, u):
                dve.wait_ge(recip_ready, t + 1)
                wait(dve, ot_filled, t)
                for dst, src in ((slice(0, HEADS), slice(0, HEADS)), (slice(HEADS, HEADS + 4), slice(8, HEADS))):
                    n_heads = src.stop - src.start
                    nc.vector.tensor_tensor(o_norm[:, dst, :], o_view[:, src, 0:HD],
                                            recip[:, src].unsqueeze(2).to_broadcast([P, n_heads, HD]), ALU.mult).then_inc(o_ready, 1)

            def ot_low(t, u):
                dve.wait_ge(ot_hi_ready, t + 1)
                low_parts(ot_alo[:], ot_b[:], ot_hi, bank_e, ot_lo_ready)

            def make_x1(t, u):
                dve.wait_ge(out_filled, t + 1)
                nc.vector.scalar_tensor_tensor(y_all[:, seq(t)], bank_e[:, 0:D], 1.0 / (W_SCALE * W_SCALE), y_all[:, seq(t)],
                                               ALU.mult, ALU.add).then_inc(x1_ready, 1)

            def ln_x1(t, u):
                ln_stats(2, t, u, y_all[:, seq(t)], (x1_ready, t + 1))

            def make_z2(t, u):
                dve.wait_ge(rstd_ready[2], t + 1)
                wait(dve, queued[u], 16 * (t - u))
                for dst, src in ((z2[u][:, 0:D], y_all[:, seq(t)]), (z2[u][:, D:2 * P], y_all[:, bass.ds(t * D + P, DB)])):
                    nc.vector.tensor_scalar(dst, src, moments[2][u][:, 0:1], rstd[2][u][:, 0:1],
                                            ALU.subtract, ALU.mult).then_inc(z2_ready, 1)

            def xm_low(t, u):
                dve.wait_ge(xm_hi_ready, t + 1)
                wait(dve, logits_filled, t)
                low_parts(xm_alo[:], xm_b[:], xm_hi, xf2, xm_ready)

            def take_logits(t, u):
                dve.wait_ge(logits_filled, t + 1)
                wait(dve, at_ready, t)
                nc.vector.tensor_scalar(logits[:], bank_w[1][:, 2 * P:2 * P + N_EXP], 1.0 / W_SCALE, None, ALU.mult).then_inc(logits_out, 1)

            def largest(t, u):
                waits_apart(dve, (loaded, LOADS), (logits_out, t + 1), (gap_ready, t))
                nc.vector.max(top[:], logits[:]).then_inc(top_ready, 1)

            def largest_at(t, u):
                waits_apart(dve, (loaded, LOADS), (top_ready, t + 1), (atf_ready, t))
                nc.vector.max_index(at[:], top[:], logits[:]).then_inc(at_ready, 1)

            def counts(t, u):
                dve.wait_ge(count_filled, t + 1)
                wait(dve, running_ready, t)
                nc.vector.tensor_copy(counted[u][:].rearrange("p a e -> p (a e)"), bank_w[1][:, COUNTS]).then_inc(count_out, 1)

            def slots(t, u):
                dve.wait_ge(place_ready, t + 1)
                wait(dve, slot_now_ready, t)
                for k in range(2):
                    wait(dve, slot_ready, 2 * t + k)
                    nc.vector.tensor_tensor_reduce(picked_place[:], picked[u][:, k, :], place[u][:], 1.0, 0.0, ALU.mult, ALU.add,
                                                   slot_f[u][:, k:k + 1]).then_inc(slot_ready, 1)

            def turn(run):
                run(maxima, 6, 0)
                run(pt_low, 7, 2)
                run(make_z2, 8)
                run(ln_y, 3)
                run(neg_maxima, 6, 0)
                run(make_y, 2)
                run(xt_low, 5)
                run(pt_low, 7, 3)
                run(ln_h, 0)
                run(maxima, 6, 1)
                run(xm_low, 8)
                run(neg_maxima, 6, 1)
                run(maxima, 6, 2)
                run(row_sums, 7)
                run(take_logits, 8)
                run(normalise, 7)
                run(counts, 9)
                run(ln_mean, 3, 1)
                run(make_z, 4)
                run(ln_mean, 0, 0)
                run(largest, 8)
                run(neg_maxima, 6, 2)
                run(slots, 9)
                run(ln_variance, 3, 1)
                run(maxima, 6, 3)
                run(ot_low, 7)
                run(qkv_low, 5, 0)
                run(pt_low, 6, 0)
                run(largest_at, 8)
                run(neg_maxima, 6, 3)
                run(make_x1, 7)
                run(qkv_low, 5, 1)
                run(ln_x1, 7)
                run(qkv_low, 5, 2)
                run(ln_mean, 7, 2)
                run(pt_low, 6, 1)
                run(ln_variance, 0, 0)
                run(ln_variance, 7, 2)

            pipeline(dve, n_seq, turn, AHEAD + 1)

        @block.tensor
        def _(pe):
            def mm(dst, lhsT, rhs, start, stop):
                return nc.tensor.matmul(dst, lhsT, rhs, start=start, stop=stop)

            pe.wait_ge(loaded, LOADS)
            for r in (0, 32):
                mm(bank_e[r:r + 1, 0:D], bv_col[:, 0:1], stage_p[:, 0, :], True, False)
                last = mm(bank_e[r:r + 1, 0:D], bv_col[0:DB, 1:2], stage_p[0:DB, 1, :], False, True)
            last.then_inc(bias_sum, 1)
            pe.wait_ge(split_step, 20)

            def transpose_x(bank, src):
                nc.tensor.transpose(bank[:, 0:P], src[:, 0:P], ident[:])
                return nc.tensor.transpose(bank[:, P:2 * P], src[:, P:2 * P], ident[:])

            def transpose_z(s, u):
                pe.wait_ge(z_ready, 2 * s + 2)
                wait(pe, qkv_lo, 3 * s)
                transpose_x(bank_w[0], z[u]).then_inc(xt_filled, 1)

            def project(s, u, j):
                w = bank_w[j % 2]
                if j == 0:
                    pe.wait_ge(xt_ready, 2 * s + 2)
                elif j == 1:
                    wait(pe, qkv_lo, 3 * s - 1)
                    wait(pe, logits_out, s - AHEAD)
                    wait(pe, count_out, s - AHEAD - 1)
                else:
                    pe.wait_ge(qkv_lo, 3 * s + 1)
                parts = (xt_hi[u][:, 0:P], xt_alo[u][:], xt_b[u][:])
                if j < 2:
                    for c in range(CH):
                        col = slice((CH * j + c) * P, (CH * j + c + 1) * P)
                        dst = w[:, c * P:(c + 1) * P]
                        for k, (x_part, w_part) in enumerate(w_qk.passes(*parts, col)):
                            mm(dst, w_part, x_part, k == 0, False)
                        last = mm(dst, bias_qk[:, col], ones_rows[:], False, True)
                else:
                    for k, (x_part, w_part) in enumerate(w_v.passes(*parts, slice(0, D))):
                        last = mm(w[:, 0:D], x_part, w_part, k == 0, k == 4)
                last.then_inc(qkv_filled, 1)

            def scores(t, u, g):
                if g == 0:
                    pe.wait_ge(qkv_lo, 3 * t + 2)
                wait(pe, pt_lo_ready, 4 * t + g - 3)
                r = slice(32 * g, 32 * g + 32)
                for c in range(GH):
                    col = slice(c * P, (c + 1) * P)
                    mm(bank_st[g][:, col], q_st[u][r, col], k_hi[u][r, col], True, False)
                    last = mm(bank_st[g][:, col], q_st[u][r, col], k_lo[u][r, col], False, True)
                last.then_inc(scores_filled, 1)

            def transpose_prob(t, u, g):
                pe.wait_ge(prob_ready, 3 * (4 * t + g) + 3)
                for e in range(GH):
                    last = nc.tensor.transpose(bank_st[g][:, e * P:(e + 1) * P], prob[g % 2][:, e, :], ident[:])
                last.then_inc(pt_filled, 1)

            def weigh_values(t, u, g):
                pe.wait_ge(pt_lo_ready, 4 * t + g + 1)
                if g == 0:
                    pe.wait_ge(qkv_lo, 3 * t + 3)
                    wait(pe, o_ready, 2 * t)
                for e in range(GH):
                    h = 4 * e + g
                    o = bank_o[:, h * VW:(h + 1) * VW]
                    col = slice(e * P, (e + 1) * P)
                    mm(o, pt_hi[g % 2][:, col], v_hi[u][:, h, :], True, False)
                    mm(o, pt_lo[g % 2][:, col], v_hi[u][:, h, :], False, False)
                    last = mm(o[:, 0:HD], pt_hi[g % 2][:, col], v_lo[u][:, h, :], False, True)
                last.then_inc(heads_done, 1)

            def transpose_o(t, u):
                pe.wait_ge(o_ready, 2 * t + 2)
                wait(pe, x1_ready, t)
                transpose_x(bank_e, o_norm[:].rearrange("p h d -> p (h d)")).then_inc(ot_filled, 1)

            def project_out(t, u):
                pe.wait_ge(ot_lo_ready, 2 * t + 2)
                for k, (o_part, w_part) in enumerate(w_p.passes(ot_hi[:, 0:P], ot_alo[:], ot_b[:], slice(0, D))):
                    mm(bank_e[:, 0:D], o_part, w_part, k == 0, False)
                mm(bank_e[:, 0:D], ones_rows[:], bias_out[:], False, True).then_inc(out_filled, 1)

            def transpose_z2(t, u):
                pe.wait_ge(z2_ready, 2 * t + 2)
                pe.wait_ge(qkv_lo, 3 * (n_seq - 1) + 2 if isinstance(t, int) and t + AHEAD >= n_seq else 3 * (t + AHEAD) + 2)
                wait(pe, logits_out, t)
                wait(pe, count_out, t - 1)
                transpose_x(bank_w[1], z2[u]).then_inc(xm_filled, 1)

            def gate_logits(t, u):
                pe.wait_ge(xm_ready, 2 * t + 2)
                for k, (x_part, w_part) in enumerate(w_g.passes(xm_hi[:, 0:P], xm_alo[:], xm_b[:], slice(0, N_EXP))):
                    last = mm(bank_w[1][:, 2 * P:2 * P + N_EXP], x_part, w_part, k == 0, k == 4)
                last.then_inc(logits_filled, 1)

            def count(t, u):
                pe.wait_ge(any_ready, t + 1)
                pe.wait_ge(logits_out, n_seq if isinstance(t, int) and t == n_seq - 1 else t + 2)
                wait(pe, count_out, t)
                at = COUNTS.start
                mm(bank_w[1][:, at:at + N_EXP], before[:], picked_any[u][:], True, True)
                mm(bank_w[1][:, at + N_EXP:at + 2 * N_EXP], all_ones[:], picked_any[u][:], True, True).then_inc(count_filled, 1)

            pe.wait_ge(consts_ready, 3)
            def turn(run):
                run(transpose_prob, 2, 2)
                run(scores, 1, 0)
                run(transpose_z, 0)
                run(transpose_prob, 2, 3)
                run(weigh_values, 2, 1)
                run(scores, 1, 1)
                run(transpose_z2, 3)
                run(weigh_values, 2, 2)
                run(scores, 1, 2)
                run(project, 0, 0)
                run(weigh_values, 2, 3)
                run(gate_logits, 3)
                run(transpose_prob, 1, 0)
                run(count, 4)
                run(scores, 1, 3)
                run(transpose_o, 2)
                run(project, 0, 1)
                run(transpose_prob, 1, 1)
                run(project_out, 2)
                run(project, 0, 2)
                run(weigh_values, 1, 0)

            pipeline(pe, n_seq, turn, AHEAD + 1)


class Route:

    def __init__(self, nc, sb, n_seq):
        self.tokens = n_seq * P
        self.stride = self.tokens + TILE
        self.x_queue = nc.dram_tensor("x_queue", [N_EXP * self.stride, ROW], F32, kind="Internal").ap()
        self.gates = sb("route_gates", [P, 2 * n_seq], F32)
        self.running = sb("route_running", [P, N_EXP], F32)
        self.tiles = 2 * self.tokens // TILE + N_EXP
        self.y_tokens = nc.dram_tensor("y_tokens", [2 * TILE + 2 * self.tokens, D], F32, kind="Internal").ap()


class Staged:

    def __init__(self, sb, sem):
        self.w1 = [sb(f"staged_w1_{u}", [P, 2, HID], F32) for u in range(2)]
        self.w2 = [sb(f"staged_w2_{u}", [P, HC, D], F32) for u in range(2)]
        self.loaded = [sem(f"staged_loaded{u}") for u in range(2)]

    def load(self, eng, A, e):
        u = e % 2
        load_split(eng, self.loaded[u], self.w1[u], A["L0_ffn_w1"][e], HID)
        eng.dma_start(self.w2[u][:], A["L0_ffn_w2"][e].rearrange("(c p) d -> p c d", p=P)).then_inc(self.loaded[u], 16)


def experts(nc, A, h_all, ident, ones_rows, psum, route, staged, sb, sem, n_seq):
    NT = route.tiles
    A2 = TILE // P
    w1 = Split(sb, "w1", N_EXP * HID)
    w2_hi = sb("w2_hi", [P, N_EXP * HC, D], F16)
    w2_lo = sb("w2_lo", [P, N_EXP * HC, D], F16)
    b1 = sb("b1", [P, N_EXP * HC], F32)
    bias2 = sb("bias2", [P, N_EXP, D], F16)
    stage_b2 = sb("stage_b2", [33, N_EXP, D], F32)
    b2_hi = sb("b2_hi", [33, N_EXP, D], F16)
    norm2 = sb("norm2", [P, 4], F32)
    zeros = sb("zeros", [P, A2, ROW], F32)
    consts = sb("consts", [P, 2, N_EXP], F32)
    tile_no = sb("tile_no", [P, NT], F32)
    filled = sb("filled", [P, N_EXP], F32)
    filled_i = sb("filled_i", [P, N_EXP], I32)
    end_i = sb("end_i", [P, N_EXP], I32)
    tiles_i = sb("tiles_i", [P, N_EXP], I32)
    tiles = sb("tiles", [P, N_EXP], F32)
    upto = [sb(f"upto{k}", [P, N_EXP], F32) for k in range(4)]
    first = sb("first", [P, N_EXP], F32)
    last_row = sb("last_row", [P, N_EXP], F32)
    t_a = sb("t_a", [P, NT, N_EXP], F32)
    t_b = sb("t_b", [1, NT, N_EXP], F32)
    t_q = sb("t_q", [1, NT, N_EXP], F32)
    t_e = sb("t_e", [P, NT], F32)
    is_first = sb("is_first", [P, A2], F32)
    expert_now = sb("expert_now", [P, 1], F32)
    dest_f = sb("dest_f", [P, A2], F32)
    dest_all = sb("dest_all", [P, A2 * NT], I32)
    dest_now = [sb(f"dest_now{u}", [P, A2], I32) for u in range(2)]
    t_r = sb("t_r", [1, NT], F32)
    tile_expert = sb("tile_expert", [1, NT], I32)
    tile_row = sb("tile_row", [1, NT], I32)
    t_c = sb("t_c", [1, NT, N_EXP], F32)

    def pair(name, shape, dt):
        return [sb(f"{name}{u}", shape, dt) for u in range(2)]

    x_rows = pair("x_rows", [P, A2, ROW], F32)
    xf = sb("c_xf", [P, 2, TILE], F32)
    x_hi = pair("c_x_hi", [P, 2, TILE], F16)
    x_alo = pair("c_x_alo", [P, TILE], F16)
    x_b = pair("c_x_b", [P, TILE], F16)
    sel = sb("c_sel", [P, 2], F32)
    DEPTH = 3
    hf, h_hi, h_lo = ([sb(f"{n}{u}", [P, TILE], dt) for u in range(DEPTH)]
                      for n, dt in (("hf", F32), ("h_hi", F16), ("h_lo", F16)))
    y_out = pair("y_out", [P, A2, D], F32)
    bank_x, bank_h, bank_y = psum[0:2], psum[2:2 + DEPTH], psum[6:8]

    loaded = sem("c_loaded")
    hi_ready = sem("c_hi_ready")
    split_ready = sem("c_split_ready")
    zeroed = sem("c_zeroed")
    table_step = sem("c_table_step")
    padded = sem("c_padded")
    marks_loaded = sem("c_marks_loaded")
    dest_step = sem("c_dest_step")
    dest_at_hand = sem("c_dest_at_hand")
    x_loaded = [sem(f"c_x_loaded{u}") for u in range(2)]
    x_filled = sem("c_x_filled")
    xf_ready = sem("c_xf_ready")
    x_hi_ready = sem("c_x_hi_ready")
    x_ready = sem("c_x_ready")
    h_filled = sem("c_h_filled")
    gelu_ready = sem("c_gelu_ready")
    h_hi_ready = sem("c_h_hi_ready")
    h_lo_ready = sem("c_h_lo_ready")
    chunk_used = sem("c_chunk_used")
    y_ready = sem("c_y_ready")
    y_stored = [sem(f"c_y_stored{u}") for u in range(2)]

    block = nc.Block()
    with block:
        @block.sync
        def _(sp):
            sp.dma_start(sel[:], A["sel"]).then_inc(loaded, 16)
            sp.dma_start(consts[:, 0, :], A["expert_no"].partition_broadcast(P)).then_inc(loaded, 16)
            sp.dma_start(consts[:, 1, :], A["queue_start"].partition_broadcast(P)).then_inc(loaded, 16)
            sp.dma_start(tile_no[:], A["tile_no"].partition_broadcast(P)).then_inc(loaded, 16)
            with nc.allow_non_contiguous_dma(reason="bias columns, once"):
                sp.dma_start(b1[:], A["L0_ffn_b1"].rearrange("e (c p) -> p (e c)", p=P)).then_inc(loaded, 16)
                for k, n in enumerate(("L0_ffn_ln2_g", "L0_ffn_ln2_b")):
                    sp.dma_start(norm2[:, k:k + 1], A[n][0, 0:P].unsqueeze(1)).then_inc(loaded, 16)
                    for r in (0, DB):
                        sp.dma_start(norm2[r:r + DB, 2 + k:3 + k], A[n][0, P:D].unsqueeze(1)).then_inc(loaded, 16)
            for r in (0, 32):
                sp.dma_start(stage_b2[r:r + 1, :, :], A["L0_ffn_b2"].unsqueeze(0)).then_inc(loaded, 16)
            sp.wait_ge(table_step, 1)
            sp.wait_ge(zeroed, 2)
            with nc.allow_non_contiguous_dma(reason="marks, once"):
                sp.dma_start(zeros[:, :, 2 * P:2 * P + 1], A["rest_rows"].unsqueeze(2)).then_inc(marks_loaded, 16)
            sp.wait_ge(marks_loaded, 16)
            for e in range(N_EXP):
                end = sp.value_load(end_i[0:1, e:e + 1], min_val=0, max_val=N_EXP * route.stride - TILE)
                sp.dma_start(route.x_queue[bass.ds(end, TILE), :].rearrange("(a p) d -> p a d", p=P), zeros[:]).then_inc(padded, 16)

            for e in range(2, N_EXP):
                sp.wait_ge(split_ready, 2 + 3 * (e - 1))
                staged.load(sp, A, e)
        LOADS = 16 * 13

        @block.gpsimd
        def _(pool):
            nc.gpsimd.memset(zeros[:], 0.0).then_inc(zeroed, 1)
            pool.wait_ge(table_step, 2)
            pool.wait_ge(padded, 16 * N_EXP)

            def load(j, u):
                wait(pool, x_filled, j - 1)
                wait(pool, dest_step, 4 * (j - 1))
                row = pool.value_load(tile_row[0:1, bass.ds(j, 1)], min_val=0, max_val=N_EXP * route.stride - TILE)
                pool.dma_start(x_rows[u][:], route.x_queue[bass.ds(row, TILE), :].rearrange("(a p) d -> p a d", p=P)
                               ).then_inc(x_loaded[u], 16)

            def destinations(j, u):
                waits_apart(pool, (zeroed, 2), (dest_step, 4 * j))
                nc.gpsimd.tensor_copy(expert_now[:], t_e[:, bass.ds(j, 1)]).then_inc(dest_step, 1)
                waits_apart(pool, (zeroed, 2), (dest_step, 4 * j + 1), (x_loaded[u], 8 * (j - u) + 16))
                nc.gpsimd.tensor_scalar(is_first[:], x_rows[u][:, :, 2 * P + 1], expert_now[:, 0:1], None, ALU.is_equal
                                        ).then_inc(dest_step, 1)
                pool.wait_ge(dest_step, 4 * j + 2)
                nc.gpsimd.tensor_tensor(dest_f[:], x_rows[u][:, :, 2 * P], is_first[:], ALU.add).then_inc(dest_step, 1)
                waits_apart(pool, (zeroed, 2), (dest_step, 4 * j + 3))
                nc.gpsimd.tensor_copy(dest_all[:, bass.ds(A2 * j, A2)], dest_f[:]).then_inc(dest_step, 1)

            def scatter(j, u):
                waits_apart(pool, (zeroed, 2), (dest_step, 4 * j + 4), (y_stored[u], 16 * (j - u)),
                            (y_stored[1 - u], 16 * (j + u)))
                nc.gpsimd.tensor_copy(dest_now[u][:], dest_all[:, bass.ds(A2 * j, A2)]).then_inc(dest_at_hand, 1)
                waits_apart(pool, (zeroed, 2), (dest_at_hand, j + 1), (y_ready, j + 1))
                for a in range(A2):
                    nc.gpsimd.indirect_dma_start(
                        out=route.y_tokens, out_offset=bass.IndirectOffsetOnAxis(ap=dest_now[u][:, a:a + 1].bitcast(U32), axis=0),
                        in_=y_out[u][:, a, :], in_offset=None).then_inc(y_stored[u], 16)

            def turn(run):
                run(load, 0)
                run(scatter, 4)
                run(destinations, 1)

            pipeline(pool, NT, turn)

            for u in range(2):
                pool.wait_ge(y_stored[u], 16 * NT)

        @block.scalar
        def _(act):
            act.wait_ge(loaded, LOADS)
            for r in (0, 32):
                nc.scalar.activation(b2_hi[r:r + 1, :, :], stage_b2[r:r + 1, :, :], ACT.Copy, scale=W_SCALE).then_inc(hi_ready, 1)
            act.wait_ge(table_step, 2)

            expert_reg, expert = [act.alloc_register(f"expert{u}") for u in range(2)], {}

            def load_expert(j, u):
                act.reg_load(expert_reg[u], tile_expert[0:1, bass.ds(j, 1)])
                recall_expert(j, u)

            def recall_expert(j, u):
                expert[u] = act.snap(expert_reg[u], min_val=0, max_val=N_EXP - 1)

            def split_high(e, u):
                if isinstance(e, int) and e < N_EXP:
                    act.wait_ge(staged.loaded[u], 64 * (e // 2) + 64)
                    c = slice(e * HID, (e + 1) * HID)
                    for dst, src in ((w1.a_hi[:, c], staged.w1[u][:, 0, :]), (w1.b_hi[:, c], staged.w1[u][:, 1, :]),
                                     (w2_hi[:, e * HC:(e + 1) * HC, :], staged.w2[u][:])):
                        nc.scalar.activation(dst, src, ACT.Copy, scale=W_SCALE).then_inc(hi_ready, 1)

            def x_affine(j, u, k):
                act.wait_ge(x_filled, j + 1)
                wait(act, x_ready, 2 * j)
                nc.scalar.activation(xf[:, k, :], bank_x[u][:, k * TILE:(k + 1) * TILE], ACT.Identity,
                                     bias=norm2[:, 2 * k + 1:2 * k + 2], scale=norm2[:, 2 * k:2 * k + 1]).then_inc(xf_ready, 1)

            def x_high(j, u):
                act.wait_ge(xf_ready, 2 * j + 2)
                wait(act, h_filled, HC * (j - 1))
                nc.scalar.copy(x_hi[u][:], xf[:]).then_inc(x_hi_ready, 1)

            def gelu(j, u, c):
                k = j * HC + c
                act.wait_ge(h_filled, k + 1)
                wait(act, h_lo_ready, k - DEPTH + 1)
                nc.scalar.activation(hf[c % DEPTH][:], bank_h[c % DEPTH][:, 0:TILE], ACT.Gelu, bias=b1[:, bass.ds(expert[u] * HC + c, 1)],
                                     scale=1.0 / W_SCALE).then_inc(gelu_ready, 1)

            def turn(run):
                run(split_high, 0)
                run(recall_expert, 2)
                run(load_expert, 1)
                run(x_high, 1)
                run(gelu, 2, 4)
                run(gelu, 2, 5)
                run(gelu, 1, 0)
                run(gelu, 1, 1)
                run(gelu, 1, 2)
                run(x_affine, 0, 0)
                run(x_affine, 0, 1)
                run(gelu, 1, 3)

            pipeline(act, NT, turn, N_EXP)

        @block.vector
        def _(dve):
            n = 0
            ops = [
                lambda: nc.vector.tensor_tensor(filled[:], route.running[:], consts[:, 1, :], ALU.subtract),
                lambda: nc.vector.tensor_scalar(filled[:], filled[:], float(TILE - 1), None, ALU.add),
                lambda: nc.vector.tensor_copy(filled_i[:], filled[:]),
                lambda: nc.vector.tensor_scalar(tiles_i[:], filled_i[:], TILE.bit_length() - 1, None, ALU.logical_shift_right),
                lambda: nc.vector.tensor_copy(tiles[:], tiles_i[:]),
                lambda: nc.vector.tensor_scalar(upto[0][:], tiles[:], 1.0, None, ALU.max),
                lambda: nc.vector.tensor_copy(tiles[:], upto[0][:]),
            ]
            for k in range(3):
                ops.append(lambda k=k: nc.vector.tensor_copy(upto[k + 1][:], upto[k][:]))
                ops.append(lambda k=k: nc.vector.tensor_tensor(upto[k + 1][:, 1 << k:N_EXP], upto[k][:, 1 << k:N_EXP],
                                                               upto[k][:, 0:N_EXP - (1 << k)], ALU.add))
            whole = [1, NT, N_EXP]
            j_of = tile_no[0:1].unsqueeze(2).to_broadcast(whole)
            all_rows = [P, NT, N_EXP]

            def per_queue(t):
                return t[0:1].unsqueeze(1).to_broadcast(whole)
            ops += [
                lambda: nc.vector.tensor_tensor(first[:], upto[3][:], tiles[:], ALU.subtract),
                lambda: nc.vector.tensor_tensor(t_a[:], tile_no[:].unsqueeze(2).to_broadcast(all_rows),
                                                upto[3][:].unsqueeze(1).to_broadcast(all_rows), ALU.is_ge),
                lambda: nc.vector.tensor_reduce(t_e[:], t_a[:], AX, ALU.add),
                lambda: nc.vector.tensor_scalar(t_e[:], t_e[:], float(N_EXP - 1), None, ALU.min),
                lambda: nc.vector.tensor_tensor(t_a[0:1], j_of, per_queue(first[:]), ALU.subtract),
                lambda: nc.vector.tensor_scalar(last_row[:], tiles[:], -1.0, None, ALU.add),
            ]
            def rows_of(number, dst):
                return [
                    lambda: nc.vector.tensor_scalar(t_c[:], number[:], float(TILE), None, ALU.mult),
                    lambda: nc.vector.tensor_tensor(t_c[:], t_c[:], per_queue(consts[:, 1, :]), ALU.add),
                    lambda: nc.vector.tensor_tensor(t_c[:], t_c[:], t_q[:], ALU.mult),
                    lambda: nc.vector.tensor_reduce(t_r[:], t_c[:], AX, ALU.add),
                    lambda: nc.vector.tensor_copy(dst[:], t_r[:]),
                ]
            ops += [lambda: nc.vector.tensor_tensor(t_q[:], per_queue(consts[:, 0, :]), t_e[0:1].unsqueeze(2).to_broadcast(whole), ALU.is_equal)]
            ops += [lambda: nc.vector.tensor_tensor(t_b[:], t_a[0:1], per_queue(last_row[:]), ALU.min)]
            ops += rows_of(t_b, tile_row)
            dve.wait_ge(loaded, LOADS)
            nc.vector.tensor_copy(end_i[:], route.running[:]).then_inc(table_step, 1)
            nc.vector.memset(bias2[:], 0.0).then_inc(zeroed, 1)
            made = sem("c_table_part_made")
            for k, op in enumerate(ops):
                op().then_inc(made, 1)
                dve.wait_ge(made, k + 1)
            dve.wait_ge(table_step, 1)
            nc.vector.tensor_copy(tile_expert[:], t_e[0:1]).then_inc(table_step, 1)

            dve.wait_ge(hi_ready, 2)
            dve.wait_ge(zeroed, 2)
            nc.vector.tensor_copy(bias2[0:1, :, :], b2_hi[0:1, :, :]).then_inc(split_ready, 1)
            nc.vector.scalar_tensor_tensor(bias2[32:33, :, :], stage_b2[32:33, :, :], W_SCALE, b2_hi[32:33, :, :], ALU.mult,
                                           ALU.subtract).then_inc(split_ready, 1)
            def split_low(e, u):
                if isinstance(e, int) and e < N_EXP:
                    dve.wait_ge(hi_ready, 2 + 3 * e + 3)
                    c, cc = slice(e * HID, (e + 1) * HID), slice(e * HC, (e + 1) * HC)
                    for dst, src, hi in ((w1.a_lo[:, c], staged.w1[u][:, 0, :], w1.a_hi[:, c]),
                                         (w1.b_lo[:, c], staged.w1[u][:, 1, :], w1.b_hi[:, c]),
                                         (w2_lo[:, cc, :], staged.w2[u][:], w2_hi[:, cc, :])):
                        nc.vector.scalar_tensor_tensor(dst, src, W_SCALE, hi, ALU.mult, ALU.subtract).then_inc(split_ready, 1)

            def x_low(j, u):
                dve.wait_ge(x_hi_ready, j + 1)
                nc.vector.tensor_tensor(x_alo[u][:], xf[:, 0, :], x_hi[u][:, 0, :], ALU.subtract).then_inc(x_ready, 1)
                nc.vector.scalar_tensor_tensor(x_b[u][:], x_hi[u][:, 1, :], sel[:, 0:1], xf[:, 1, :], ALU.mult, ALU.add
                                               ).then_inc(x_ready, 1)

            def y_part(j, u):
                dve.wait_ge(chunk_used, HC * j + HC)
                wait(dve, y_stored[u], 16 * (j - u))
                nc.vector.tensor_scalar(y_out[u][:].rearrange("p a d -> p (a d)"), bank_y[u][:, 0:A2 * D], 1.0 / W_SCALE, None,
                                        ALU.mult).then_inc(y_ready, 1)

            def h_high(j, u, c):
                k = j * HC + c
                dve.wait_ge(gelu_ready, k + 1)
                wait(dve, chunk_used, k - DEPTH + 1)
                nc.vector.tensor_copy(h_hi[c % DEPTH][:], hf[c % DEPTH][:]).then_inc(h_hi_ready, 1)

            def h_low(j, u, c):
                dve.wait_ge(h_hi_ready, j * HC + c + 1)
                nc.vector.tensor_tensor(h_lo[c % DEPTH][:], hf[c % DEPTH][:], h_hi[c % DEPTH][:], ALU.subtract).then_inc(h_lo_ready, 1)

            def turn(run):
                run(split_low, 0)
                run(h_low, 2, 5)
                run(h_high, 1, 0)
                run(h_low, 1, 0)
                run(h_high, 1, 1)
                run(h_low, 1, 1)
                run(h_high, 1, 2)
                run(y_part, 2)
                run(h_low, 1, 2)
                run(h_high, 1, 3)
                run(x_low, 0)
                run(h_low, 1, 3)
                run(h_high, 1, 4)
                run(h_low, 1, 4)
                run(h_high, 1, 5)

            pipeline(dve, NT, turn, N_EXP)

        @block.tensor
        def _(pe):
            def mm(dst, lhsT, rhs, start, stop, **k):
                return nc.tensor.matmul(dst, lhsT, rhs, start=start, stop=stop, **k)

            pe.wait_ge(table_step, 2)

            def transpose_x(j, u):
                pe.wait_ge(x_loaded[u], 8 * (j - u) + 16)
                wait(pe, xf_ready, 2 * (j - 1))
                for a in range(A2):
                    c = slice(a * P, (a + 1) * P)
                    d = slice(TILE + a * P, TILE + (a + 1) * P)
                    nc.tensor.transpose(bank_x[u][:, c], x_rows[u][:, a, 0:P], ident[:])
                    last = nc.tensor.transpose(bank_x[u][:, d], x_rows[u][:, a, P:2 * P], ident[:])
                last.then_inc(x_filled, 1)

            def up(j, u, c):
                e = expert[u]
                k = j * HC + c
                wait(pe, gelu_ready, k - DEPTH + 1)
                if c == 0:
                    pe.wait_ge(x_ready, 2 * j + 2)
                    if isinstance(j, int) and j < N_EXP:
                        pe.wait_ge(split_ready, 2 + 3 * (j + 1))
                dst = bank_h[c % DEPTH][:, 0:TILE]
                for i, (x_part, w_part) in enumerate(w1.passes(x_hi[u][:, 0, :], x_alo[u][:], x_b[u][:], bass.ds(e * HID + c * P, P))):
                    last = mm(dst, w_part, x_part, i == 0, i == 4)
                last.then_inc(h_filled, 1)

            def down(j, u, c):
                e = expert[u]
                k = j * HC + c
                if c == 0:
                    wait(pe, y_ready, j - 1)
                pe.wait_ge(h_lo_ready, k + 1)
                row = bass.ds(e * HC + c, 1)
                wh, wl = (w[:, row, :].rearrange("p o d -> p (o d)") for w in (w2_hi, w2_lo))
                for a in range(A2):
                    dst = bank_y[u][:, a * D:(a + 1) * D]
                    tok = slice(a * P, (a + 1) * P)
                    if c == 0:
                        mm(dst, ones_rows[:], bias2[:, bass.ds(e, 1), :].rearrange("p o d -> p (o d)"), a == 0, False,
                           skip_group_check=True)
                    mm(dst, h_hi[c % DEPTH][:, tok], wh, False, False, skip_group_check=True)
                    mm(dst, h_hi[c % DEPTH][:, tok], wl, False, False, skip_group_check=True)
                    last = mm(dst, h_lo[c % DEPTH][:, tok], wh, False, c == HC - 1, skip_group_check=True)
                last.then_inc(chunk_used, 1)

            expert_reg, expert = [pe.alloc_register(f"expert{u}") for u in range(2)], {}

            def load_expert(j, u):
                pe.reg_load(expert_reg[u], tile_expert[0:1, bass.ds(j, 1)])
                recall_expert(j, u)

            def recall_expert(j, u):
                expert[u] = pe.snap(expert_reg[u], min_val=0, max_val=N_EXP - 1)

            def turn(run):
                run(recall_expert, 2)
                run(load_expert, 1)
                run(down, 2, 1)
                run(up, 2, 5)
                run(down, 2, 2)
                run(up, 1, 0)
                run(down, 2, 3)
                run(up, 1, 1)
                run(up, 1, 2)
                run(down, 2, 4)
                run(transpose_x, 0)
                run(up, 1, 3)
                run(down, 2, 5)
                run(down, 1, 0)
                run(up, 1, 4)

            pipeline(pe, NT, turn, N_EXP)


def combine(nc, A, h_all, route, out, sb, sem, n_seq):
    DEPTH = 8
    y_rows = [sb(f"y_rows{u}", [P, 2, D], F32) for u in range(DEPTH)]
    fetched = [sem(f"d_fetched{u}") for u in range(DEPTH)]
    added = sem("d_added")
    stored = sem("d_stored")

    def seq(s):
        return bass.ts(s, D)

    block = nc.Block()
    with block:
        @block.sync
        def _(sp):
            def fetch(s, u):
                sp.dma_start(y_rows[u][:], route.y_tokens[bass.ds(2 * P * s + 2 * TILE, 2 * P), :].rearrange("(p k) d -> p k d", k=2)
                             ).then_inc(fetched[u], 16)

            for u in range(DEPTH):
                fetch(u, u)
            with sp.Fori(1, n_seq // DEPTH) as i:
                for u in range(DEPTH):
                    sp.wait_ge(added, 2 * DEPTH * (i - 1) + 2 * u + 2)
                    fetch(DEPTH * i + u, u)

        @block.vector
        def _(dve):
            with dve.Fori(0, n_seq // DEPTH) as i:
                for u in range(DEPTH):
                    s = DEPTH * i + u
                    dve.wait_ge(fetched[u], 16 * i + 16)
                    for k in range(2):
                        dve.wait_ge(added, 2 * s + k)
                        nc.vector.scalar_tensor_tensor(h_all[:, seq(s)], y_rows[u][:, k, :], route.gates[:, bass.ds(2 * s + 1 - k, 1)],
                                                       h_all[:, seq(s)], ALU.mult, ALU.add).then_inc(added, 1)

        @block.scalar
        def _(act):
            with act.Fori(0, n_seq) as s:
                act.wait_ge(added, 2 * s + 2)
                act.dma_start(out[bass.ds(s, 1), :, :].rearrange("b s d -> s (b d)"), h_all[:, seq(s)]).then_inc(stored, 16)
            act.wait_ge(stored, 16 * n_seq)


def kernel(**inputs):
    import numpy as np
    import concourse.bacc as bacc
    from concourse.bass_utils import run_bass_kernel_spmd

    a = {k: np.asarray(v) for k, v in inputs.items()}
    n_seq, n_tok = a["x"].shape
    for k in ("x", "itok_BS_0_1003", "itok_BS_0_5", "mask_BS_i1_0"):
        a[k] = a[k].T
    a["L0_attn_qkv_wT"] = a.pop("L0_attn_qkv_w").T
    a["L0_attn_proj_wT"] = a.pop("L0_attn_proj_w").T

    w, b = a["L0_ffn_qkv_w"], a["L0_ffn_qkv_b"]
    twice = np.concatenate([np.arange(16 * h, 16 * h + 16) for h in range(2 * HEADS) for _ in range(2)])
    a["qk_dup_wT"], a["qk_dup_b"] = w[:, twice], b[twice]

    p = np.arange(P)
    a["sel"] = np.stack([-(p >= DB).astype(np.float32), -(p % 32 >= 16).astype(np.float32)], axis=1)
    a["token_rows"] = (2 * (P * np.arange(n_seq)[None, :] + p[:, None]) + 2 * TILE).astype(np.float32)
    a["rest_rows"] = (2 * (P * np.arange(TILE // P)[None, :] + p[:, None])).astype(np.float32)
    a["expert_no"] = np.arange(N_EXP, dtype=np.float32)
    a["queue_start"] = (np.arange(N_EXP) * (n_seq * n_tok + TILE)).astype(np.float32)
    a["tile_no"] = np.arange(2 * n_seq * n_tok // TILE + N_EXP, dtype=np.float32)

    nc = bacc.Bacc("TRN2", target_bir_lowering=False, num_devices=1)
    arrays, aps = {}, {}
    for name, v in a.items():
        v = np.ascontiguousarray(v if v.ndim > 1 else v[None])
        arrays[f"in_{name}"] = v
        aps[name] = nc.dram_tensor(f"in_{name}", v.shape, mybir.dt.from_np(v.dtype), kind="ExternalInput").ap()
    out = nc.dram_tensor("out", [n_seq, n_tok, D], F32, kind="ExternalOutput").ap()
    build(nc, aps, out)
    return run_bass_kernel_spmd(nc, [arrays], core_ids=[0]).results[0]["out"]
```
